# Optimizing a Trainium2 kernel written in Bass

```python
import numpy as np
import jax
import jax.numpy as jnp

def _softmax(x, axis=-1):
    return jax.nn.softmax(x, axis=axis)

def _gelu(x):
    return jax.nn.gelu(x, approximate=True)

def _silu(x):
    return jax.nn.silu(x)

def _sigmoid(x):
    return jax.nn.sigmoid(x)

def _layernorm(x, axis=-1, eps=1e-05):
    m = jnp.mean(x, axis=axis, keepdims=True)
    v = jnp.var(x, axis=axis, keepdims=True)
    return (x - m) / jnp.sqrt(v + eps)

def _scatter_add(tgt, idx, src, axis=0):
    return tgt.at[idx].add(src)

def _segment_sum(src, seg, n):
    return jax.ops.segment_sum(src, seg, n)
kernel_name = 'mk_seq_postln_d4_jaxref_r8_2ce64b'

def setup_inputs(seed: int=0):
    np.random.seed(seed)
    _w = jnp.asarray

    def _L0_attn_setup():
        import jax, jax.numpy as jnp
        import numpy as np
        B, L, E, H = (8, 256, 128, 16)
        D = E // H
        EPS = 1e-06
        key = jax.random.key(seed)
        ks = jax.random.split(key, 9)
        s = 1.0 / np.sqrt(E)

        def lin_w(k):
            return jax.random.uniform(k, (E, E), jnp.float32, -s, s)

        def lin_b(k):
            return jax.random.uniform(k, (E,), jnp.float32, -s, s)
        return {'query': jax.random.normal(ks[0], (B, L, E), jnp.float32), 'Wq': lin_w(ks[1]), 'bq': lin_b(ks[2]), 'Wk': lin_w(ks[3]), 'bk': lin_b(ks[4]), 'Wv': lin_w(ks[5]), 'bv': lin_b(ks[6]), 'Wo': lin_w(ks[7]), 'bo': lin_b(ks[8])}
    _L0_attn_in = _L0_attn_setup()

    def _L0_ffn_setup():
        import jax, jax.numpy as jnp
        import numpy as np
        DIM = 128
        HIDDEN = 512
        N_EXPERTS = 8
        K = 2
        TEMP = 1.0

        def _expert_ffn(xf, wa, ba, wb, bb):
            h = xf @ wa.T + ba
            h1, h2 = jnp.split(h, 2, axis=-1)
            h = jax.nn.silu(h1) * h2
            return h @ wb.T + bb
        key = jax.random.key(seed)
        ks = jax.random.split(key, 7)
        s = 0.02
        x = jax.random.normal(ks[0], (4, 256, DIM), dtype=jnp.float32)
        router_w = jax.random.normal(ks[1], (N_EXPERTS, DIM), dtype=jnp.float32) * s
        router_b = jnp.zeros((N_EXPERTS,), dtype=jnp.float32)
        w1 = jax.random.normal(ks[2], (N_EXPERTS, 2 * HIDDEN, DIM), dtype=jnp.float32) * s
        b1 = jnp.zeros((N_EXPERTS, 2 * HIDDEN), dtype=jnp.float32)
        w2 = jax.random.normal(ks[3], (N_EXPERTS, DIM, HIDDEN), dtype=jnp.float32) * s
        b2 = jnp.zeros((N_EXPERTS, DIM), dtype=jnp.float32)
        return {'x': x, 'router_w': router_w, 'router_b': router_b, 'w1': w1, 'b1': b1, 'w2': w2, 'b2': b2}
    _L0_ffn_in = _L0_ffn_setup()

    def _L1_attn_setup():
        import jax, jax.numpy as jnp
        import numpy as np
        DIM = 128
        BATCH = 8
        SEQ = 256
        key = jax.random.key(seed)
        ks = jax.random.split(key, 10)
        s = 0.02
        return {'x': jax.random.normal(ks[0], (BATCH, SEQ, DIM), dtype=jnp.float32), 'Wq': jax.random.normal(ks[1], (DIM, DIM), dtype=jnp.float32) * s, 'bq': jnp.zeros((DIM,), jnp.float32), 'Wk': jax.random.normal(ks[2], (DIM, DIM), dtype=jnp.float32) * s, 'bk': jnp.zeros((DIM,), jnp.float32), 'Wv': jax.random.normal(ks[3], (DIM, DIM), dtype=jnp.float32) * s, 'bv': jnp.zeros((DIM,), jnp.float32), 'Wo': jax.random.normal(ks[4], (DIM, DIM), dtype=jnp.float32) * s, 'bo': jnp.zeros((DIM,), jnp.float32), 'decay_param': jnp.asarray(0.0, jnp.float32)}
    _L1_attn_in = _L1_attn_setup()

    def _L1_ffn_setup():
        import jax, jax.numpy as jnp
        import numpy as np
        D_IN, D_HID = (128, 512)

        def _ternary(key, shape):
            return jax.random.randint(key, shape, -1, 2).astype(jnp.float32)

        def _tlin(x, w, s):
            return jnp.einsum('bsi,oi->bso', x, w) * s
        key = jax.random.key(seed)
        ks = jax.random.split(key, 12)
        inv = lambda fan: 1.0 / np.sqrt(fan).astype(np.float32)
        return {'x': jax.random.normal(ks[0], (4, 256, D_IN), dtype=jnp.float32), 'w1_w': _ternary(ks[1], (D_HID, D_IN)), 'w1_s': jax.random.uniform(ks[2], (D_HID,), dtype=jnp.float32) * inv(D_IN), 'w2_w': _ternary(ks[3], (D_HID, D_IN)), 'w2_s': jax.random.uniform(ks[4], (D_HID,), dtype=jnp.float32) * inv(D_IN), 'h1_w': _ternary(ks[5], (D_HID, D_HID)), 'h1_s': jax.random.uniform(ks[6], (D_HID,), dtype=jnp.float32) * inv(D_HID), 'h2_w': _ternary(ks[7], (D_HID, D_HID)), 'h2_s': jax.random.uniform(ks[8], (D_HID,), dtype=jnp.float32) * inv(D_HID), 'w3_w': _ternary(ks[9], (D_IN, D_HID)), 'w3_s': jax.random.uniform(ks[10], (D_IN,), dtype=jnp.float32) * inv(D_HID)}
    _L1_ffn_in = _L1_ffn_setup()

    def _L2_attn_setup():
        import jax, jax.numpy as jnp
        import numpy as np
        import math
        D_MODEL = 128
        D_INNER = 256
        D_HALF = D_INNER // 2
        D_STATE = 16
        D_CONV = 4
        DT_RANK = 64
        B_SZ = 4
        L = 256

        def _dw_conv(x, w, b):
            y = jax.lax.conv_general_dilated(x, w, window_strides=(1,), padding='SAME', feature_group_count=x.shape[-1], dimension_numbers=('NWC', 'WIO', 'NWC'))
            return y + b

        def _selective_scan(u, delta, A, Bc, Cc, D):
            b, l, d = u.shape
            n = A.shape[1]

            def step(h, inp):
                d_t, u_t, B_t, C_t = inp
                dA = jnp.exp(d_t[..., None] * A)
                h = dA * h + (d_t * u_t)[..., None] * B_t[:, None, :]
                y = jnp.einsum('bdn,bn->bd', h, C_t)
                return (h, y)
            h0 = jnp.zeros((b, d, n), u.dtype)
            xs = (jnp.moveaxis(delta, 1, 0), jnp.moveaxis(u, 1, 0), jnp.moveaxis(Bc, 1, 0), jnp.moveaxis(Cc, 1, 0))
            _, ys = jax.lax.scan(step, h0, xs)
            return jnp.moveaxis(ys, 0, 1) + u * D
        key = jax.random.key(seed)
        ks = jax.random.split(key, 12)
        x = jax.random.normal(ks[0], (B_SZ, L, D_MODEL), jnp.float32)
        W_in = jax.random.normal(ks[1], (D_MODEL, D_INNER), jnp.float32) * D_MODEL ** (-0.5)
        conv_x_w = jax.random.normal(ks[2], (D_CONV, 1, D_HALF), jnp.float32) * D_CONV ** (-0.5)
        conv_x_b = jnp.zeros((D_HALF,), jnp.float32)
        conv_z_w = jax.random.normal(ks[3], (D_CONV, 1, D_HALF), jnp.float32) * D_CONV ** (-0.5)
        conv_z_b = jnp.zeros((D_HALF,), jnp.float32)
        W_xdbl = jax.random.normal(ks[4], (D_HALF, DT_RANK + 2 * D_STATE), jnp.float32) * D_HALF ** (-0.5)
        dt_init_std = DT_RANK ** (-0.5)
        W_dt = jax.random.uniform(ks[5], (DT_RANK, D_HALF), jnp.float32, -dt_init_std, dt_init_std)
        rand_vals = jax.random.uniform(ks[6], (D_HALF,))
        dt_bias = jnp.exp(rand_vals * (math.log(0.1) - math.log(0.001)) + math.log(0.001))
        dt_bias = jnp.clip(dt_bias, 0.0001)
        inv_dt = dt_bias + jnp.log(-jnp.expm1(-dt_bias))
        D = jnp.ones((D_HALF,), jnp.float32)
        W_out = jax.random.normal(ks[7], (D_INNER, D_MODEL), jnp.float32) * D_INNER ** (-0.5)
        b_out = jnp.zeros((D_MODEL,), jnp.float32)
        return dict(x=x, W_in=W_in, conv_x_w=conv_x_w, conv_x_b=conv_x_b, conv_z_w=conv_z_w, conv_z_b=conv_z_b, W_xdbl=W_xdbl, W_dt=W_dt, inv_dt=inv_dt, D=D, W_out=W_out, b_out=b_out)
    _L2_attn_in = _L2_attn_setup()

    def _L2_ffn_setup():
        import jax, jax.numpy as jnp
        import numpy as np
        DIM = 128
        DEPTH = 2
        HEADS = 8
        DIM_HEAD = 64
        WINDOW = 64
        INNER = HEADS * DIM_HEAD
        HID = int(DIM * 4 * 2 / 3)
        B, N = (2, 1024)
        QK_SCALE = 8.0

        def shift_token(t):
            t1, t2 = jnp.split(t, 2, axis=-1)
            t2 = jnp.pad(t2, ((0, 0), (1, 0), (0, 0)))[:, :-1]
            return jnp.concatenate([t1, t2], axis=-1)

        def l2norm(t):
            return t / jnp.clip(jnp.linalg.norm(t, axis=-1, keepdims=True), 1e-12)

        def rotate_half(x):
            x1, x2 = jnp.split(x, 2, axis=-1)
            return jnp.concatenate([-x2, x1], axis=-1)

        def rotary_xpos(q, k):
            n = q.shape[-2]
            half_idx = jnp.arange(0, DIM_HEAD, 2, dtype=jnp.float32)
            inv_freq = 1.0 / 10000.0 ** (half_idx / DIM_HEAD)
            t = jnp.arange(n, dtype=jnp.float32)
            freqs = t[:, None] * inv_freq[None, :]
            freqs = jnp.concatenate([freqs, freqs], axis=-1)
            base = (half_idx + 0.4 * DIM_HEAD) / (1.4 * DIM_HEAD)
            power = (t - n // 2) / float(WINDOW // 2)
            scale = base[None, :] ** power[:, None]
            scale = jnp.concatenate([scale, scale], axis=-1)
            cos, sin = (jnp.cos(freqs), jnp.sin(freqs))
            q = q * cos * scale + rotate_half(q) * sin * scale
            k = k * cos / scale + rotate_half(k) * sin / scale
            return (q, k)

        def local_attention(q, k, v):
            b, h, n, d = q.shape
            w = n // WINDOW
            bq = q.reshape(b, h, w, WINDOW, d) * QK_SCALE
            bk = k.reshape(b, h, w, WINDOW, d)
            bv = v.reshape(b, h, w, WINDOW, d)

            def look_around(t):
                p = jnp.pad(t, ((0, 0), (0, 0), (1, 0), (0, 0), (0, 0)))
                return jnp.concatenate([p[:, :, :w], p[:, :, 1:]], axis=3)
            bk, bv = (look_around(bk), look_around(bv))
            bt = jnp.arange(n).reshape(w, WINDOW)
            btp = jnp.pad(bt, ((1, 0), (0, 0)), constant_values=-1)
            btk = jnp.concatenate([btp[:w], btp[1:]], axis=1)
            sim = jnp.einsum('bhwid,bhwjd->bhwij', bq, bk)
            i = bt[:, :, None]
            j = btk[:, None, :]
            mask = (i < j) | (i > j + WINDOW) | (j == -1)
            sim = jnp.where(mask, -jnp.finfo(sim.dtype).max, sim)
            attn = jax.nn.softmax(sim, axis=-1)
            out = jnp.einsum('bhwij,bhwjd->bhwid', attn, bv)
            return out.reshape(b, h, n, d)

        def _layer(x, wqkv, qs, ksc, wo, lg, lb, w1, b1, w2, b2):
            b, n, _ = x.shape
            h = shift_token(x)
            qkv = h @ wqkv
            q, k, v = jnp.split(qkv, 3, axis=-1)
            to_heads = lambda t: t.reshape(b, n, HEADS, DIM_HEAD).transpose(0, 2, 1, 3)
            q, k, v = (to_heads(q), to_heads(k), to_heads(v))
            q = l2norm(q) * qs
            k = l2norm(k) * ksc
            q, k = rotary_xpos(q, k)
            o = local_attention(q, k, v)
            o = o.transpose(0, 2, 1, 3).reshape(b, n, INNER)
            x = x + o @ wo
            h = shift_token(x)
            mu = h.mean(-1, keepdims=True)
            var = h.var(-1, keepdims=True)
            h = (h - mu) / jnp.sqrt(var + 1e-05) * lg + lb
            h = h @ w1 + b1
            a, g = jnp.split(h, 2, axis=-1)
            h = a * jax.nn.gelu(g, approximate=False)
            x = x + h @ w2 + b2
            return x
        key = jax.random.key(seed)
        ks = jax.random.split(key, 6)
        return {'x': jax.random.normal(ks[0], (B, N, DIM), jnp.float32), 'wqkv': jax.random.normal(ks[1], (DEPTH, DIM, 3 * INNER), jnp.float32) * 0.02, 'q_scale': jnp.ones((DEPTH, DIM_HEAD), jnp.float32), 'k_scale': jnp.ones((DEPTH, DIM_HEAD), jnp.float32), 'wo': jax.random.normal(ks[2], (DEPTH, INNER, DIM), jnp.float32) * 0.02, 'ln_g': jnp.ones((DEPTH, DIM), jnp.float32), 'ln_b': jnp.zeros((DEPTH, DIM), jnp.float32), 'w1': jax.random.normal(ks[3], (DEPTH, DIM, 2 * HID), jnp.float32) * 0.02, 'b1': jnp.zeros((DEPTH, 2 * HID), jnp.float32), 'w2': jax.random.normal(ks[4], (DEPTH, HID, DIM), jnp.float32) * 0.02, 'b2': jnp.zeros((DEPTH, DIM), jnp.float32)}
    _L2_ffn_in = _L2_ffn_setup()

    def _L3_attn_setup():
        import jax, jax.numpy as jnp
        import numpy as np
        NUM_HEADS = 16
        NUM_KV_HEADS = 4
        HEAD_DIM = 64
        HIDDEN = 128
        R_SOFTPLUS_0 = 1.442695041
        key = jax.random.key(seed)
        ks = jax.random.split(key, 6)
        B, S = (2, 256)
        qkv_out = (NUM_HEADS + 2 * NUM_KV_HEADS) * HEAD_DIM
        return {'hidden_states': jax.random.normal(ks[0], (B, S, HIDDEN), dtype=jnp.float32), 'scaling': jax.random.normal(ks[1], (HEAD_DIM,), dtype=jnp.float32), 'qkv_w': jax.random.normal(ks[2], (qkv_out, HIDDEN), dtype=jnp.float32) * (1.0 / np.sqrt(HIDDEN)), 'qkv_b': jax.random.normal(ks[3], (qkv_out,), dtype=jnp.float32) * 0.01, 'o_w': jax.random.normal(ks[4], (HIDDEN, NUM_HEADS * HEAD_DIM), dtype=jnp.float32) * (1.0 / np.sqrt(NUM_HEADS * HEAD_DIM)), 'o_b': jax.random.normal(ks[5], (HIDDEN,), dtype=jnp.float32) * 0.01}
    _L3_attn_in = _L3_attn_setup()

    def _L3_ffn_setup():
        import jax, jax.numpy as jnp
        import numpy as np
        D_IN, D_HID = (128, 512)

        def _ternary(key, shape):
            return jax.random.randint(key, shape, -1, 2).astype(jnp.float32)

        def _tlin(x, w, s):
            return jnp.einsum('bsi,oi->bso', x, w) * s
        key = jax.random.key(seed)
        ks = jax.random.split(key, 12)
        inv = lambda fan: 1.0 / np.sqrt(fan).astype(np.float32)
        return {'x': jax.random.normal(ks[0], (4, 256, D_IN), dtype=jnp.float32), 'w1_w': _ternary(ks[1], (D_HID, D_IN)), 'w1_s': jax.random.uniform(ks[2], (D_HID,), dtype=jnp.float32) * inv(D_IN), 'w2_w': _ternary(ks[3], (D_HID, D_IN)), 'w2_s': jax.random.uniform(ks[4], (D_HID,), dtype=jnp.float32) * inv(D_IN), 'h1_w': _ternary(ks[5], (D_HID, D_HID)), 'h1_s': jax.random.uniform(ks[6], (D_HID,), dtype=jnp.float32) * inv(D_HID), 'h2_w': _ternary(ks[7], (D_HID, D_HID)), 'h2_s': jax.random.uniform(ks[8], (D_HID,), dtype=jnp.float32) * inv(D_HID), 'w3_w': _ternary(ks[9], (D_IN, D_HID)), 'w3_s': jax.random.uniform(ks[10], (D_IN,), dtype=jnp.float32) * inv(D_HID)}
    _L3_ffn_in = _L3_ffn_setup()
    _d = {'L0_attn_query': _L0_attn_in['query'], 'L0_attn_Wq': _L0_attn_in['Wq'], 'L0_attn_bq': _L0_attn_in['bq'], 'L0_attn_Wk': _L0_attn_in['Wk'], 'L0_attn_bk': _L0_attn_in['bk'], 'L0_attn_Wv': _L0_attn_in['Wv'], 'L0_attn_bv': _L0_attn_in['bv'], 'L0_attn_Wo': _L0_attn_in['Wo'], 'L0_attn_bo': _L0_attn_in['bo'], 'L0_ffn_router_w': _L0_ffn_in['router_w'], 'L0_ffn_router_b': _L0_ffn_in['router_b'], 'L0_ffn_w1': _L0_ffn_in['w1'], 'L0_ffn_b1': _L0_ffn_in['b1'], 'L0_ffn_w2': _L0_ffn_in['w2'], 'L0_ffn_b2': _L0_ffn_in['b2'], 'L1_attn_Wq': _L1_attn_in['Wq'], 'L1_attn_bq': _L1_attn_in['bq'], 'L1_attn_Wk': _L1_attn_in['Wk'], 'L1_attn_bk': _L1_attn_in['bk'], 'L1_attn_Wv': _L1_attn_in['Wv'], 'L1_attn_bv': _L1_attn_in['bv'], 'L1_attn_Wo': _L1_attn_in['Wo'], 'L1_attn_bo': _L1_attn_in['bo'], 'L1_attn_decay_param': _L1_attn_in['decay_param'], 'L1_ffn_w1_w': _L1_ffn_in['w1_w'], 'L1_ffn_w1_s': _L1_ffn_in['w1_s'], 'L1_ffn_w2_w': _L1_ffn_in['w2_w'], 'L1_ffn_w2_s': _L1_ffn_in['w2_s'], 'L1_ffn_h1_w': _L1_ffn_in['h1_w'], 'L1_ffn_h1_s': _L1_ffn_in['h1_s'], 'L1_ffn_h2_w': _L1_ffn_in['h2_w'], 'L1_ffn_h2_s': _L1_ffn_in['h2_s'], 'L1_ffn_w3_w': _L1_ffn_in['w3_w'], 'L1_ffn_w3_s': _L1_ffn_in['w3_s'], 'L2_attn_W_in': _L2_attn_in['W_in'], 'L2_attn_conv_x_w': _L2_attn_in['conv_x_w'], 'L2_attn_conv_x_b': _L2_attn_in['conv_x_b'], 'L2_attn_conv_z_w': _L2_attn_in['conv_z_w'], 'L2_attn_conv_z_b': _L2_attn_in['conv_z_b'], 'L2_attn_W_xdbl': _L2_attn_in['W_xdbl'], 'L2_attn_W_dt': _L2_attn_in['W_dt'], 'L2_attn_inv_dt': _L2_attn_in['inv_dt'], 'L2_attn_D': _L2_attn_in['D'], 'L2_attn_W_out': _L2_attn_in['W_out'], 'L2_attn_b_out': _L2_attn_in['b_out'], 'L2_ffn_wqkv': _L2_ffn_in['wqkv'], 'L2_ffn_q_scale': _L2_ffn_in['q_scale'], 'L2_ffn_k_scale': _L2_ffn_in['k_scale'], 'L2_ffn_wo': _L2_ffn_in['wo'], 'L2_ffn_ln_g': _L2_ffn_in['ln_g'], 'L2_ffn_ln_b': _L2_ffn_in['ln_b'], 'L2_ffn_w1': _L2_ffn_in['w1'], 'L2_ffn_b1': _L2_ffn_in['b1'], 'L2_ffn_w2': _L2_ffn_in['w2'], 'L2_ffn_b2': _L2_ffn_in['b2'], 'L3_attn_scaling': _L3_attn_in['scaling'], 'L3_attn_qkv_w': _L3_attn_in['qkv_w'], 'L3_attn_qkv_b': _L3_attn_in['qkv_b'], 'L3_attn_o_w': _L3_attn_in['o_w'], 'L3_attn_o_b': _L3_attn_in['o_b'], 'L3_ffn_w1_w': _L3_ffn_in['w1_w'], 'L3_ffn_w1_s': _L3_ffn_in['w1_s'], 'L3_ffn_w2_w': _L3_ffn_in['w2_w'], 'L3_ffn_w2_s': _L3_ffn_in['w2_s'], 'L3_ffn_h1_w': _L3_ffn_in['h1_w'], 'L3_ffn_h1_s': _L3_ffn_in['h1_s'], 'L3_ffn_h2_w': _L3_ffn_in['h2_w'], 'L3_ffn_h2_s': _L3_ffn_in['h2_s'], 'L3_ffn_w3_w': _L3_ffn_in['w3_w'], 'L3_ffn_w3_s': _L3_ffn_in['w3_s']}
    _x0 = _d['L0_attn_query']
    _d['L0_attn_query'] = jax.random.normal(jax.random.fold_in(jax.random.key(seed), 1), (1, 2048, 128), dtype=_x0.dtype)
    del _x0
    return _d

def reference(L0_attn_query, L0_attn_Wq, L0_attn_bq, L0_attn_Wk, L0_attn_bk, L0_attn_Wv, L0_attn_bv, L0_attn_Wo, L0_attn_bo, L0_ffn_router_w, L0_ffn_router_b, L0_ffn_w1, L0_ffn_b1, L0_ffn_w2, L0_ffn_b2, L1_attn_Wq, L1_attn_bq, L1_attn_Wk, L1_attn_bk, L1_attn_Wv, L1_attn_bv, L1_attn_Wo, L1_attn_bo, L1_attn_decay_param, L1_ffn_w1_w, L1_ffn_w1_s, L1_ffn_w2_w, L1_ffn_w2_s, L1_ffn_h1_w, L1_ffn_h1_s, L1_ffn_h2_w, L1_ffn_h2_s, L1_ffn_w3_w, L1_ffn_w3_s, L2_attn_W_in, L2_attn_conv_x_w, L2_attn_conv_x_b, L2_attn_conv_z_w, L2_attn_conv_z_b, L2_attn_W_xdbl, L2_attn_W_dt, L2_attn_inv_dt, L2_attn_D, L2_attn_W_out, L2_attn_b_out, L2_ffn_wqkv, L2_ffn_q_scale, L2_ffn_k_scale, L2_ffn_wo, L2_ffn_ln_g, L2_ffn_ln_b, L2_ffn_w1, L2_ffn_b1, L2_ffn_w2, L2_ffn_b2, L3_attn_scaling, L3_attn_qkv_w, L3_attn_qkv_b, L3_attn_o_w, L3_attn_o_b, L3_ffn_w1_w, L3_ffn_w1_s, L3_ffn_w2_w, L3_ffn_w2_s, L3_ffn_h1_w, L3_ffn_h1_s, L3_ffn_h2_w, L3_ffn_h2_s, L3_ffn_w3_w, L3_ffn_w3_s):

    def _L0_attn_ref(query, Wq, bq, Wk, bk, Wv, bv, Wo, bo):
        import jax, jax.numpy as jnp
        import numpy as np
        B, L, E, H = (8, 256, 128, 16)
        D = E // H
        EPS = 1e-06
        bsz, tgt_len, embed_dim = query.shape
        n_head = H
        head_dim = embed_dim // n_head
        m = tgt_len
        q = query @ Wq + bq
        k = query @ Wk + bk
        v = query @ Wv + bv

        def to_heads(x):
            return x.reshape(bsz, tgt_len, n_head, head_dim).transpose(0, 2, 1, 3)
        q = jax.nn.softmax(to_heads(q), axis=-1)
        k = jax.nn.softmax(to_heads(k), axis=-1)
        v = to_heads(v)
        comp_q = 1.0 - q
        comp_k = 1.0 - k
        idx = np.pi / 2 * jnp.arange(1, m + 1, dtype=jnp.float32) / m
        sin = jnp.sin(idx)[None, None, :, None]
        cos = jnp.cos(idx)[None, None, :, None]

        def feat(x):
            return jnp.concatenate([x * sin, x * cos], axis=-1)
        qf, comp_qf = (feat(q), feat(comp_q))
        kf, comp_kf = (feat(k), feat(comp_k))

        def branch(qf_, kf_):
            kv = jnp.einsum('bhld,bhlm->bhdm', kf_, v)
            z = 1.0 / jnp.maximum(jnp.einsum('bhld,bhd->bhl', qf_, kf_.sum(axis=2)), EPS)
            return jnp.einsum('bhld,bhdm,bhl->bhlm', qf_, kv, z)
        attn = branch(qf, kf) + branch(comp_qf, comp_kf)
        out = attn.transpose(2, 0, 1, 3).reshape(tgt_len, bsz, embed_dim)
        out = out @ Wo + bo
        return out.reshape(bsz, tgt_len, embed_dim)

    def _L0_ffn_ref(x, router_w, router_b, w1, b1, w2, b2):
        import jax, jax.numpy as jnp
        import numpy as np
        DIM = 128
        HIDDEN = 512
        N_EXPERTS = 8
        K = 2
        TEMP = 1.0

        def _expert_ffn(xf, wa, ba, wb, bb):
            h = xf @ wa.T + ba
            h1, h2 = jnp.split(h, 2, axis=-1)
            h = jax.nn.silu(h1) * h2
            return h @ wb.T + bb
        b, t, d = x.shape
        logits = (x @ router_w.T + router_b) / TEMP
        topk_val, topk_idx = jax.lax.top_k(logits, K)
        weights = jax.nn.softmax(topk_val, axis=-1)
        xf = x.reshape(-1, d)
        outs = jax.vmap(_expert_ffn, in_axes=(None, 0, 0, 0, 0))(xf, w1, b1, w2, b2)
        outs = jnp.transpose(outs, (1, 0, 2))
        idx = topk_idx.reshape(-1, K)
        gathered = jnp.take_along_axis(outs, idx[:, :, None], axis=1)
        combined = (gathered * weights.reshape(-1, K, 1)).sum(axis=1)
        return combined.reshape(b, t, d)

    def _L1_attn_ref(x, Wq, bq, Wk, bk, Wv, bv, Wo, bo, decay_param):
        import jax, jax.numpy as jnp
        import numpy as np
        DIM = 128
        BATCH = 8
        SEQ = 256
        q = x @ Wq + bq
        k = jax.nn.elu(x @ Wk + bk) + 1.0
        v = x @ Wv + bv
        decay = jax.nn.sigmoid(decay_param)
        B, S, D = x.shape

        def step(mem, qkv):
            q_t, k_t, v_t = qkv
            read = jnp.einsum('bd,bde->be', q_t, mem)
            mem = decay * mem + k_t[:, :, None] * v_t[:, None, :]
            return (mem, read)
        mem0 = jnp.zeros((B, D, D), x.dtype)
        _, outs = jax.lax.scan(step, mem0, (q.transpose(1, 0, 2), k.transpose(1, 0, 2), v.transpose(1, 0, 2)))
        out = outs.transpose(1, 0, 2)
        return out @ Wo + bo

    def _L1_ffn_ref(x, w1_w, w1_s, w2_w, w2_s, h1_w, h1_s, h2_w, h2_s, w3_w, w3_s):
        import jax, jax.numpy as jnp
        import numpy as np
        D_IN, D_HID = (128, 512)

        def _ternary(key, shape):
            return jax.random.randint(key, shape, -1, 2).astype(jnp.float32)

        def _tlin(x, w, s):
            return jnp.einsum('bsi,oi->bso', x, w) * s
        h = jax.nn.silu(_tlin(x, w1_w, w1_s)) * _tlin(x, w2_w, w2_s)
        h = jax.nn.gelu(_tlin(h, h1_w, h1_s), approximate=False)
        h = jax.nn.gelu(_tlin(h, h2_w, h2_s), approximate=False)
        return _tlin(h, w3_w, w3_s)

    def _L2_attn_ref(x, W_in, conv_x_w, conv_x_b, conv_z_w, conv_z_b, W_xdbl, W_dt, inv_dt, D, W_out, b_out):
        import jax, jax.numpy as jnp
        import numpy as np
        import math
        D_MODEL = 128
        D_INNER = 256
        D_HALF = D_INNER // 2
        D_STATE = 16
        D_CONV = 4
        DT_RANK = 64
        B_SZ = 4
        L = 256

        def _dw_conv(x, w, b):
            y = jax.lax.conv_general_dilated(x, w, window_strides=(1,), padding='SAME', feature_group_count=x.shape[-1], dimension_numbers=('NWC', 'WIO', 'NWC'))
            return y + b

        def _selective_scan(u, delta, A, Bc, Cc, D):
            b, l, d = u.shape
            n = A.shape[1]

            def step(h, inp):
                d_t, u_t, B_t, C_t = inp
                dA = jnp.exp(d_t[..., None] * A)
                h = dA * h + (d_t * u_t)[..., None] * B_t[:, None, :]
                y = jnp.einsum('bdn,bn->bd', h, C_t)
                return (h, y)
            h0 = jnp.zeros((b, d, n), u.dtype)
            xs = (jnp.moveaxis(delta, 1, 0), jnp.moveaxis(u, 1, 0), jnp.moveaxis(Bc, 1, 0), jnp.moveaxis(Cc, 1, 0))
            _, ys = jax.lax.scan(step, h0, xs)
            return jnp.moveaxis(ys, 0, 1) + u * D
        xz = x @ W_in
        xs, z = jnp.split(xz, 2, axis=-1)
        A = -jnp.tile(jnp.arange(1, D_STATE + 1, dtype=jnp.float32), (D_HALF, 1))
        xs = jax.nn.silu(_dw_conv(xs, conv_x_w, conv_x_b))
        z = jax.nn.silu(_dw_conv(z, conv_z_w, conv_z_b))
        x_dbl = xs @ W_xdbl
        dt_low, Bc, Cc = jnp.split(x_dbl, [DT_RANK, DT_RANK + D_STATE], axis=-1)
        dt = dt_low @ W_dt + inv_dt
        delta = jax.nn.softplus(dt + inv_dt)
        y = _selective_scan(xs, delta, A, Bc, Cc, D)
        y = jnp.concatenate([y, z], axis=-1)
        return y @ W_out + b_out

    def _L2_ffn_ref(x, wqkv, q_scale, k_scale, wo, ln_g, ln_b, w1, b1, w2, b2):
        import jax, jax.numpy as jnp
        import numpy as np
        DIM = 128
        DEPTH = 2
        HEADS = 8
        DIM_HEAD = 64
        WINDOW = 64
        INNER = HEADS * DIM_HEAD
        HID = int(DIM * 4 * 2 / 3)
        B, N = (2, 1024)
        QK_SCALE = 8.0

        def shift_token(t):
            t1, t2 = jnp.split(t, 2, axis=-1)
            t2 = jnp.pad(t2, ((0, 0), (1, 0), (0, 0)))[:, :-1]
            return jnp.concatenate([t1, t2], axis=-1)

        def l2norm(t):
            return t / jnp.clip(jnp.linalg.norm(t, axis=-1, keepdims=True), 1e-12)

        def rotate_half(x):
            x1, x2 = jnp.split(x, 2, axis=-1)
            return jnp.concatenate([-x2, x1], axis=-1)

        def rotary_xpos(q, k):
            n = q.shape[-2]
            half_idx = jnp.arange(0, DIM_HEAD, 2, dtype=jnp.float32)
            inv_freq = 1.0 / 10000.0 ** (half_idx / DIM_HEAD)
            t = jnp.arange(n, dtype=jnp.float32)
            freqs = t[:, None] * inv_freq[None, :]
            freqs = jnp.concatenate([freqs, freqs], axis=-1)
            base = (half_idx + 0.4 * DIM_HEAD) / (1.4 * DIM_HEAD)
            power = (t - n // 2) / float(WINDOW // 2)
            scale = base[None, :] ** power[:, None]
            scale = jnp.concatenate([scale, scale], axis=-1)
            cos, sin = (jnp.cos(freqs), jnp.sin(freqs))
            q = q * cos * scale + rotate_half(q) * sin * scale
            k = k * cos / scale + rotate_half(k) * sin / scale
            return (q, k)

        def local_attention(q, k, v):
            b, h, n, d = q.shape
            w = n // WINDOW
            bq = q.reshape(b, h, w, WINDOW, d) * QK_SCALE
            bk = k.reshape(b, h, w, WINDOW, d)
            bv = v.reshape(b, h, w, WINDOW, d)

            def look_around(t):
                p = jnp.pad(t, ((0, 0), (0, 0), (1, 0), (0, 0), (0, 0)))
                return jnp.concatenate([p[:, :, :w], p[:, :, 1:]], axis=3)
            bk, bv = (look_around(bk), look_around(bv))
            bt = jnp.arange(n).reshape(w, WINDOW)
            btp = jnp.pad(bt, ((1, 0), (0, 0)), constant_values=-1)
            btk = jnp.concatenate([btp[:w], btp[1:]], axis=1)
            sim = jnp.einsum('bhwid,bhwjd->bhwij', bq, bk)
            i = bt[:, :, None]
            j = btk[:, None, :]
            mask = (i < j) | (i > j + WINDOW) | (j == -1)
            sim = jnp.where(mask, -jnp.finfo(sim.dtype).max, sim)
            attn = jax.nn.softmax(sim, axis=-1)
            out = jnp.einsum('bhwij,bhwjd->bhwid', attn, bv)
            return out.reshape(b, h, n, d)

        def _layer(x, wqkv, qs, ksc, wo, lg, lb, w1, b1, w2, b2):
            b, n, _ = x.shape
            h = shift_token(x)
            qkv = h @ wqkv
            q, k, v = jnp.split(qkv, 3, axis=-1)
            to_heads = lambda t: t.reshape(b, n, HEADS, DIM_HEAD).transpose(0, 2, 1, 3)
            q, k, v = (to_heads(q), to_heads(k), to_heads(v))
            q = l2norm(q) * qs
            k = l2norm(k) * ksc
            q, k = rotary_xpos(q, k)
            o = local_attention(q, k, v)
            o = o.transpose(0, 2, 1, 3).reshape(b, n, INNER)
            x = x + o @ wo
            h = shift_token(x)
            mu = h.mean(-1, keepdims=True)
            var = h.var(-1, keepdims=True)
            h = (h - mu) / jnp.sqrt(var + 1e-05) * lg + lb
            h = h @ w1 + b1
            a, g = jnp.split(h, 2, axis=-1)
            h = a * jax.nn.gelu(g, approximate=False)
            x = x + h @ w2 + b2
            return x
        for l in range(DEPTH):
            x = _layer(x, wqkv[l], q_scale[l], k_scale[l], wo[l], ln_g[l], ln_b[l], w1[l], b1[l], w2[l], b2[l])
        return x

    def _L3_attn_ref(hidden_states, scaling, qkv_w, qkv_b, o_w, o_b):
        import jax, jax.numpy as jnp
        import numpy as np
        NUM_HEADS = 16
        NUM_KV_HEADS = 4
        HEAD_DIM = 64
        HIDDEN = 128
        R_SOFTPLUS_0 = 1.442695041
        B, S, _ = hidden_states.shape
        H, KV, D = (NUM_HEADS, NUM_KV_HEADS, HEAD_DIM)
        rep = H // KV
        qkv = hidden_states @ qkv_w.T + qkv_b
        xq, xk, xv = jnp.split(qkv, [H * D, H * D + KV * D], axis=-1)
        xq = xq.reshape(B, S, H, D)
        xk = xk.reshape(B, S, KV, D)
        xv = xv.reshape(B, S, KV, D)
        scale = R_SOFTPLUS_0 / jnp.sqrt(jnp.float32(D)) * jax.nn.softplus(scaling)
        xq = xq * scale[None, None, None, :]
        xk = jnp.repeat(xk, rep, axis=2)
        xv = jnp.repeat(xv, rep, axis=2)
        scores = jnp.einsum('bqhd,bkhd->bhqk', xq, xk)
        probs = jax.nn.softmax(scores.astype(jnp.float32), axis=-1).astype(xq.dtype)
        out = jnp.einsum('bhqk,bkhd->bqhd', probs, xv)
        out = out.reshape(B, S, H * D)
        return out @ o_w.T + o_b

    def _L3_ffn_ref(x, w1_w, w1_s, w2_w, w2_s, h1_w, h1_s, h2_w, h2_s, w3_w, w3_s):
        import jax, jax.numpy as jnp
        import numpy as np
        D_IN, D_HID = (128, 512)

        def _ternary(key, shape):
            return jax.random.randint(key, shape, -1, 2).astype(jnp.float32)

        def _tlin(x, w, s):
            return jnp.einsum('bsi,oi->bso', x, w) * s
        h = jax.nn.silu(_tlin(x, w1_w, w1_s)) * _tlin(x, w2_w, w2_s)
        h = jax.nn.gelu(_tlin(h, h1_w, h1_s), approximate=False)
        h = jax.nn.gelu(_tlin(h, h2_w, h2_s), approximate=False)
        return _tlin(h, w3_w, w3_s)
    x = L0_attn_query
    x = _layernorm(x + _L0_attn_ref(x, L0_attn_Wq, L0_attn_bq, L0_attn_Wk, L0_attn_bk, L0_attn_Wv, L0_attn_bv, L0_attn_Wo, L0_attn_bo), axis=-1)
    x = _layernorm(x + _L0_ffn_ref(x, L0_ffn_router_w, L0_ffn_router_b, L0_ffn_w1, L0_ffn_b1, L0_ffn_w2, L0_ffn_b2), axis=-1)
    x = _layernorm(x + _L1_attn_ref(x, L1_attn_Wq, L1_attn_bq, L1_attn_Wk, L1_attn_bk, L1_attn_Wv, L1_attn_bv, L1_attn_Wo, L1_attn_bo, L1_attn_decay_param), axis=-1)
    x = _layernorm(x + _L1_ffn_ref(x, L1_ffn_w1_w, L1_ffn_w1_s, L1_ffn_w2_w, L1_ffn_w2_s, L1_ffn_h1_w, L1_ffn_h1_s, L1_ffn_h2_w, L1_ffn_h2_s, L1_ffn_w3_w, L1_ffn_w3_s), axis=-1)
    x = _layernorm(x + _L2_attn_ref(x, L2_attn_W_in, L2_attn_conv_x_w, L2_attn_conv_x_b, L2_attn_conv_z_w, L2_attn_conv_z_b, L2_attn_W_xdbl, L2_attn_W_dt, L2_attn_inv_dt, L2_attn_D, L2_attn_W_out, L2_attn_b_out), axis=-1)
    x = _layernorm(x + _L2_ffn_ref(x, L2_ffn_wqkv, L2_ffn_q_scale, L2_ffn_k_scale, L2_ffn_wo, L2_ffn_ln_g, L2_ffn_ln_b, L2_ffn_w1, L2_ffn_b1, L2_ffn_w2, L2_ffn_b2), axis=-1)
    x = _layernorm(x + _L3_attn_ref(x, L3_attn_scaling, L3_attn_qkv_w, L3_attn_qkv_b, L3_attn_o_w, L3_attn_o_b), axis=-1)
    x = _layernorm(x + _L3_ffn_ref(x, L3_ffn_w1_w, L3_ffn_w1_s, L3_ffn_w2_w, L3_ffn_w2_s, L3_ffn_h1_w, L3_ffn_h1_s, L3_ffn_h2_w, L3_ffn_h2_s, L3_ffn_w3_w, L3_ffn_w3_s), axis=-1)
    return x

_drawn_inputs = setup_inputs


def setup_inputs(seed=0):
    import zlib

    import numpy as np

    out = dict(_drawn_inputs(seed))
    spreads = {'L0_ffn_router_b': (0.0, 0.1),
     'L0_ffn_b1': (0.0, 0.8),
     'L0_ffn_b2': (0.0, 0.1),
     'L1_attn_bq': (0.0, 0.36),
     'L1_attn_bk': (0.0, 0.557),
     'L1_attn_bv': (0.0, 0.1),
     'L1_attn_bo': (0.0, 0.1),
     'L2_attn_conv_x_b': (0.0, 0.1),
     'L2_attn_conv_z_b': (0.0, 0.1),
     'L2_attn_D': (1.0, 0.2),
     'L2_attn_b_out': (0.0, 0.1),
     'L2_ffn_q_scale': (1.0, 0.6),
     'L2_ffn_k_scale': (1.0, 0.6),
     'L2_ffn_ln_g': (1.0, 0.6),
     'L2_ffn_ln_b': (0.0, 0.8),
     'L2_ffn_b1': (0.0, 0.8),
     'L2_ffn_b2': (0.0, 0.451)}
    factors = {'L0_attn_Wq': 8.0,
     'L0_attn_bq': 8.0,
     'L0_attn_Wk': 8.0,
     'L0_attn_bk': 8.0,
     'L0_attn_Wv': 3.085,
     'L0_ffn_w1': 5.908,
     'L0_ffn_w2': 5.831,
     'L1_ffn_w1_w': 8.0,
     'L1_ffn_w1_s': 8.0,
     'L1_ffn_w2_w': 8.0,
     'L1_ffn_w2_s': 8.0,
     'L1_ffn_h1_w': 8.0,
     'L1_ffn_h1_s': 8.0,
     'L1_ffn_h2_w': 8.0,
     'L1_ffn_h2_s': 8.0,
     'L1_ffn_w3_w': 8.0,
     'L1_ffn_w3_s': 8.0,
     'L2_attn_W_dt': 64.0,
     'L2_attn_inv_dt': 29.768,
     'L2_ffn_w1': 6.642,
     'L2_ffn_w2': 6.557,
     'L3_attn_qkv_b': 5.819,
     'L3_attn_o_b': 5.082,
     'L3_ffn_w1_w': 8.0,
     'L3_ffn_w1_s': 8.0,
     'L3_ffn_w2_w': 8.0,
     'L3_ffn_w2_s': 8.0,
     'L3_ffn_h1_w': 8.0,
     'L3_ffn_h1_s': 8.0,
     'L3_ffn_h2_w': 8.0,
     'L3_ffn_h2_s': 8.0,
     'L3_ffn_w3_w': 8.0,
     'L3_ffn_w3_s': 8.0,
     'L2_attn_W_xdbl': 8.0}
    for name, (base, spread) in spreads.items():
        noise = np.random.default_rng([zlib.crc32(name.encode()), seed]).standard_normal(out[name].shape)
        drawn = base * np.exp(spread * noise) if base else spread * noise
        out[name] = jnp.asarray(drawn.astype(out[name].dtype))
    for name, factor in factors.items():
        out[name] = (out[name] * factor).astype(out[name].dtype)
    return out
```

```python
from contextlib import ExitStack

import numpy as np

import concourse.bass as bass
from concourse import mybir

F32 = mybir.dt.float32
BF16 = mybir.dt.bfloat16
F16 = mybir.dt.float16
I32 = mybir.dt.int32
U32 = mybir.dt.uint32
ALU = mybir.AluOpType
ACT = mybir.ActivationFunctionType
AX = mybir.AxisListType

T, P, NT, NB = 2048, 128, 16, 4
HID2 = 341
BLK3 = [(0, 128), (128, 128), (256, 85)]

SPEC = [
    ("ident", 128), ("bmask", 128), ("hmask", 16), ("sin", 16), ("cos", 16), ("ones", 128),
    ("b0", 384), ("bo0", 128), ("rb", 8), ("iota8", 8), ("mb1", 64), ("mb2", 128),
    ("l1bq", 1), ("l1bk", 1), ("l1bkv", 256), ("l1bo", 128), ("decay", 1), ("expn", 128), ("tri", 128),
    ("trow", 128), ("scol", 1),
    ("f1s1", 4), ("f1s2", 4), ("f1h1", 4), ("f1h2", 4), ("f1s3", 128),
    ("cxw", 4), ("czw", 4), ("cxb", 1), ("czb", 1), ("invdt", 1), ("Dp", 1), ("bout", 128), ("acol", 16),
    ("qks", 256), ("lg", 2), ("lb", 2), ("fb1", 12), ("fb2", 256),
    ("scal", 1), ("qb", 16), ("kb", 4), ("vb", 256), ("ob", 128),
    ("f3s1", 4), ("f3s2", 4), ("f3h1", 4), ("f3h2", 4), ("f3s3", 128),
]
OFF, NC = {}, 0
for _n, _w in SPEC:
    OFF[_n] = (NC, _w)
    NC += _w
BSPEC = [("identb", 128), ("maskS", 192), ("maskA", 128), ("maskB", 64), ("selB", 2048), ("selC", 2048), ("selm", 1024)]
BOFF, NBC = {}, 0
for _n, _w in BSPEC:
    BOFF[_n] = (NBC, _w)
    NBC += _w


class Eng:

    def __init__(self, sem):
        self.sem, self.n, self.ops, self.seen = sem, 0, [], {}

    def wait(self, *after):
        for t in after:
            if t is None:
                continue
            if isinstance(t, list):
                self.wait(*t)
                continue
            sem, v = t
            if self.seen.get(id(sem), 0) < v:
                self.seen[id(sem)] = v
                self.ops.append(lambda e, s=sem, n=v: e.wait_ge(s, n))

    def run(self, fn, *after):
        self.wait(*after)
        self.ops.append(fn)

    def do(self, fn, *after):
        self.wait(*after)
        self.n += 1
        self.ops.append(lambda e: fn(e).then_inc(self.sem, 1))
        return (self.sem, self.n)

    @property
    def last(self):
        return (self.sem, self.n)


class Ring:

    def __init__(self, bufs):
        self.bufs, self.free, self.i = bufs, [[] for _ in bufs], 0

    def take(self):
        k = self.i % len(self.bufs)
        self.i += 1
        return k, self.bufs[k], self.free[k]

    def release(self, k, *tokens):
        self.free[k] = list(tokens)


def program(nc, A, out, upto=8):
    ctx = ExitStack()
    with ctx:
        def sb(name, shape, dt=F32):
            return ctx.enter_context(nc.sbuf_tensor(name, shape, dt))

        X = sb("X", [P, NT, P])
        XT = sb("XT", [P, T + 1])
        CB = sb("CB", [P, NC])
        CBB = sb("CBB", [P, NBC], BF16)
        W0 = sb("W0", [P, 12288])
        W1 = sb("W1", [P, 5632])
        W2 = sb("W2", [P, 1512])
        NWK = 20300
        WK = sb("WK", [P, NWK])
        WO2 = sb("WO2", [P, 256])
        XB = sb("XB", [P, 4, P])
        Y = sb("Y", [P, 2, 4, P])
        ST = sb("ST", [P, 2, 4, 6])
        MV = sb("MV", [P, 2, 4, 2])
        NR = sb("NR", [P, 3, 256])
        PS = ctx.enter_context(nc.psum_tensor("PS", [P, 8, 512], F32))
        eye = CB[:, OFF["ident"][0]:OFF["ident"][0] + 128]

        def c(name, a=0, b=None, p0=0, p1=P):
            o, w = OFF[name]
            return CB[p0:p1, o + a:o + (w if b is None else b)]

        def cb(name, a=0, b=None, p0=0, p1=P):
            o, w = BOFF[name]
            return CBB[p0:p1, o + a:o + (w if b is None else b)]

        def wk(off, n):
            assert off + n <= NWK, (off, n)
            return WK[:, off:off + n]

        def sem(name):
            return ctx.enter_context(nc.semaphore(name))

        pe, act, dve, pool, sp = (Eng(sem(f"s_{n}")) for n in ("pe", "act", "dve", "pool", "sp"))
        engines = [pe, act, dve, pool, sp]

        def mm(o, l, r, start, stop, *after, sig=False, skip=False):
            f = lambda e: e.matmul(o, l, r, start=start, stop=stop, skip_group_check=skip)
            return pe.do(f, *after) if sig else pe.run(f, *after)

        def tr(o, i, *after, sig=False):
            f = lambda e: e.transpose(o, i, eye)
            return pe.do(f, *after) if sig else pe.run(f, *after)

        def av(o, i, func, *after, bias=0.0, scale=1.0):
            return act.do(lambda e: e.activation(o, i, func, bias=bias, scale=scale), *after)

        def tt(eng, o, a, b, op, *after):
            return eng.do(lambda e: e.tensor_tensor(o, a, b, op), *after)

        def ts(eng, o, a, s1, s2, op0, op1, *after):
            if op1 is None:
                return eng.do(lambda e: e.tensor_scalar(o, a, s1, None, op0), *after)
            return eng.do(lambda e: e.tensor_scalar(o, a, s1, s2, op0, op1), *after)

        def stt(o, a, s, b, op0, op1, *after):
            return dve.do(lambda e: e.scalar_tensor_tensor(out=o, in0=a, scalar=s, in1=b, op0=op0, op1=op1), *after)

        def cp(eng, o, i, *after):
            return eng.do(lambda e: e.tensor_copy(o, i), *after)

        def red(o, i, op, *after, negate=None):
            return dve.do(lambda e: e.tensor_reduce(o, i, AX.X, op, negate=negate), *after)

        def ms(eng, o, v, *after):
            return eng.do(lambda e: e.memset(o, v), *after)

        def rcp(o, i, *after):
            return dve.do(lambda e: e.reciprocal(o, i), *after)

        def load(dst, src, *after):
            s = sem(f"s_ld{load.n}")
            load.n += 1
            sp.run(lambda e: e.dma_start(dst, src).then_inc(s, 16), *after)
            return (s, 16)
        load.n = 0

        def barrier():
            ends = [e.last for e in (pe, act, dve, pool) if e.n]
            for e in (pe, act, dve, pool):
                e.wait(ends)
            return ends

        def rsqrt(o, v, n, slot, *after):
            a, b = NR[:, 0, slot:slot + n], NR[:, 1, slot:slot + n]
            t = dve.do(lambda e: e.tensor_single_scalar(a.bitcast(I32), v.bitcast(I32), 1, ALU.logical_shift_right), *after)
            t = ts(dve, o.bitcast(I32), a.bitcast(I32), -1.0, 1597463007.0, ALU.mult, ALU.add, t)
            for _ in range(3):
                t = tt(dve, a, o, o, ALU.mult, t)
                t = stt(b, a, -0.5, v, ALU.mult, ALU.mult, t)
                t = stt(o, b, 1.5, o, ALU.add, ALU.mult, t)
            return t

        def bank(b, n=512, p0=0, p1=P):
            return PS[p0:p1, b, 0:n]

        x_keep = nc.dram_tensor("x_keep", (P, T), F32, kind="Internal").ap()

        c1 = OFF["rb"][0]
        d_cb = load(CB[:, 0:c1], A["cb"][:, 0:c1])
        d_x = load(X[:, :, :], A["x"].rearrange("(t p) f -> p t f", p=P))
        d_w2 = load(W2[:, :], A["w2"])
        sp.wait(d_cb, d_x, d_w2)
        d_cb2 = load(CB[:, c1:], A["cb"][:, c1:])
        d_cbb = load(CBB[:, :].bitcast(mybir.dt.uint16), A["cbb"])
        d_moe = []
        for e_ in range(8):
            a_ = load(W0[:, e_ * 1024:(e_ + 1) * 1024], A["mw1"][:, e_ * 1024:(e_ + 1) * 1024])
            b_ = load(W0[:, 8192 + e_ * 512:8192 + (e_ + 1) * 512], A["mw2"][:, e_ * 512:(e_ + 1) * 512])
            d_moe.append([a_, b_])
        d_wo2 = load(WO2[:, :], A["wout"])
        d_f1 = load(W1[:, :], A["f1w"])

        state = {"x": d_x, "free": []}

        def transpose_x(banks, shifted=False):
            ring = Ring(banks)
            done = []
            for b in range(NB):
                k, bk, free = ring.take()
                for j in range(4):
                    t = tr(PS[:, bk, j * 128:(j + 1) * 128], X[:, 4 * b + j, :], d_cb, state["x"], free, sig=(j == 3))
                if not shifted:
                    if b % 2:
                        u = av(XT[:, b * 512:(b + 1) * 512], bank(bk), ACT.Copy, t)
                    else:
                        u = cp(dve, XT[:, b * 512:(b + 1) * 512], bank(bk), t)
                    done.append(u)
                    ring.release(k, u)
                else:
                    u = cp(dve, XT[0:64, b * 512:(b + 1) * 512], bank(bk, p1=64), t)
                    v = av(XT[64:128, b * 512 + 1:(b + 1) * 512 + 1], bank(bk, p0=64), ACT.Copy, t)
                    done.append([u, v])
                    ring.release(k, u, v)
            return done

        def ln_block(b, src, src_tok, slot, bias=None):
            y = Y[:, slot, :, :]
            xs = X[:, 4 * b:4 * b + 4, :]
            t0 = tt(dve, y, src, xs, ALU.add, src_tok, state["x"], state.get(("y", slot)))
            t = t0
            if bias is not None:
                t = tt(dve, y, y, bias.unsqueeze(1).broadcast_to([P, 4, P]), ALU.add, t)
            for j in range(4):
                s = dve.do(lambda e, j=j: e.bn_stats(ST[:, slot, j, :], y[:, j, :]), t)
            for j in range(4):
                s = dve.do(lambda e, j=j: e.bn_aggr(MV[:, slot, j, :], ST[:, slot, j, :]), s)
            var = NR[:, 2, slot * 8:slot * 8 + 4]
            rs = NR[:, 2, 16 + slot * 8:16 + slot * 8 + 4]
            s = ts(dve, var, MV[:, slot, :, 1], 1e-5, None, ALU.add, None, s)
            s = rsqrt(rs, var, 4, slot * 8, s)
            for j in range(4):
                u = ts(dve, X[:, 4 * b + j, :], y[:, j, :], MV[:, slot, j, 0:1], rs[:, j:j + 1], ALU.subtract, ALU.mult, s)
            state[("y", slot)] = u
            return t0, u

        def l0_attn():
            wqkv, wo = W2[:, 0:384], W2[:, 384:512]
            Q, K, V = wk(0, 2048).rearrange("p (t f) -> p t f", t=NT), wk(2048, 2048).rearrange("p (t f) -> p t f", t=NT), wk(4096, NT * 129).rearrange("p (t f) -> p t f", t=NT)
            o = 4096 + NT * 129
            TMP = [wk(o + i * 512, 512) for i in range(2)]
            o += 1024
            K4 = [wk(o + i * 512, 512).rearrange("p (s f) -> p s f", s=4) for i in range(2)]
            o += 1024
            R = wk(o, 576).rearrange("p (s f) -> p s f", s=4)
            o += 576
            QT, CQT = wk(o, 2048), wk(o + 2048, 2048)
            o += 4096
            NUM = [wk(o + i * 288, 288) for i in range(2)]
            o += 576
            AO = wk(o, 2048).rearrange("p (t f) -> p t f", t=NT)
            o += 2048
            SM = [wk(o + i * 64, 64) for i in range(2)]
            o += 128
            AT = QT
            xt = transpose_x([0, 1])
            one = ms(pool, V[:, :, 128], 1.0)
            ring = Ring([2, 3])
            tmp, k4r = Ring(TMP), Ring(K4)
            kvd = None
            qd = []
            mid = {}

            def first(t):
                k, bk, free = ring.take()
                m = mm(bank(bk, 384), XT[:, t * 128:(t + 1) * 128], wqkv, True, True, d_w2, xt[t // 4], free, sig=True)
                kt, tb, tfree = tmp.take()
                qk = tb[:, 0:256]
                a = tt(dve, qk, PS[:, bk, 0:256], c("b0", 0, 256), ALU.add, m, tfree)
                v = tt(dve, V[:, t, 0:128], PS[:, bk, 256:384], c("b0", 256, 384), ALU.add, m)
                ring.release(k, v, a)
                g = qk.rearrange("p (g d) -> p g d", d=8)
                sm = SM[t % 2]
                a = red(sm[:, 0:32], g, ALU.max, a)
                a = tt(dve, g, g, sm[:, 0:32].unsqueeze(2).broadcast_to([P, 32, 8]), ALU.subtract, a)
                mid[t] = (kt, g, av(qk, qk, ACT.Exp, a), v)

            def second(t):
                kt, g, a, v = mid.pop(t)
                sm = SM[t % 2]
                a = red(sm[:, 32:64], g, ALU.add, a)
                a = rcp(sm[:, 32:64], sm[:, 32:64], a)
                r = sm[:, 32:64].unsqueeze(2).broadcast_to([P, 32, 8])
                k_ = tt(dve, K[:, t, :].rearrange("p (g d) -> p g d", d=8), g[:, 16:32, :], r[:, 16:32, :], ALU.mult, a)
                q_ = tt(dve, Q[:, t, :].rearrange("p (g d) -> p g d", d=8), g[:, 0:16, :], r[:, 0:16, :], ALU.mult, a)
                tmp.release(kt, q_)
                qd.append(q_)
                kk, kb, kfree = k4r.take()
                sn, cs = c("sin", t, t + 1), c("cos", t, t + 1)
                ts(dve, kb[:, 0, :], K[:, t, :], sn, None, ALU.mult, None, k_, kfree)
                ts(dve, kb[:, 1, :], K[:, t, :], cs, None, ALU.mult, None, k_)
                a = ts(dve, K[:, t, :], K[:, t, :], -1.0, 1.0, ALU.mult, ALU.add, dve.last)
                ts(dve, kb[:, 2, :], K[:, t, :], sn, None, ALU.mult, None, a)
                a = ts(dve, kb[:, 3, :], K[:, t, :], cs, None, ALU.mult, None, a)
                for s in range(4):
                    m = mm(bank(4 + s, 129), kb[:, s, :], V[:, t, 0:129], t == 0, t == NT - 1, a, v, one, sig=(s == 3))
                k4r.release(kk, m)
                return m
            for t in range(NT + 1):
                if t < NT:
                    first(t)
                if t:
                    m = second(t - 1)
            kvd = m
            rd = []
            for s in range(4):
                tt(dve, R[:, s, 0:128], PS[:, 4 + s, 0:128], c("bmask"), ALU.mult, kvd)
                rd.append(ts(dve, R[:, s, 128:144], c("hmask"), PS[:, 4 + s, 128:129], None, ALU.mult, None, kvd))
            ring = Ring([0, 1])
            qt = []
            for b in range(NB):
                k, bk, free = ring.take()
                for j in range(4):
                    m = tr(PS[:, bk, j * 128:(j + 1) * 128], Q[:, 4 * b + j, :], qd[4 * b + j], free, xt if b < 2 else None, sig=(j == 3))
                s_ = slice(b * 512, (b + 1) * 512)
                u = av(QT[:, s_], bank(bk), ACT.Copy, m)
                w = ts(dve, CQT[:, s_], QT[:, s_], -1.0, 1.0, ALU.mult, ALU.add, u)
                ring.release(k, u)
                qt.append([u, w])
            ring = Ring([2, 3, 4, 5])
            nr = Ring(NUM)
            aod = []
            for t in range(NT):
                s_ = slice(t * 128, (t + 1) * 128)
                toks = []
                for br, src in enumerate((QT, CQT)):
                    k, bk, free = ring.take()
                    m = mm(bank(bk, 288), src[:, s_], R[:, 2 * br:2 * br + 2, :], True, True, rd, qt[t // 4], free, sig=True)
                    toks.append((k, bk, m))
                kn, nb, nfree = nr.take()
                N = [nb[:, 0:144], nb[:, 144:288]]
                pieces = [ts(dve, N[i], PS[:, bk, 0:144], c("sin", t, t + 1), None, ALU.mult, None, m, nfree) for i, (k, bk, m) in enumerate(toks)]
                for i, (k, bk, m) in enumerate(toks):
                    pieces[i] = stt(N[i], PS[:, bk, 144:288], c("cos", t, t + 1), N[i], ALU.mult, ALU.add, pieces[i])
                    ring.release(k, pieces[i])
                n2 = nb.rearrange("p (b f) -> p b f", b=2)
                den = n2[:, :, 128:144]
                a = ts(dve, den, den, 1e-6, None, ALU.max, None, pieces)
                a = rcp(den, den, a)
                nv = n2[:, :, 0:128].rearrange("p b (h d) -> p b h d", d=8)
                pieces = tt(dve, nv, nv, den.unsqueeze(3).broadcast_to([P, 2, 16, 8]), ALU.mult, a)
                a = tt(dve, AO[:, t, :], nb[:, 0:128], nb[:, 144:272], ALU.add, pieces)
                nr.release(kn, a)
                aod.append(a)
            ring = Ring([0, 1])
            last_q = pe.last
            ev = []
            for b in range(NB):
                k, bk, free = ring.take()
                for j in range(4):
                    m = tr(PS[:, bk, j * 128:(j + 1) * 128], AO[:, 4 * b + j, :], aod[4 * b + j], qt, free, sig=(j == 3))
                u = av(AT[:, b * 512:(b + 1) * 512], bank(bk), ACT.Copy, m, last_q)
                ring.release(k, u)
                ev.append(u)
            ring = Ring([6, 7])
            res = []
            for b in range(NB):
                k, bk, free = ring.take()
                for j in range(4):
                    t = 4 * b + j
                    m = mm(PS[:, bk, j * 128:(j + 1) * 128], AT[:, t * 128:(t + 1) * 128], wo, True, True, ev[b], rd, free, sig=(j == 3))
                t0, u = ln_block(b, PS[:, bk, :].rearrange("p (t f) -> p t f", t=4), m, b % 2, c("bo0"))
                ring.release(k, t0)
                res.append(u)
            state["x"] = res[-1]

        def l0_ffn():
            G = wk(0, 128).rearrange("p (t e) -> p t e", t=NT)
            GT = wk(128, 2048)
            ACC = wk(2176, 2048).rearrange("p (t f) -> p t f", t=NT)
            H = [wk(4224 + i * 2048, 2048).rearrange("p (k n) -> p k n", k=4) for i in range(2)]
            S1 = [wk(8320 + i * 512, 512) for i in range(3)]
            L = wk(9856, 128).rearrange("p (t e) -> p t e", t=NT)
            M8 = wk(9984, 128).rearrange("p (t e) -> p t e", t=NT)
            IX = wk(10112, 128).rearrange("p (t e) -> p t e", t=NT)
            IF = wk(10240, 128).rearrange("p (t e) -> p t e", t=NT)
            GW = wk(10368, 64).rearrange("p (s t) -> p s t", s=4)
            O1 = wk(10432, 128).rearrange("p (t e) -> p t e", t=NT)
            router = W2[:, 512:520]
            xt = transpose_x([0, 1])
            for t in range(NT):
                m = mm(PS[:, 2, t * 8:t * 8 + 8], XT[:, t * 128:(t + 1) * 128], router, True, True, d_w2, xt[t // 4], sig=(t == NT - 1))
            a = tt(dve, L[:, :, :], PS[:, 2, 0:128].rearrange("p (t e) -> p t e", t=NT),
                   c("rb").unsqueeze(1).broadcast_to([P, NT, 8]), ALU.add, m)
            for t in range(NT):
                b = dve.do(lambda e, t=t: e.max(M8[:, t, :], L[:, t, :]), a)
            for t in range(NT):
                b2 = dve.do(lambda e, t=t: e.max_index(IX[:, t, :].bitcast(U32), M8[:, t, :], L[:, t, :]), b)
            a = cp(dve, IF[:, :, :], IX[:, :, :].bitcast(U32), b2)
            g = tt(dve, GW[:, 0, :], M8[:, :, 1], M8[:, :, 0], ALU.subtract, b)
            g = av(GW[:, 1, :], GW[:, 0, :], ACT.Exp, g)
            g = ts(dve, GW[:, 2, :], GW[:, 1, :], 1.0, None, ALU.add, None, g)
            g = rcp(GW[:, 2, :], GW[:, 2, :], g)
            g = tt(dve, GW[:, 3, :], GW[:, 1, :], GW[:, 2, :], ALU.mult, g)
            for t in range(NT):
                ts(dve, G[:, t, :], c("iota8"), IF[:, t, 0:1], GW[:, 2, t:t + 1], ALU.is_equal, ALU.mult, a, g)
                o1 = ts(dve, O1[:, t, :], c("iota8"), IF[:, t, 1:2], GW[:, 3, t:t + 1], ALU.is_equal, ALU.mult, a, g)
            g = tt(dve, G[:, :, :], G[:, :, :], O1[:, :, :], ALU.add, o1)
            ring = Ring([2, 3])
            gt = []
            for b_ in range(NB):
                k, bk, free = ring.take()
                for j in range(4):
                    m = tr(PS[0:8, bk, j * 128:(j + 1) * 128], G[:, 4 * b_ + j, :], g, a, free, sig=(j == 3))
                u = av(GT[0:8, b_ * 512:(b_ + 1) * 512], bank(bk, p1=8), ACT.Copy, m)
                ring.release(k, u)
                gt.append(u)
            accd = [None] * NT
            for b_ in range(NB):
                k, bk, free = ring.take()
                for j in range(4):
                    t = 4 * b_ + j
                    m = mm(PS[:, bk, j * 128:(j + 1) * 128], GT[0:8, t * 128:(t + 1) * 128], c("mb2", p1=8), True, True, gt[b_], free, sig=(j == 3))
                u = cp(dve, ACC[:, 4 * b_:4 * b_ + 4, :], PS[:, bk, :].rearrange("p (t f) -> p t f", t=4), m)
                ring.release(k, u)
                accd[b_] = u
            ring = Ring([0, 1, 2, 3, 4, 5])
            for i, u in enumerate((xt[2], xt[3], ring.free[2], ring.free[3])):
                ring.release(i, u)
            ring.free[2] = [accd[2]]
            ring.free[3] = [accd[3]]
            oring = Ring([6, 7])
            hr, s1r = Ring(H), Ring(S1)
            pend = []

            def second(e, b_, kh, hb, hd):
                k, bk, free = oring.take()
                w2e = W0[:, 8192 + e * 512:8192 + (e + 1) * 512].rearrange("p (k f) -> p k f", k=4)
                for j in range(4):
                    for kb in range(4):
                        m = mm(PS[:, bk, j * 128:(j + 1) * 128], hb[:, kb, j * 128:(j + 1) * 128], w2e[:, kb, :], kb == 0, kb == 3,
                               hd, d_moe[e], free, sig=(kb == 3 and j == 3))
                hr.release(kh, m)
                for j in range(4):
                    t = 4 * b_ + j
                    u = stt(ACC[:, t, :], PS[:, bk, j * 128:(j + 1) * 128], G[:, t, e:e + 1], ACC[:, t, :], ALU.mult, ALU.add, m, accd[b_])
                accd[b_] = u
                oring.release(k, u)

            for e in range(8):
                for b_ in range(NB):
                    kh, hb, hfree = hr.take()
                    hd = []
                    for kb in range(4):
                        k1, b1, f1 = ring.take()
                        m1 = mm(bank(b1), W0[:, e * 1024 + kb * 128:e * 1024 + (kb + 1) * 128], XT[:, b_ * 512:(b_ + 1) * 512], True, True,
                                d_moe[e], xt, f1, sig=True)
                        k2, b2, f2 = ring.take()
                        m2 = mm(bank(b2), W0[:, e * 1024 + 512 + kb * 128:e * 1024 + 512 + (kb + 1) * 128], XT[:, b_ * 512:(b_ + 1) * 512], True, True,
                                f2, sig=True)
                        ks, s1, sf = s1r.take()
                        a = av(s1, bank(b1), ACT.Silu, m1, sf, bias=c("mb1", e * 8 + kb, e * 8 + kb + 1))
                        ring.release(k1, a)
                        h = stt(hb[:, kb, :], bank(b2), c("mb1", e * 8 + 4 + kb, e * 8 + 5 + kb), s1, ALU.add, ALU.mult, m2, a, hfree)
                        ring.release(k2, h)
                        s1r.release(ks, h)
                        hd.append(h)
                        if kb == 1 and pend:
                            second(*pend.pop())
                    pend.append((e, b_, kh, hb, hd))
            second(*pend.pop())
            for b_ in range(NB):
                t0, u = ln_block(b_, ACC[:, 4 * b_:4 * b_ + 4, :], accd[b_], b_ % 2)
            state["x"] = u

        def l1_attn():
            w = W2[:, 520:1032]
            QT, KT = wk(0, 2048), wk(2048, 2048)
            K, V = wk(4096, 2048).rearrange("p (t f) -> p t f", t=NT), wk(6144, 2048).rearrange("p (t f) -> p t f", t=NT)
            DT, QD = wk(8192, 128), wk(8320, 2048)
            DROW, SC = wk(10368, 128), wk(10496, 16)
            M = wk(10512, 128)
            PT = [wk(10640 + i * 128, 128) for i in range(2)]
            OT = wk(10896, 2048)
            TM = [wk(12944 + i * 512, 512) for i in range(4)]
            xt = transpose_x([0, 1])
            p_ = c("decay")
            a = ts(dve, SC[:, 0:1], p_, -1.0, None, ALU.mult, None, d_cb)
            a = tt(dve, SC[:, 1:2], SC[:, 0:1], p_, ALU.min, a)
            a = av(SC[:, 2:3], SC[:, 1:2], ACT.Exp, a)
            a = ts(dve, SC[:, 2:3], SC[:, 2:3], 1.0, None, ALU.add, None, a)
            a = av(SC[:, 3:4], SC[:, 2:3], ACT.Ln, a)
            a = ts(dve, SC[:, 4:5], SC[:, 0:1], 0.0, SC[:, 3:4], ALU.max, ALU.add, a)
            a = ts(dve, SC[:, 5:6], SC[:, 4:5], -1.0, None, ALU.mult, None, a)
            la = SC[:, 5:6]
            d1 = av(DT, c("expn"), ACT.Exp, a, scale=la)
            d2 = av(DROW, c("trow"), ACT.Exp, a, scale=la)
            d3 = av(SC[:, 6:7], c("scol"), ACT.Exp, a, scale=la)
            d4 = av(SC[:, 8:9], c("trow", 0, 1), ACT.Exp, a, scale=la)
            d5 = ts(dve, SC[:, 9:10], la, 128.0, None, ALU.mult, None, a)
            d4 = av(SC[:, 7:8], SC[:, 9:10], ACT.Exp, d5)
            d1 = tt(dve, DT, DT, c("tri"), ALU.mult, d1)
            ring = Ring([2, 3, 4, 5])
            tr_ = Ring(TM)
            qd, kd, kvd = [], [], []
            for b in range(NB):
                s_ = slice(b * 512, (b + 1) * 512)
                k, bk, free = ring.take()
                m = mm(bank(bk), w[:, 0:128], XT[:, s_], True, True, d_w2, xt[b], free, sig=True)
                a = ts(dve, QT[:, s_], bank(bk), c("l1bq"), None, ALU.add, None, m)
                ring.release(k, a)
                a = tt(dve, QD[:, s_].rearrange("p (c n) -> p c n", n=128), QT[:, s_].rearrange("p (c n) -> p c n", n=128),
                       DROW.unsqueeze(1).broadcast_to([P, 4, 128]), ALU.mult, a, d2)
                qd.append(a)
                k, bk, free = ring.take()
                m = mm(bank(bk), w[:, 128:256], XT[:, s_], True, True, free, sig=True)
                kt, tb, tf = tr_.take()
                a = ts(dve, tb, bank(bk), c("l1bk"), 0.0, ALU.add, ALU.min, m, tf)
                a2 = ts(dve, KT[:, s_], bank(bk), c("l1bk"), 0.0, ALU.add, ALU.max, m)
                ring.release(k, a2)
                a = av(tb, tb, ACT.Exp, a)
                a = tt(dve, KT[:, s_], KT[:, s_], tb, ALU.add, a, a2)
                tr_.release(kt, a)
                kd.append(a)
            for t in range(NT):
                k, bk, free = ring.take()
                m = mm(bank(bk, 256), XT[:, t * 128:(t + 1) * 128], w[:, 128:384], True, True, free, sig=True)
                kt, tb, tf = tr_.take()
                a = tt(dve, tb[:, 0:128], PS[:, bk, 0:128], c("l1bkv", 0, 128), ALU.add, m, tf)
                v = tt(dve, V[:, t, :], PS[:, bk, 128:256], c("l1bkv", 128, 256), ALU.add, m)
                ring.release(k, v)
                x1 = ts(dve, tb[:, 128:256], tb[:, 0:128], 0.0, None, ALU.min, None, a)
                x1 = av(tb[:, 128:256], tb[:, 128:256], ACT.Exp, x1)
                x1 = stt(tb[:, 0:128], tb[:, 0:128], 0.0, tb[:, 128:256], ALU.max, ALU.add, x1)
                x1 = ts(dve, K[:, t, :], tb[:, 0:128], SC[:, 6:7], None, ALU.mult, None, x1, d3)
                tr_.release(kt, x1)
                kvd.append([x1, v])
            ring, ring2 = Ring([0, 1]), Ring([2, 3])
            ring3 = Ring([4, 5])
            ptr = Ring(PT)
            md = ms(dve, M, 0.0)
            od = []
            for t in range(NT):
                s_ = slice(t * 128, (t + 1) * 128)
                k, bk, free = ring.take()
                m = mm(bank(bk, 128), KT[:, s_], QT[:, s_], True, True, qd, kd, kvd, free, sig=True)
                kp, pb_, pf = ptr.take()
                a = tt(dve, pb_, bank(bk, 128), DT, ALU.mult, m, d1, pf)
                ring.release(k, a)
                k, bk, free = ring2.take()
                mm(bank(bk, 128), M, QD[:, s_], True, False, md, free)
                m = mm(bank(bk, 128), V[:, t, :], pb_, False, True, a, sig=True)
                ptr.release(kp, m)
                o_ = av(OT[:, s_], bank(bk, 128), ACT.Copy, m)
                ring2.release(k, o_)
                od.append(o_)
                k, bk, free = ring3.take()
                m2 = mm(bank(bk, 128), K[:, t, :], V[:, t, :], True, True, free, sig=True)
                md = stt(M, M, SC[:, 7:8], bank(bk, 128), ALU.mult, ALU.add, m2, m, d4, md)
                ring3.release(k, md)
            ring = Ring([6, 7])
            for b in range(NB):
                k, bk, free = ring.take()
                for j in range(4):
                    t = 4 * b + j
                    m = mm(PS[:, bk, j * 128:(j + 1) * 128], OT[:, t * 128:(t + 1) * 128], w[:, 384:512], True, True, od[t], free, sig=(j == 3))
                t0, u = ln_block(b, PS[:, bk, :].rearrange("p (t f) -> p t f", t=4), m, b % 2, c("l1bo"))
                ring.release(k, t0)
            state["x"] = u

        def tern(W, loaded, f):
            H1 = wk(0, 8192).rearrange("p (k n) -> p k n", k=4)
            H2 = wk(8192, 8192).rearrange("p (k n) -> p k n", k=4)
            S1 = [wk(16384 + i * 512, 512) for i in range(3)]
            w1, w2 = W[:, 0:512], W[:, 512:1024]
            h1 = W[:, 1024:3072].rearrange("p (k n) -> p k n", k=4)
            h2 = W[:, 3072:5120].rearrange("p (k n) -> p k n", k=4)
            w3 = W[:, 5120:5632].rearrange("p (k n) -> p k n", k=4)
            xt = transpose_x([0, 1])
            ring, s1r = Ring([2, 3, 4, 5, 6, 7]), Ring(S1)
            hd = [[] for _ in range(NB)]
            for b in range(NB):
                s_ = slice(b * 512, (b + 1) * 512)
                for ob in range(4):
                    o_ = slice(ob * 128, (ob + 1) * 128)
                    k1, b1, f1 = ring.take()
                    m1 = mm(bank(b1), w1[:, o_], XT[:, s_], True, True, loaded, xt[b], f1, sig=True)
                    k2, b2, f2 = ring.take()
                    m2 = mm(bank(b2), w2[:, o_], XT[:, s_], True, True, f2, sig=True)
                    ks, s1, sf = s1r.take()
                    a = av(s1, bank(b1), ACT.Silu, m1, sf, scale=c(f + "s1", ob, ob + 1))
                    ring.release(k1, a)
                    h = stt(H1[:, ob, s_], bank(b2), c(f + "s2", ob, ob + 1), s1, ALU.mult, ALU.mult, m2, a)
                    ring.release(k2, h)
                    s1r.release(ks, h)
                    hd[b].append(h)
            src, dst = H1, H2
            for wl, sc in ((h1, f + "h1"), (h2, f + "h2")):
                nd = [[] for _ in range(NB)]
                for b in range(NB):
                    s_ = slice(b * 512, (b + 1) * 512)
                    for ob in range(4):
                        k, bk, free = ring.take()
                        for kb in range(4):
                            m = mm(bank(bk), wl[:, kb, ob * 128:(ob + 1) * 128], src[:, kb, s_], kb == 0, kb == 3, hd[b], free, sig=(kb == 3))
                        a = av(dst[:, ob, s_], bank(bk), ACT.Gelu, m, hd[b], scale=c(sc, ob, ob + 1))
                        ring.release(k, a)
                        nd[b].append(a)
                hd = nd
                src, dst = dst, src
            for b in range(NB):
                k, bk, free = ring.take()
                for j in range(4):
                    t = 4 * b + j
                    for kb in range(4):
                        m = mm(PS[:, bk, j * 128:(j + 1) * 128], src[:, kb, t * 128:(t + 1) * 128], w3[:, kb, :], kb == 0, kb == 3, hd[b], free, sig=(kb == 3 and j == 3))
                p3 = PS[:, bk, :].rearrange("p (t f) -> p t f", t=4)
                a = tt(dve, XB[:, :, :], p3, c(f + "s3").unsqueeze(1).broadcast_to([P, 4, P]), ALU.mult, m, state.get("xb"))
                ring.release(k, a)
                t0, u = ln_block(b, XB[:, :, :], a, b % 2)
                state["xb"] = t0
            state["x"] = u

        def mamba():
            w_in, w_x, w_dt = W2[:, 1032:1288], W2[:, 1288:1384], W2[0:64, 1384:1512]
            PX, PZ = wk(0, 2051), wk(2051, 2051)
            o = 4102
            U, ZS = wk(o, 2048), wk(o + 2048, 2048)
            DE, DU = wk(0, 2048), wk(2048, 2048)
            LOW = wk(o + 4096, 2048)
            YA = LOW
            SPL = wk(o + 6144, 1024).bitcast(BF16)
            o += 7168
            RB = [wk(o + i * 2048, 2048) for i in range(4)]
            xt = transpose_x([0, 1])
            z = [ms(dve, PX[:, 0:1], 0.0), ms(dve, PX[:, 2049:2051], 0.0), ms(dve, PZ[:, 0:1], 0.0), ms(dve, PZ[:, 2049:2051], 0.0)]
            zs = ms(pool, SPL[96:128, :], 0.0)
            ring = Ring([2, 3, 4, 5])
            cd = []
            for h, dst in ((0, PX), (1, PZ)):
                for b in range(NB):
                    k, bk, free = ring.take()
                    m = mm(bank(bk), w_in[:, h * 128:(h + 1) * 128], XT[:, b * 512:(b + 1) * 512], True, True, d_w2, xt[b], free, sig=True)
                    a = av(dst[:, 1 + b * 512:1 + (b + 1) * 512], bank(bk), ACT.Copy, m)
                    ring.release(k, a)
                    cd.append(a)
            for src, wn, bn, dst, tmp in ((PX, "cxw", "cxb", U, RB[0]), (PZ, "czw", "czb", ZS, RB[1])):
                a = ts(dve, tmp, src[:, 0:T], c(wn, 0, 1), None, ALU.mult, None, cd, z)
                for j in range(1, 4):
                    a = stt(tmp, src[:, j:j + T], c(wn, j, j + 1), tmp, ALU.mult, ALU.add, a)
                if src is PX:
                    ud = av(dst, tmp, ACT.Silu, a, bias=c(bn))
                else:
                    zd = av(dst, tmp, ACT.Silu, a, bias=c(bn))
            conv_end = a
            BC = []
            ring = Ring([2, 3, 4, 5])
            for b in range(NB):
                s_ = slice(b * 512, (b + 1) * 512)
                k, bk, free = ring.take()
                m = mm(PS[0:64, bk, :], w_x[:, 0:64], U[:, s_], True, True, ud, zd, free, sig=True)
                l = av(LOW[0:64, s_], PS[0:64, bk, :], ACT.Copy, m)
                ring.release(k, l)
                k, bk, free = ring.take()
                m = mm(PS[0:32, bk, :], w_x[:, 64:96], U[:, s_], True, True, free, sig=True)
                p32 = RB[2][0:32, s_]
                a = cp(dve, SPL[0:32, s_], PS[0:32, bk, :], m)
                r = tt(dve, p32, PS[0:32, bk, :], SPL[0:32, s_], ALU.subtract, a)
                ring.release(k, r)
                a = cp(dve, SPL[32:64, s_], p32, r)
                pm = RB[3][0:32, s_]
                a = cp(dve, pm, SPL[32:64, s_], a)
                a = tt(dve, p32, p32, pm, ALU.subtract, a)
                a = cp(dve, SPL[64:96, s_], p32, a)
                BC.append([a, l])
            dd = []
            E1, E2 = RB[0], RB[1]
            inv2 = NR[:, 2, 100:101]
            iv = ts(dve, inv2, c("invdt"), 2.0, None, ALU.mult, None)
            for b in range(NB):
                s_ = slice(b * 512, (b + 1) * 512)
                k, bk, free = ring.take()
                m = mm(bank(bk), w_dt, LOW[0:64, s_], True, True, BC[b], free, sig=True)
                a = av(E1[:, s_], bank(bk), ACT.Abs, m, iv, bias=inv2)
                r = ts(dve, DE[:, s_], bank(bk), inv2, 0.0, ALU.add, ALU.max, a, conv_end)
                ring.release(k, a, r)
                dd.append([a, r])
            a = av(E1, E1, ACT.Exp, dd, scale=-1.0)
            a = ts(dve, E1, E1, 1.0, None, ALU.add, None, a)
            a = av(E2, E1, ACT.Ln, a)
            a = tt(dve, DE, DE, E2, ALU.add, a)
            dl = tt(dve, DU, DE, U, ALU.mult, a)
            ya = ts(pool, YA, U, c("Dp"), None, ALU.mult, None, BC, dd, ud, zs)
            ra, rh = Ring(RB[0:2]), Ring(RB[2:4])
            for r_ in (ra, rh):
                for i in range(len(r_.bufs)):
                    r_.release(i, dl)
            rB, rC = Ring([0, 1, 2, 3]), Ring([4, 5, 6, 7])
            for i in range(4):
                rB.release(i, dd)
                rC.release(i, dd)
            for n in range(16):
                ka, da, fa = ra.take()
                e_ = av(da, DE, ACT.Exp, dl, fa, scale=-float(n + 1))
                kh, hb, fh = rh.take()
                for b in range(NB):
                    s_ = slice(b * 512, (b + 1) * 512)
                    k, bk, free = rB.take()
                    m = mm(bank(bk), cb("selB", n * 128, (n + 1) * 128), SPL[:, s_], True, True, BC, zs, d_cbb, free, sig=True)
                    w_ = tt(dve, hb[:, s_], DU[:, s_], bank(bk), ALU.mult, m, fh)
                    rB.release(k, w_)
                s = dve.do(lambda e, hb=hb, da=da: e.tensor_tensor_scan(hb, da, hb, 0.0, ALU.mult, ALU.add), e_, w_)
                ra.release(ka, s)
                for b in range(NB):
                    s_ = slice(b * 512, (b + 1) * 512)
                    k, bk, free = rC.take()
                    m = mm(bank(bk), cb("selC", n * 128, (n + 1) * 128), SPL[:, s_], True, True, free, sig=True)
                    w_ = tt(dve, hb[:, s_], hb[:, s_], bank(bk), ALU.mult, m, s)
                    rC.release(k, w_)
                ya = tt(pool, YA, YA, hb, ALU.add, w_, ya)
                rh.release(kh, ya)
            ring = Ring([0, 1])
            wo = A_wout
            ring.release(0, rB.free[0])
            ring.release(1, rB.free[1])
            for b in range(NB):
                k, bk, free = ring.take()
                for j in range(4):
                    t = 4 * b + j
                    s_ = slice(t * 128, (t + 1) * 128)
                    mm(PS[:, bk, j * 128:(j + 1) * 128], YA[:, s_], wo[0], True, False, ya, d_wo2, free)
                    m = mm(PS[:, bk, j * 128:(j + 1) * 128], ZS[:, s_], wo[1], False, True, zd, sig=(j == 3))
                t0, u = ln_block(b, PS[:, bk, :].rearrange("p (t f) -> p t f", t=4), m, b % 2, c("bout"))
                ring.release(k, t0)
            state["x"] = u

        def local_layer(l):
            o0 = l * 3114
            wqkv = W0[:, o0:o0 + 1536]
            wo = W0[:, o0 + 1536:o0 + 2048].rearrange("p (k f) -> p k f", k=4)
            w1 = W0[:, o0 + 2048:o0 + 2730]
            w2 = W0[:, o0 + 2730:o0 + 3114].rearrange("p (k f) -> p k f", k=3)
            o = [0]

            def take(n):
                o[0] += n
                return wk(o[0] - n, n)
            CT = take(2048).rearrange("p (t s d) -> p t s d", t=NT, s=2)
            SN = take(2048).rearrange("p (t s d) -> p t s d", t=NT, s=2)
            QK = [take(1024) for _ in range(2)]
            RO = [take(1024) for _ in range(2)]
            PB = take(1024)
            VV = [take(520).rearrange("p (h d) -> p h d", h=8) for _ in range(4)]
            QT = [take(512).rearrange("p (h n) -> p h n", h=4) for _ in range(2)]
            KZ = [take(1024).rearrange("p (h n) -> p h n", h=8) for _ in range(3)]
            PT = [take(1536).rearrange("p (h n) -> p h n", h=8) for _ in range(2)]
            O, OTT = take(512), take(512)
            SS, RS_ = take(32), take(32)
            NM = [take(8) for _ in range(2)]
            N3 = [take(64).bitcast(BF16) for _ in range(2)]
            DEN = take(8)
            tab = W1[:, 2560:5632].rearrange("p (s c t d) -> p s c t d", s=2, c=3, t=NT)
            td = None
            for s in range(2):
                for hf in range(2):
                    sc = c("qks", l * 128 + s * 64 + hf * 32, l * 128 + s * 64 + hf * 32 + 32).unsqueeze(1).broadcast_to([P, NT, 32])
                    td = tt(pool, CT[:, :, s, hf * 32:hf * 32 + 32], tab[:, s, 0, :, :], sc, ALU.mult, d_l3w, td)
                    oh = 1 - hf
                    td = tt(pool, SN[:, :, s, oh * 32:oh * 32 + 32], tab[:, s, 2 if oh == 0 else 1, :, :], sc, ALU.mult, td)
            zz = [ms(dve, k_[:, :, :], 0.0) for k_ in KZ] + [ms(dve, n_[0:96, :], 0.0) for n_ in N3]
            zv = [ms(dve, v_[:, :, 64], 1.0) for v_ in VV]
            if l == 0:
                state["kept"] = load(x_keep, X[:, :, :].rearrange("p t f -> p (t f)"), state["x"])
            z0 = ms(dve, XT[64:128, 0:1], 0.0)
            xt = transpose_x([0, 1], shifted=True)
            ra = Ring([0, 2])
            rb = Ring([4, 6])
            ra.release(0, xt)
            ra.release(1, xt)
            qkr, ror, qtr, kzr, ptr, vr = Ring(QK), Ring(RO), Ring(QT), Ring(KZ), Ring(PT), Ring(VV)
            tl = [dict() for _ in range(NT)]
            hold = {"O": None, "OTT": None, "PB": None, "N": None, "SS": None}

            def s0(t):
                d = tl[t]
                s_ = slice(t * 128, (t + 1) * 128)
                xd = [z0, xt[t // 4], xt[max(t * 128 - 1, 0) // 512]]
                k, bk, free = ra.take()
                mm(bank(bk), XT[:, s_], wqkv[:, 0:512], True, True, d_l2, xd, free)
                m = mm(bank(bk + 1), XT[:, s_], wqkv[:, 512:1024], True, True, sig=True)
                kq, qb_, qf = qkr.take()
                a = av(qb_.rearrange("p (b n) -> p b n", b=2), PS[:, bk:bk + 2, :], ACT.Copy, m, qf)
                ra.release(k, a)
                d["qk"] = (kq, qb_, a)
                k, bk, free = ra.take()
                m = mm(bank(bk), XT[:, s_], wqkv[:, 1024:1536], True, True, free, sig=True)
                kv, vb, vf = vr.take()
                v = av(vb[:, :, 0:64], PS[:, bk, :].rearrange("p (h d) -> p h d", h=8), ACT.Copy, m, vf, zv)
                ra.release(k, v)
                d["v"] = (kv, vb, v)
                kr, rbuf, rf = ror.take()
                sq = av(rbuf, qb_, ACT.Square, a, rf)
                d["ro"] = (kr, rbuf, sq)

            def s0v(t):
                d = tl[t]
                kq, qb_, a = d["qk"]
                kr, rbuf, sq = d["ro"]
                ss, rs = SS[:, 0:16], RS_[:, 0:16]
                g = red(ss, rbuf.rearrange("p (h d) -> p h d", h=16), ALU.add, sq, hold["SS"])
                g = ts(dve, ss, ss, 1e-24, None, ALU.max, None, g)
                g = rsqrt(rs, ss, 16, 32, g)
                q4 = qb_.rearrange("p (h d) -> p h d", h=16)
                g = tt(dve, q4, q4, rs.unsqueeze(2).broadcast_to([P, 16, 64]), ALU.mult, g, a)
                hold["SS"] = g
                v = tt(dve, rbuf.rearrange("p (s h d) -> p s h d", s=2, h=8), qb_.rearrange("p (s h d) -> p s h d", s=2, h=8),
                       CT[:, t, :, :].unsqueeze(2).broadcast_to([P, 2, 8, 64]), ALU.mult, g, td)
                q5 = qb_.rearrange("p (s h f d) -> p s h f d", s=2, h=8, f=2)
                p5 = PB.rearrange("p (s h f d) -> p s h f d", s=2, h=8, f=2)
                for hf in range(2):
                    w_ = tt(pool, p5[:, :, :, hf, :], q5[:, :, :, 1 - hf, :],
                            SN[:, t, :, hf * 32:hf * 32 + 32].unsqueeze(2).broadcast_to([P, 2, 8, 32]), ALU.mult, g, td, hold["PB"])
                qkr.release(kq, w_, v)
                r = tt(dve, rbuf, rbuf, PB, ALU.add, w_, v)
                hold["PB"] = r
                d["rot"] = r

            def s1(t):
                d = tl[t]
                kr, rbuf, _ = d["ro"]
                k, bk, free = ra.take()
                for j in range(8):
                    m = tr(PS[:, bk + j // 4, (j % 4) * 128:(j % 4 + 1) * 128], rbuf[:, j * 128:(j + 1) * 128], d["rot"], free, sig=(j == 7))
                ror.release(kr, m)
                kq, q_, qf = qtr.take()
                kz, z_, zf = kzr.take()
                a = av(q_, PS[:, bk, :].rearrange("p (h n) -> p h n", h=4), ACT.Copy, m, qf)
                pv = PS[:, bk + 1, :].rearrange("p (h n) -> p h n", h=4)
                z4 = z_.rearrange("p (h a) n -> p h a n", a=2)
                b1 = av(z4[0:64, :, 0, :], pv[0:64, :, :], ACT.Copy, m, zf, zz)
                b2 = av(z4[64:128, :, 1, :], pv[64:128, :, :], ACT.Copy, m, zf, zz)
                ra.release(k, a, b2)
                d["q"], d["k"] = (kq, q_, a), (kz, z_, b2)

            def s2(t):
                d = tl[t]
                _, q_, qd = d["q"]
                _, z_, zd = d["k"]
                nm = NM[t % 2]
                for hg in range(2):
                    k, bk, free = rb.take()
                    for i in range(4):
                        h = hg * 4 + i
                        b_, c0 = bk + i // 2, (i % 2) * 192
                        if t:
                            mm(PS[:, b_, c0:c0 + 192], cb("identb"), cb("maskS"), True, False, d_cbb, free, qd, zd)
                            mm(PS[:, b_, c0:c0 + 64], q_[:, h // 2, :], tl[t - 1]["k"][1][:, h, 64:128], False, False)
                        else:
                            mm(PS[:, b_, c0 + 64:c0 + 192], cb("identb"), cb("maskS", 64, 192), True, False, d_cbb, free, qd, zd)
                        m = mm(PS[:, b_, c0 + 64:c0 + 192], q_[:, h // 2, :], z_[:, h, :], False, True, sig=(i == 3))
                    lo = 0 if t else 64
                    src = PS[:, bk:bk + 2, 0:384].rearrange("p b (h n) -> p b h n", h=2)[:, :, :, lo:192]
                    r = red(nm[:, hg * 4:hg * 4 + 4], src, ALU.max, m, negate=True)
                    rb.release(k, r)
                d["nm"] = r

            def s3(t):
                d = tl[t]
                nm, n3 = NM[t % 2], N3[t % 2]
                k, bk, free = ra.take()
                m = tr(PS[0:8, bk, 0:128], nm, d["nm"], free, sig=True)
                src = PS[0:8, bk, 0:128]
                a = cp(dve, n3[0:8, :], src, m, tl[t - 2].get("st") if t > 1 else None, zz)
                a = tt(dve, n3[32:40, :], src, n3[0:8, :], ALU.subtract, a)
                ra.release(k, a)
                d["n3"] = a

            def s4(t):
                d = tl[t]
                n3 = N3[t % 2]
                _, q_, qd = d["q"]
                _, z_, zd = d["k"]
                kp, p_, pf = ptr.take()
                for hg in range(2):
                    k, bk, free = rb.take()
                    for i in range(4):
                        h = hg * 4 + i
                        b_, c0 = bk + i // 2, (i % 2) * 192
                        A_, B_ = PS[:, b_, c0:c0 + 128], PS[:, b_, c0 + 128:c0 + 192]
                        sel = cb("selm", h * 128, (h + 1) * 128, p1=96)
                        mm(A_, cb("identb"), cb("maskA"), True, False, free)
                        mm(A_, sel, n3[0:96, :], False, False, d["n3"])
                        m = mm(A_, z_[:, h, :], q_[:, h // 2, :], False, True, sig=(i == 3 and not t))
                        if t:
                            mm(B_, cb("identb"), cb("maskB"), True, False)
                            mm(B_, sel, n3[0:96, 0:64], False, False)
                            m = mm(B_, tl[t - 1]["k"][1][:, h, :], q_[:, h // 2, 0:64], False, True, sig=(i == 3))
                    hi = 192 if t else 128
                    for bb in range(2):
                        src = PS[:, bk + bb, 0:384].rearrange("p (h n) -> p h n", h=2)
                        a = av(p_[:, hg * 4 + 2 * bb:hg * 4 + 2 * bb + 2, 0:hi], src[:, :, 0:hi], ACT.Exp, m, pf)
                    rb.release(k, a)
                d["st"] = m
                qtr.release(d["q"][0], m)
                if t:
                    kzr.release(tl[t - 1]["k"][0], m)
                d["p"] = (kp, p_, a)

            def s5(t):
                d = tl[t]
                kp, p_, pd = d["p"]
                k, bk, free = ra.take()
                for h in range(8):
                    o_ = PS[:, bk + h // 4, (h % 4) * 65:(h % 4 + 1) * 65]
                    m = mm(o_, p_[:, h, 0:128], d["v"][1][:, h, :], True, True, pd, d["v"][2], free, sig=(h == 7 and not t))
                    if t:
                        m = mm(o_[0:64, :], p_[:, h, 128:192], tl[t - 1]["v"][1][:, h, :], False, True, sig=(h == 7), skip=True)
                ptr.release(kp, m)
                if t:
                    vr.release(tl[t - 1]["v"][0], m)
                src = PS[:, bk:bk + 2, 0:260].rearrange("p b (h d) -> p b h d", h=4)
                a = rcp(DEN.rearrange("p (b h) -> p b h", b=2), src[:, :, :, 64], m, hold["O"])
                a = tt(dve, O.rearrange("p (b h d) -> p b h d", b=2, h=4), src[:, :, :, 0:64],
                       DEN.rearrange("p (b h) -> p b h", b=2).unsqueeze(3).broadcast_to([P, 2, 4, 64]), ALU.mult, a, hold["O"])
                ra.release(k, a)
                d["o"] = a

            def s6(t):
                d = tl[t]
                k, bk, free = ra.take()
                for j in range(4):
                    m = tr(PS[:, bk, j * 128:(j + 1) * 128], O[:, j * 128:(j + 1) * 128], d["o"], free, sig=(j == 3))
                hold["O"] = m
                a = av(OTT, bank(bk), ACT.Copy, m, hold["OTT"])
                for j in range(4):
                    m = mm(bank(bk + 1, 128), OTT[:, j * 128:(j + 1) * 128], wo[:, j, :], j == 0, j == 3, a, sig=(j == 3))
                hold["OTT"] = m
                x = tt(dve, X[:, t, :], X[:, t, :], bank(bk + 1, 128), ALU.add, m, xt, state["kept"])
                ra.release(k, x)
                state["x"] = x

            for i in range(NT + 3):
                if 3 <= i:
                    s5(i - 3)
                if i < NT:
                    s0(i)
                if 2 <= i < NT + 2:
                    s2(i - 2)
                if 3 <= i:
                    s6(i - 3)
                if 2 <= i < NT + 2:
                    s3(i - 2)
                if 1 <= i <= NT:
                    s1(i - 1)
                if 2 <= i < NT + 2:
                    s4(i - 2)
                if i < NT:
                    s0v(i)
            barrier()
            HN = wk(0, 2048)
            FH = [wk(2048 + i * 1536, 1536).rearrange("p (k n) -> p k n", k=3) for i in range(2)]
            GE = [wk(5120 + i * 512, 512) for i in range(3)]
            xt = transpose_x([0, 1], shifted=True)
            r2 = Ring([2, 3])
            hnd = []
            for b in range(NB):
                k, bk, free = r2.take()
                sl = b % 2
                for j in range(4):
                    t = 4 * b + j
                    m = tr(PS[:, bk, j * 128:(j + 1) * 128], XT[:, t * 128:(t + 1) * 128], xt[b], xt[max(b - 1, 0)], free, sig=(j == 3))
                for j in range(4):
                    s = dve.do(lambda e, j=j, bk=bk, sl=sl: e.bn_stats(ST[:, sl, j, :], PS[:, bk, j * 128:(j + 1) * 128]), m)
                for j in range(4):
                    s2_ = dve.do(lambda e, j=j, sl=sl: e.bn_aggr(MV[:, sl, j, :], ST[:, sl, j, :]), s)
                var, rs = NR[:, 2, sl * 8:sl * 8 + 4], NR[:, 2, 16 + sl * 8:20 + sl * 8]
                s = ts(dve, var, MV[:, sl, :, 1], 1e-5, None, ALU.add, None, s2_)
                s = rsqrt(rs, var, 4, sl * 8, s)
                for j in range(4):
                    u = ts(dve, Y[:, sl, j, :], PS[:, bk, j * 128:(j + 1) * 128], MV[:, sl, j, 0:1], rs[:, j:j + 1], ALU.subtract, ALU.mult, s, state.get(("y", sl)))
                r2.release(k, u)
                k, bk, free = r2.take()
                for j in range(4):
                    m = tr(PS[:, bk, j * 128:(j + 1) * 128], Y[:, sl, j, :], u, free, sig=(j == 3))
                state[("y", sl)] = m
                a = av(HN[:, b * 512:(b + 1) * 512], bank(bk), ACT.Identity, m, scale=c("lg", l, l + 1), bias=c("lb", l, l + 1))
                r2.release(k, a)
                hnd.append(a)
            if l == 1:
                X5 = wk(8192, 2048)
                d_ = load(X5, x_keep, state["kept"], pe.last, act.last, dve.last, pool.last)
                state["x"] = tt(pool, X[:, :, :], X[:, :, :], X5.rearrange("p (t f) -> p t f", t=NT), ALU.add, d_, xt)
            ring, ger, fhr, oring = Ring([4, 5, 6, 7]), Ring(GE), Ring(FH), Ring([0, 1])
            oring.release(0, xt)
            oring.release(1, xt)
            for b in range(NB):
                s_ = slice(b * 512, (b + 1) * 512)
                kf, fb, ff = fhr.take()
                hd = []
                for kb, (off, w_) in enumerate(BLK3):
                    k1, b1, f1 = ring.take()
                    m1 = mm(bank(b1, p1=w_), w1[:, HID2 + off:HID2 + off + w_], HN[:, s_], True, True, hnd[b], f1, sig=True)
                    k2, b2, f2 = ring.take()
                    m2 = mm(bank(b2, p1=w_), w1[:, off:off + w_], HN[:, s_], True, True, f2, sig=True)
                    kg, ge, gf = ger.take()
                    a = av(ge[0:w_, :], bank(b1, p1=w_), ACT.Gelu, m1, gf, bias=c("fb1", l * 6 + 3 + kb, l * 6 + 4 + kb, p1=w_))
                    ring.release(k1, a)
                    h = stt(fb[0:w_, kb, :], bank(b2, p1=w_), c("fb1", l * 6 + kb, l * 6 + kb + 1, p1=w_), ge[0:w_, :], ALU.add, ALU.mult, m2, a, ff)
                    ring.release(k2, h)
                    ger.release(kg, h)
                    hd.append(h)
                k, bk, free = oring.take()
                for j in range(4):
                    for kb, (off, w_) in enumerate(BLK3):
                        m = mm(PS[:, bk, j * 128:(j + 1) * 128], fb[0:w_, kb, j * 128:(j + 1) * 128], w2[0:w_, kb, :], kb == 0, kb == 2, hd, free, sig=(j == 3 and kb == 2))
                fhr.release(kf, m)
                pv = PS[:, bk, :].rearrange("p (t f) -> p t f", t=4)
                if l == 0:
                    xs = X[:, 4 * b:4 * b + 4, :]
                    u = tt(dve, xs, pv, xs, ALU.add, m, state["x"])
                    oring.release(k, u)
                    u = tt(dve, xs, xs, c("fb2", 0, 128).unsqueeze(1).broadcast_to([P, 4, P]), ALU.add, u)
                else:
                    t0, u = ln_block(b, pv, m, b % 2, c("fb2", 128, 256))
                    oring.release(k, t0)
            state["x"] = u

        def l3_attn():
            wq, wkv, ow = W1[:, 0:1024], W1[:, 1024:1536], W1[:, 1536:2560].rearrange("p (k f) -> p k f", k=8)
            K1 = wk(0, 4096).bitcast(F16).rearrange("p (g n) -> p g n", g=4)
            K2 = wk(4096, 4096).bitcast(F16).rearrange("p (g n) -> p g n", g=4)
            OT = wk(8192, 4096).rearrange("p (h n) -> p h n", h=8)
            PTB = [wk(12288 + i * 512, 512) for i in range(6)]
            OU = wk(18432, 512)
            QF = [wk(15360 + i * 512, 512) for i in range(2)]
            RC = XB[:, :, :].rearrange("p t f -> p (t f)")
            V = W0[:, 0:4096].rearrange("p (t g d) -> p t g d", t=NT, g=4)
            AC = [W0[:, 4096 + i * 512:4608 + i * 512] for i in range(4)]
            Q1 = [wk(16384 + i * 256, 256).bitcast(F16) for i in range(4)]
            Q2 = [wk(17408 + i * 256, 256).bitcast(F16) for i in range(4)]
            SC, QBS = NR[:, 0, 64:80], NR[:, 0, 80:96]
            PM = [NR[:, 1, 64 + i * 8:72 + i * 8].rearrange("p (t s) -> p t s", t=4) for i in range(4)]
            NM = [NR[:, 1, 128 + i * 4:132 + i * 4] for i in range(4)]
            xt = transpose_x([0, 1])
            a = ts(dve, SC[:, 0:1], c("scal"), -1.0, None, ALU.mult, None)
            a = tt(dve, SC[:, 1:2], SC[:, 0:1], c("scal"), ALU.min, a)
            a = av(SC[:, 2:3], SC[:, 1:2], ACT.Exp, a)
            a = ts(dve, SC[:, 2:3], SC[:, 2:3], 1.0, None, ALU.add, None, a)
            a = av(SC[:, 3:4], SC[:, 2:3], ACT.Ln, a)
            a = ts(dve, SC[:, 4:5], c("scal"), 0.0, SC[:, 3:4], ALU.max, ALU.add, a)
            scd = ts(dve, SC[:, 5:6], SC[:, 4:5], 8.0 * 1.442695041, None, ALU.mult, None, a)
            scale = SC[:, 5:6]
            qbd = ts(dve, QBS, c("qb"), scale, None, ALU.mult, None, scd)
            zq = [ms(dve, q_[64:128, :], 0.0) for q_ in Q2]
            WQ2, WK2 = W1[:, 2560:4608], W1[:, 4608:5120]
            wd = [cp(dve, WK2.rearrange("p (h a d) -> p h a d", a=2, d=64), wkv[:, 0:256].rearrange("p (h d) -> p h d", d=64).unsqueeze(2).broadcast_to([P, 4, 2, 64]), d_l3w),
                  cp(pool, WQ2.rearrange("p (h a d) -> p h a d", a=2, d=64), wq.rearrange("p (h d) -> p h d", d=64).unsqueeze(2).broadcast_to([P, 16, 2, 64]), d_l3w)]
            ring = Ring([2, 3, 4, 5])
            kd = [[] for _ in range(4)]
            for g in range(4):
                wk2 = WK2[:, g * 128:(g + 1) * 128]
                for b in range(NB):
                    s_ = slice(b * 512, (b + 1) * 512)
                    k, bk, free = ring.take()
                    m = mm(bank(bk), wk2, XT[:, s_], True, True, wd, xt[b], free, sig=True)
                    a = av(K2[:, g, s_], bank(bk), ACT.Identity, m, bias=c("kb", g, g + 1))
                    a2 = stt(K1[64:128, g, s_], bank(bk, p0=64), c("kb", g, g + 1, p0=64), K2[64:128, g, s_], ALU.add, ALU.subtract, a)
                    ring.release(k, a2)
                    a3 = cp(dve, K1[0:64, g, s_], K2[0:64, g, s_], a)
                    z = ms(dve, K2[64:128, g, s_], 0.0, a2)
                    kd[g] += [a, a2, a3, ms(dve, K2[64:65, g, s_], 64.0, z)]
            vd = []
            for t in range(NT):
                k, bk, free = ring.take()
                m = mm(bank(bk, 256), XT[:, t * 128:(t + 1) * 128], wkv[:, 256:512], True, True, free, sig=True)
                a = tt(dve, V[:, t, :, :], PS[:, bk, 0:256].rearrange("p (g d) -> p g d", g=4), c("vb").rearrange("p (g d) -> p g d", g=4), ALU.add, m)
                ring.release(k, a)
                vd.append(a)
            setup = [e.last for e in (act, dve, pool)]
            mr, sr, orr, misc = Ring([0, 2]), Ring([4, 5]), Ring([6]), Ring([7])
            qr = [Ring([0, 1]), Ring([2, 3])]
            ptr, acr = Ring(PTB), Ring(AC)
            rcf = {"rc": None, "ot": None}
            jobs = [(b, pr) for b in range(NB) for pr in range(8)]
            info = {}
            qff = [None, None]

            def prefetch(job):
                b, pr = job
                g = pr // 2
                d = {"q": [None, None]}
                info[job] = d

                def qproj(i):
                    h = 2 * pr + i
                    k, bk, free = misc.take()
                    w_ = WQ2[:, h * 128:(h + 1) * 128]
                    m = mm(bank(bk), w_, XT[:, b * 512:(b + 1) * 512], True, True, xt, free, setup, sig=True)
                    kq, qi, qf = qr[i].take()
                    a = av(Q1[qi], bank(bk), ACT.Identity, m, qf, qbd, scd, scale=scale, bias=QBS[:, h:h + 1])
                    a1 = av(QF[i][0:64, :], bank(bk, p1=64), ACT.Identity, qff[i], scale=scale[0:64, :], bias=QBS[0:64, h:h + 1])
                    misc.release(k, a1)
                    a2 = tt(dve, Q2[qi][0:64, :], QF[i][0:64, :], Q1[qi][0:64, :], ALU.subtract, a1, zq[-1], qf)
                    qff[i] = a2
                    d["q"][i] = (kq, qi, a, a2)

                def maxes(i, t, hf):
                    _, qi, a, _ = d["q"][i]
                    k, bk, free = mr.take()
                    for n in range(2):
                        o_ = hf * 1024 + n * 512
                        m = mm(bank(bk + n), Q1[qi][:, t * 128:(t + 1) * 128], K1[:, g, o_:o_ + 512], True, True, a, kd[g], free, setup, sig=(n == 1))
                    r = red(PM[qi][:, t, hf:hf + 1], PS[:, bk:bk + 2, :].rearrange("p b n -> p (b n)"), ALU.max, m)
                    mr.release(k, r)
                    d[("m", i)] = r

                def rowmax(i):
                    kq, qi, a, a2 = d["q"][i]
                    r = red(NM[qi], PM[qi], ALU.max, d[("m", i)], negate=True)
                    k, bk, free = misc.take()
                    for t in range(4):
                        m = mm(PS[64:65, bk, t * 128:(t + 1) * 128], NM[qi][:, t:t + 1], c("ident"), True, True, r, free, sig=(t == 3))
                    u = av(Q2[qi][64:65, :], PS[64:65, bk, :], ACT.Copy, m, zq, scale=1.0 / 64)
                    misc.release(k, u)
                    d[("r", i)] = [u, a, a2]

                steps = [lambda: (qproj(0), qproj(1))]
                for t in range(4):
                    for hf in range(2):
                        for i in range(2):
                            steps.append(lambda i=i, t=t, hf=hf: maxes(i, t, hf))
                steps.append(lambda: rowmax(0))
                steps.append(lambda: rowmax(1))
                return steps

            def finish(b):
                k, bk, free = misc.take()
                for j in range(4):
                    for pr in range(8):
                        m = mm(PS[:, bk, j * 128:(j + 1) * 128], OT[:, pr, j * 128:(j + 1) * 128], ow[:, pr, :], pr == 0, pr == 7, rcf["otd"], free, sig=(j == 3 and pr == 7))
                rcf["ot"] = m
                t0, u = ln_block(b, PS[:, bk, :].rearrange("p (t f) -> p t f", t=4), m, b % 2, c("ob"))
                misc.release(k, t0)
                state["x2"] = u

            for s in prefetch(jobs[0]):
                s()
            for ji, job in enumerate(jobs):
                b, pr = job
                g = pr // 2
                d = info[job]
                nxt = prefetch(jobs[ji + 1]) if ji + 1 < len(jobs) else []
                ko, ob, of = orr.take()
                ac = [acr.take() for _ in range(2)]
                acd = [None, None]
                pend = None

                def pv(kt, pts):
                    for i, (kp, p_, a) in enumerate(pts):
                        m = mm(PS[64 * i:64 * i + 64, ob, :], V[:, kt, g, :], p_, kt == 0, kt == 15, a, vd[kt], of, sig=True)
                        eng = pool if i else dve
                        if kt == 0:
                            u = cp(eng, ac[i][1], p_, a, ac[i][2], pool.last)
                        else:
                            u = tt(eng, ac[i][1], ac[i][1], p_, ALU.add, a, acd[i])
                        acd[i] = u
                        ptr.release(kp, m, u)
                    return m
                for kt in range(NT):
                    pts = []
                    for i in range(2):
                        kq, qi, a, _ = d["q"][i]
                        k, bk, free = sr.take()
                        s_ = slice(kt * 128, (kt + 1) * 128)
                        mm(bank(bk), K1[:, g, s_], Q1[qi], True, False, d[("r", i)], kd[g], free)
                        m = mm(bank(bk), K2[:, g, s_], Q2[qi], False, True, sig=True)
                        if kt == NT - 1:
                            qr[i].release(kq, m)
                        kp, p_, pf = ptr.take()
                        a = av(p_, bank(bk), ACT.Exp, m, pf, scale=1.0 / 64)
                        sr.release(k, a)
                        pts.append((kp, p_, a))
                    if pend:
                        pv(*pend)
                    pend = (kt, pts)
                    for _ in range(2 if kt in (1, 4, 7, 15) else 1):
                        if nxt:
                            nxt.pop(0)()
                m = pv(*pend)
                ou = av(OU, bank(ob), ACT.Copy, m, rcf["rc"])
                orr.release(ko, ou)
                for s in nxt:
                    s()
                k, bk, free = misc.take()
                for i in range(2):
                    m2 = mm(PS[64 * i:64 * i + 64, bk, :], c("ones", 0, 64), ac[i][1], True, True, acd[i], free, sig=True)
                    acr.release(ac[i][0], m2)
                r = rcp(RC, bank(bk), m2, rcf["rc"])
                misc.release(k, r)
                r = tt(dve, OT[:, pr, :], OU, RC, ALU.mult, r, ou, rcf["ot"])
                rcf["rc"] = rcf["otd"] = r
                if pr == 7:
                    finish(b)
            state["x"] = state["x2"]

        A_wout = [WO2[:, 0:128], WO2[:, 128:256]]

        phases = [l0_attn, l0_ffn, l1_attn, lambda: tern(W1[:, :], d_f1, "f1"), mamba,
                  lambda: (local_layer(0), barrier(), local_layer(1)), l3_attn, lambda: tern(W0[:, 6228:11860], d_f3, "f3")]
        pe.wait(d_cb)
        act.wait(d_cb)
        dve.wait(d_cb)
        pool.wait(d_cb)
        for i_, ph in enumerate(phases[:upto]):
            ph()
            ends = barrier()
            if i_ == 0:
                for e in (pe, act, dve, pool):
                    e.wait(d_cb2)
            if i_ == 1:
                d_l2 = load(W0[:, 0:6228], A["l2w"], ends)
                d_f3 = load(W0[:, 6228:11860], A["f3w"])
            if i_ == 3:
                d_l3w = load(W1[:, :], A["l3w"], ends)

        s_out = sem("s_out")
        sp.run(lambda e: e.dma_start(out.rearrange("(t p) f -> p t f", p=P), X[:, :, :]).then_inc(s_out, 16), state["x"])
        sp.wait((s_out, 16))

        block = ctx.enter_context(nc.Block())

        @block.sync
        def _(eng):
            for op in sp.ops:
                op(eng)

        @block.tensor
        def _(eng):
            for op in pe.ops:
                op(eng)

        @block.scalar
        def _(eng):
            for op in act.ops:
                op(eng)

        @block.vector
        def _(eng):
            for op in dve.ops:
                op(eng)

        @block.gpsimd
        def _(eng):
            for op in pool.ops:
                op(eng)


def cols(v):
    return np.ascontiguousarray(v.reshape(-1, P).T)


def rows(v):
    return np.broadcast_to(v.reshape(1, -1), (P, v.size))


def tall(a):
    k = a.shape[0] // P
    return np.ascontiguousarray(a.reshape(k, P, -1).transpose(1, 0, 2).reshape(P, -1))


def pad_rows(a, n=P):
    o = np.zeros((n,) + a.shape[1:], a.dtype)
    o[:a.shape[0]] = a
    return o


def twice(a):
    return np.concatenate([a, a], 0)


def lay_out(i):
    f = np.float32
    t = np.arange(T)
    s = {}
    ar = np.arange(P)
    s["ident"] = np.eye(P, dtype=f)
    s["bmask"] = (ar[:, None] // 8 == ar[None] // 8).astype(f)
    s["hmask"] = (ar[:, None] // 8 == np.arange(16)[None]).astype(f)
    idx = (f(np.pi / 2) * np.arange(1, T + 1, dtype=f) / f(T)).astype(f)
    s["sin"], s["cos"] = cols(np.sin(idx).astype(f)), cols(np.cos(idx).astype(f))
    s["ones"] = np.ones((P, P), f)
    s["b0"] = rows(np.concatenate([i["L0_attn_bq"], i["L0_attn_bk"], i["L0_attn_bv"]]))
    s["bo0"] = rows(i["L0_attn_bo"])
    s["rb"] = rows(i["L0_ffn_router_b"])
    s["iota8"] = rows(np.arange(8, dtype=f))
    s["mb1"] = cols(i["L0_ffn_b1"].reshape(-1))
    s["mb2"] = pad_rows(i["L0_ffn_b2"])
    s["l1bq"], s["l1bk"] = cols(i["L1_attn_bq"]), cols(i["L1_attn_bk"])
    s["l1bkv"] = rows(np.concatenate([i["L1_attn_bk"], i["L1_attn_bv"]]))
    s["l1bo"] = rows(i["L1_attn_bo"])
    s["decay"] = np.broadcast_to(np.asarray(i["L1_attn_decay_param"]).reshape(1, 1), (P, 1))
    n = ar[None, :] - 1 - ar[:, None]
    s["expn"] = np.maximum(n, 0).astype(f)
    s["tri"] = (n >= 0).astype(f)
    s["trow"] = rows(ar.astype(f))
    s["scol"] = (127 - ar).astype(f).reshape(P, 1)
    for k, m in (("f1", "L1_ffn_"), ("f3", "L3_ffn_")):
        s[k + "s1"], s[k + "s2"] = cols(i[m + "w1_s"]), cols(i[m + "w2_s"])
        s[k + "h1"], s[k + "h2"] = cols(i[m + "h1_s"]), cols(i[m + "h2_s"])
        s[k + "s3"] = rows(i[m + "w3_s"])
    s["cxw"] = i["L2_attn_conv_x_w"].reshape(4, P).T
    s["czw"] = i["L2_attn_conv_z_w"].reshape(4, P).T
    s["cxb"], s["czb"] = cols(i["L2_attn_conv_x_b"]), cols(i["L2_attn_conv_z_b"])
    s["invdt"], s["Dp"] = cols(i["L2_attn_inv_dt"]), cols(i["L2_attn_D"])
    s["bout"] = rows(i["L2_attn_b_out"])
    s["acol"] = np.zeros((P, 16), f)
    s["qks"] = rows(np.concatenate([i["L2_ffn_q_scale"], i["L2_ffn_k_scale"]], 1).reshape(-1))
    s["lg"], s["lb"] = i["L2_ffn_ln_g"].T, i["L2_ffn_ln_b"].T
    fb = np.zeros((2, 2, 3, P), f)
    for b, (o, w) in enumerate(BLK3):
        fb[:, :, b, :w] = i["L2_ffn_b1"].reshape(2, 2, HID2)[:, :, o:o + w]
    s["fb1"] = fb.reshape(12, P).T
    s["fb2"] = rows(i["L2_ffn_b2"].reshape(-1))
    s["scal"] = twice(i["L3_attn_scaling"].reshape(64, 1))
    qb = i["L3_attn_qkv_b"]
    s["qb"] = twice(qb[:1024].reshape(16, 64).T)
    s["kb"] = twice(qb[1024:1280].reshape(4, 64).T)
    s["vb"] = rows(qb[1280:])
    s["ob"] = rows(i["L3_attn_o_b"])
    a = {}
    a["cb"] = np.concatenate([np.asarray(s[k], f).reshape(P, w) for k, w in SPEC], 1)

    z = {}
    neg = -1e30
    q_, k_ = ar[:, None], np.arange(192)[None] - 64
    z["identb"] = np.eye(P)
    z["maskS"] = np.where((k_ <= q_) & (k_ >= q_ - 64), 0, neg)
    j_, i_ = ar[:, None], ar[None]
    z["maskA"] = np.where((j_ <= i_) & (j_ >= i_ - 64), 0, neg)
    z["maskB"] = np.where(j_ - 128 >= i_[:, :64] - 64, 0, neg)
    for nm, o in (("selB", 0), ("selC", 16)):
        m = np.zeros((P, 16, P))
        for st in range(16):
            for part in range(3):
                m[32 * part + o + st, st, :] = 1
        z[nm] = m.reshape(P, -1)
    m = np.zeros((P, 8, P))
    for h in range(8):
        for part in range(3):
            m[32 * part + h, h, :] = 1
    z["selm"] = m.reshape(P, -1)
    a["cbb"] = (np.concatenate([z[k] for k, w in BSPEC], 1).astype(f).view(np.uint32) >> 16).astype(np.uint16)

    a["x"] = i["L0_attn_query"].reshape(T, P)
    w_x = i["L2_attn_W_xdbl"]
    a["w2"] = np.concatenate([
        i["L0_attn_Wq"], i["L0_attn_Wk"], i["L0_attn_Wv"], i["L0_attn_Wo"], i["L0_ffn_router_w"].T,
        i["L1_attn_Wq"], i["L1_attn_Wk"], i["L1_attn_Wv"], i["L1_attn_Wo"],
        i["L2_attn_W_in"], w_x, pad_rows(i["L2_attn_W_dt"])], 1)
    a["wout"] = tall(i["L2_attn_W_out"])
    a["mw1"] = np.ascontiguousarray(i["L0_ffn_w1"].reshape(8 * 1024, P).T)
    a["mw2"] = np.concatenate([tall(np.ascontiguousarray(w.T)) for w in i["L0_ffn_w2"]], 1)
    for k, m in (("f1w", "L1_ffn_"), ("f3w", "L3_ffn_")):
        a[k] = np.concatenate([i[m + "w1_w"].T, i[m + "w2_w"].T] + [tall(np.ascontiguousarray(i[m + n].T)) for n in ("h1_w", "h2_w", "w3_w")], 1)
    lw = []
    for l in range(2):
        lw += [i["L2_ffn_wqkv"][l], tall(i["L2_ffn_wo"][l]), i["L2_ffn_w1"][l], tall(pad_rows(i["L2_ffn_w2"][l], 384))]
    a["l2w"] = np.concatenate(lw, 1)
    half = np.arange(0, 64, 2, dtype=f)
    inv = (f(1.0) / f(10000.0) ** (half / f(64))).astype(f)
    fr = t.astype(f)[:, None] * inv[None]
    base = (half + f(0.4 * 64)) / f(1.4 * 64)
    pw = (t - T // 2).astype(f) / f(32)
    sc = base[None] ** pw[:, None]
    co, si = np.cos(fr), np.sin(fr)
    tb = np.stack([8 * co * sc, 8 * si * sc, -8 * si * sc, co / sc, si / sc, -si / sc]).astype(f)
    tb = tb.reshape(6, NT, P, 32).transpose(2, 0, 1, 3).reshape(P, 3072)
    a["l3w"] = np.concatenate([i["L3_attn_qkv_w"].T, tall(np.ascontiguousarray(i["L3_attn_o_w"].T)), tb], 1)
    return {k: np.ascontiguousarray(v) for k, v in a.items()}


def kernel(**inputs):
    import concourse.bacc as _bacc
    from concourse.bass_utils import run_bass_kernel_spmd as _run

    arrays = lay_out({k: np.asarray(v) for k, v in inputs.items()})
    nc = _bacc.Bacc("TRN2", target_bir_lowering=False, num_devices=1)
    aps = {k: nc.dram_tensor(f"in_{k}", v.shape, mybir.dt.from_np(v.dtype), kind="ExternalInput").ap() for k, v in arrays.items()}
    out = nc.dram_tensor("out_0", (T, P), F32, kind="ExternalOutput").ap()
    program(nc, aps, out)
    r = _run(nc, [{f"in_{k}": v for k, v in arrays.items()}], core_ids=[0])
    return r.results[0]["out_0"].reshape(1, T, P)
```

```python
from contextlib import ExitStack

import numpy as np

import concourse.bass as bass
from concourse import mybir

F32 = mybir.dt.float32
BF16 = mybir.dt.bfloat16
F16 = mybir.dt.float16
I32 = mybir.dt.int32
U32 = mybir.dt.uint32
ALU = mybir.AluOpType
ACT = mybir.ActivationFunctionType
AX = mybir.AxisListType

T, P, NT, NB = 2048, 128, 16, 4
HID2 = 341
BLK3 = [(0, 128), (128, 128), (256, 85)]

SPEC = [
    ("ident", 128), ("bmask", 128), ("hmask", 16), ("sin", 16), ("cos", 16), ("ones", 128),
    ("b0", 384), ("bo0", 128), ("rb", 8), ("iota8", 8), ("mb1", 64), ("mb2", 128),
    ("l1bq", 1), ("l1bk", 1), ("l1bkv", 256), ("l1bo", 128), ("decay", 1), ("expn", 128), ("tri", 128),
    ("trow", 128), ("scol", 1),
    ("f1s1", 4), ("f1s2", 4), ("f1h1", 4), ("f1h2", 4), ("f1s3", 128),
    ("cxw", 4), ("czw", 4), ("cxb", 1), ("czb", 1), ("invdt", 1), ("Dp", 1), ("bout", 128), ("acol", 16),
    ("qks", 256), ("lg", 2), ("lb", 2), ("fb1", 12), ("fb2", 256),
    ("scal", 1), ("qb", 16), ("kb", 4), ("vb", 256), ("ob", 128),
    ("f3s1", 4), ("f3s2", 4), ("f3h1", 4), ("f3h2", 4), ("f3s3", 128),
]
OFF, NC = {}, 0
for _n, _w in SPEC:
    OFF[_n] = (NC, _w)
    NC += _w
BSPEC = [("identb", 128), ("maskS", 192), ("selB", 2048), ("selC", 2048)]
BOFF, NBC = {}, 0
for _n, _w in BSPEC:
    BOFF[_n] = (NBC, _w)
    NBC += _w


class Eng:

    def __init__(self, sem):
        self.sem, self.n, self.ops, self.seen = sem, 0, [], {}

    def wait(self, *after):
        for t in after:
            if t is None:
                continue
            if isinstance(t, list):
                self.wait(*t)
                continue
            sem, v = t
            if self.seen.get(id(sem), 0) < v:
                self.seen[id(sem)] = v
                self.ops.append(lambda e, s=sem, n=v: e.wait_ge(s, n))

    def run(self, fn, *after):
        self.wait(*after)
        self.ops.append(fn)

    def do(self, fn, *after):
        self.wait(*after)
        self.n += 1
        self.ops.append(lambda e: fn(e).then_inc(self.sem, 1))
        return (self.sem, self.n)

    @property
    def last(self):
        return (self.sem, self.n)


class Ring:

    def __init__(self, bufs):
        self.bufs, self.free, self.i = bufs, [[] for _ in bufs], 0

    def take(self):
        k = self.i % len(self.bufs)
        self.i += 1
        return k, self.bufs[k], self.free[k]

    def release(self, k, *tokens):
        self.free[k] = list(tokens)


def program(nc, A, out, upto=8):
    ctx = ExitStack()
    with ctx:
        def sb(name, shape, dt=F32):
            return ctx.enter_context(nc.sbuf_tensor(name, shape, dt))

        X = sb("X", [P, NT, P])
        XT = sb("XT", [P, T + 1])
        CB = sb("CB", [P, NC])
        CBB = sb("CBB", [P, NBC], BF16)
        W0 = sb("W0", [P, 12288])
        W1 = sb("W1", [P, 5632])
        W2 = sb("W2", [P, 1512])
        NWK = 20860
        WK = sb("WK", [P, NWK])
        WO2 = sb("WO2", [P, 256])
        XB = sb("XB", [P, 4, P])
        Y = sb("Y", [P, 2, 4, P])
        ST = sb("ST", [P, 2, 4, 6])
        MV = sb("MV", [P, 2, 4, 2])
        NR = sb("NR", [P, 3, 256])
        PS = ctx.enter_context(nc.psum_tensor("PS", [P, 8, 512], F32))
        eye = CB[:, OFF["ident"][0]:OFF["ident"][0] + 128]

        def c(name, a=0, b=None, p0=0, p1=P):
            o, w = OFF[name]
            return CB[p0:p1, o + a:o + (w if b is None else b)]

        def cb(name, a=0, b=None, p0=0, p1=P):
            o, w = BOFF[name]
            return CBB[p0:p1, o + a:o + (w if b is None else b)]

        def wk(off, n):
            assert off + n <= NWK, (off, n)
            return WK[:, off:off + n]

        def sem(name):
            return ctx.enter_context(nc.semaphore(name))

        pe, act, dve, pool, sp = (Eng(sem(f"s_{n}")) for n in ("pe", "act", "dve", "pool", "sp"))
        engines = [pe, act, dve, pool, sp]

        def mm(o, l, r, start, stop, *after, sig=False, skip=False):
            f = lambda e: e.matmul(o, l, r, start=start, stop=stop, skip_group_check=skip)
            return pe.do(f, *after) if sig else pe.run(f, *after)

        def tr(o, i, *after, sig=False):
            f = lambda e: e.transpose(o, i, eye)
            return pe.do(f, *after) if sig else pe.run(f, *after)

        def av(o, i, func, *after, bias=0.0, scale=1.0):
            return act.do(lambda e: e.activation(o, i, func, bias=bias, scale=scale), *after)

        def tt(eng, o, a, b, op, *after):
            return eng.do(lambda e: e.tensor_tensor(o, a, b, op), *after)

        def ts(eng, o, a, s1, s2, op0, op1, *after):
            if op1 is None:
                return eng.do(lambda e: e.tensor_scalar(o, a, s1, None, op0), *after)
            return eng.do(lambda e: e.tensor_scalar(o, a, s1, s2, op0, op1), *after)

        def stt(o, a, s, b, op0, op1, *after):
            return dve.do(lambda e: e.scalar_tensor_tensor(out=o, in0=a, scalar=s, in1=b, op0=op0, op1=op1), *after)

        def cp(eng, o, i, *after):
            return eng.do(lambda e: e.tensor_copy(o, i), *after)

        def red(o, i, op, *after, negate=None):
            return dve.do(lambda e: e.tensor_reduce(o, i, AX.X, op, negate=negate), *after)

        def ms(eng, o, v, *after):
            return eng.do(lambda e: e.memset(o, v), *after)

        def rcp(o, i, *after):
            return dve.do(lambda e: e.reciprocal(o, i), *after)

        def load(dst, src, *after):
            s = sem(f"s_ld{load.n}")
            load.n += 1
            sp.run(lambda e: e.dma_start(dst, src).then_inc(s, 16), *after)
            return (s, 16)
        load.n = 0

        def barrier():
            ends = [e.last for e in (pe, act, dve, pool) if e.n]
            for e in (pe, act, dve, pool):
                e.wait(ends)
            return ends

        def rsqrt(o, v, n, slot, *after):
            a, b = NR[:, 0, slot:slot + n], NR[:, 1, slot:slot + n]
            t = dve.do(lambda e: e.tensor_single_scalar(a.bitcast(I32), v.bitcast(I32), 1, ALU.logical_shift_right), *after)
            t = ts(dve, o.bitcast(I32), a.bitcast(I32), -1.0, 1597463007.0, ALU.mult, ALU.add, t)
            for _ in range(3):
                t = tt(dve, a, o, o, ALU.mult, t)
                t = stt(b, a, -0.5, v, ALU.mult, ALU.mult, t)
                t = stt(o, b, 1.5, o, ALU.add, ALU.mult, t)
            return t

        def bank(b, n=512, p0=0, p1=P):
            return PS[p0:p1, b, 0:n]

        x_keep = nc.dram_tensor("x_keep", (P, T), F32, kind="Internal").ap()

        c1 = OFF["rb"][0]
        d_cb = load(CB[:, 0:c1], A["cb"][:, 0:c1])
        d_x = load(X[:, :, :], A["x"].rearrange("(t p) f -> p t f", p=P))
        d_w2 = load(W2[:, :], A["w2"])
        sp.wait(d_cb, d_x, d_w2)
        d_cb2 = load(CB[:, c1:], A["cb"][:, c1:])
        d_cbb = load(CBB[:, :].bitcast(mybir.dt.uint16), A["cbb"])
        d_moe = []
        for e_ in range(8):
            a_ = load(W0[:, e_ * 1024:(e_ + 1) * 1024], A["mw1"][:, e_ * 1024:(e_ + 1) * 1024])
            b_ = load(W0[:, 8192 + e_ * 512:8192 + (e_ + 1) * 512], A["mw2"][:, e_ * 512:(e_ + 1) * 512])
            d_moe.append([a_, b_])
        d_wo2 = load(WO2[:, :], A["wout"])
        d_f1 = load(W1[:, :], A["f1w"])

        state = {"x": d_x, "free": []}

        def transpose_x(banks, shifted=False):
            ring = Ring(banks)
            done = []
            for b in range(NB):
                k, bk, free = ring.take()
                for j in range(4):
                    t = tr(PS[:, bk, j * 128:(j + 1) * 128], X[:, 4 * b + j, :], d_cb, state["x"], free, sig=(j == 3))
                if not shifted:
                    if b % 2:
                        u = av(XT[:, b * 512:(b + 1) * 512], bank(bk), ACT.Copy, t)
                    else:
                        u = cp(dve, XT[:, b * 512:(b + 1) * 512], bank(bk), t)
                    done.append(u)
                    ring.release(k, u)
                else:
                    u = cp(dve, XT[0:64, b * 512:(b + 1) * 512], bank(bk, p1=64), t)
                    v = av(XT[64:128, b * 512 + 1:(b + 1) * 512 + 1], bank(bk, p0=64), ACT.Copy, t)
                    done.append([u, v])
                    ring.release(k, u, v)
            return done

        def ln_stats(slot, y, tok):
            for j in range(4):
                s = dve.do(lambda e, j=j: e.bn_stats(ST[:, slot, j, :], y[:, j, :]), tok)
            for j in range(4):
                a = dve.do(lambda e, j=j: e.bn_aggr(MV[:, slot, j, :], ST[:, slot, j, :]), s)
            return a

        def ln_scale(slot, n, tok):
            var = NR[:, 2, slot * 4:slot * 4 + 4 * n]
            rs = NR[:, 2, 16 + slot * 4:16 + slot * 4 + 4 * n]
            s = ts(dve, var.rearrange("p (s j) -> p s j", j=4), MV[:, slot:slot + n, :, 1], 1e-5, None, ALU.add, None, tok)
            return rs, rsqrt(rs, var, 4 * n, slot * 4, s)

        def ln_pre(b, src, src_tok, slot, bias=None):
            y = Y[:, slot, :, :]
            xs = X[:, 4 * b:4 * b + 4, :]
            t0 = tt(dve, y, src, xs, ALU.add, src_tok, state["x"], state.get(("y", slot)))
            t = t0
            if bias is not None:
                t = tt(dve, y, y, bias.unsqueeze(1).broadcast_to([P, 4, P]), ALU.add, t)
            return t0, ln_stats(slot, y, t)

        def ln_post(b0, n, slot, tok):
            rs, s = ln_scale(slot, n, tok)
            for i in range(n):
                for j in range(4):
                    u = ts(dve, X[:, 4 * (b0 + i) + j, :], Y[:, slot + i, j, :], MV[:, slot + i, j, 0:1], rs[:, 4 * i + j:4 * i + j + 1], ALU.subtract, ALU.mult, s)
                state[("y", slot + i)] = u
            return u

        def ln_block(b, src, src_tok, slot, bias=None, pair=True):
            t0, a = ln_pre(b, src, src_tok, slot, bias)
            if not pair:
                return t0, ln_post(b, 1, slot, a)
            return t0, ln_post(b - 1, 2, slot - 1, a) if slot else None

        def l0_attn():
            wqkv, wo = W2[:, 0:384], W2[:, 384:512]
            Q, K, V = wk(0, 2048).rearrange("p (t f) -> p t f", t=NT), wk(2048, 2048).rearrange("p (t f) -> p t f", t=NT), wk(4096, NT * 129).rearrange("p (t f) -> p t f", t=NT)
            o = 4096 + NT * 129
            TMP = [wk(o + i * 512, 512) for i in range(2)]
            o += 1024
            K4 = [wk(o + i * 512, 512).rearrange("p (s f) -> p s f", s=4) for i in range(2)]
            o += 1024
            R = wk(o, 576).rearrange("p (s f) -> p s f", s=4)
            o += 576
            QT, CQT = wk(o, 2048), wk(o + 2048, 2048)
            o += 4096
            NUM = [wk(o + i * 288, 288) for i in range(2)]
            o += 576
            AO = wk(o, 2048).rearrange("p (t f) -> p t f", t=NT)
            o += 2048
            SM = [wk(o + i * 64, 64) for i in range(2)]
            o += 128
            AT = QT
            xt = transpose_x([0, 1])
            one = ms(pool, V[:, :, 128], 1.0)
            ring = Ring([2, 3])
            tmp, k4r = Ring(TMP), Ring(K4)
            kvd = None
            qd = []
            mid = {}

            def first(t):
                k, bk, free = ring.take()
                m = mm(bank(bk, 384), XT[:, t * 128:(t + 1) * 128], wqkv, True, True, d_w2, xt[t // 4], free, sig=True)
                kt, tb, tfree = tmp.take()
                qk = tb[:, 0:256]
                a = tt(dve, qk, PS[:, bk, 0:256], c("b0", 0, 256), ALU.add, m, tfree)
                v = tt(dve, V[:, t, 0:128], PS[:, bk, 256:384], c("b0", 256, 384), ALU.add, m)
                ring.release(k, v, a)
                g = qk.rearrange("p (g d) -> p g d", d=8)
                sm = SM[t % 2]
                a = red(sm[:, 0:32], g, ALU.max, a)
                a = tt(dve, g, g, sm[:, 0:32].unsqueeze(2).broadcast_to([P, 32, 8]), ALU.subtract, a)
                mid[t] = (kt, g, av(qk, qk, ACT.Exp, a), v)

            def second(t):
                kt, g, a, v = mid.pop(t)
                sm = SM[t % 2]
                a = red(sm[:, 32:64], g, ALU.add, a)
                a = rcp(sm[:, 32:64], sm[:, 32:64], a)
                r = sm[:, 32:64].unsqueeze(2).broadcast_to([P, 32, 8])
                k_ = tt(dve, K[:, t, :].rearrange("p (g d) -> p g d", d=8), g[:, 16:32, :], r[:, 16:32, :], ALU.mult, a)
                q_ = tt(dve, Q[:, t, :].rearrange("p (g d) -> p g d", d=8), g[:, 0:16, :], r[:, 0:16, :], ALU.mult, a)
                tmp.release(kt, q_)
                qd.append(q_)
                kk, kb, kfree = k4r.take()
                sn, cs = c("sin", t, t + 1), c("cos", t, t + 1)
                ts(dve, kb[:, 0, :], K[:, t, :], sn, None, ALU.mult, None, k_, kfree)
                ts(dve, kb[:, 1, :], K[:, t, :], cs, None, ALU.mult, None, k_)
                a = ts(dve, K[:, t, :], K[:, t, :], -1.0, 1.0, ALU.mult, ALU.add, dve.last)
                ts(dve, kb[:, 2, :], K[:, t, :], sn, None, ALU.mult, None, a)
                a = ts(dve, kb[:, 3, :], K[:, t, :], cs, None, ALU.mult, None, a)
                for s in range(4):
                    m = mm(bank(4 + s, 129), kb[:, s, :], V[:, t, 0:129], t == 0, t == NT - 1, a, v, one, sig=(s == 3))
                k4r.release(kk, m)
                return m
            for t in range(NT + 1):
                if t < NT:
                    first(t)
                if t:
                    m = second(t - 1)
            kvd = m
            rd = []
            for s in range(4):
                tt(dve, R[:, s, 0:128], PS[:, 4 + s, 0:128], c("bmask"), ALU.mult, kvd)
                rd.append(ts(dve, R[:, s, 128:144], c("hmask"), PS[:, 4 + s, 128:129], None, ALU.mult, None, kvd))
            ring = Ring([0, 1])
            qt = []
            for b in range(NB):
                k, bk, free = ring.take()
                for j in range(4):
                    m = tr(PS[:, bk, j * 128:(j + 1) * 128], Q[:, 4 * b + j, :], qd[4 * b + j], free, xt if b < 2 else None, sig=(j == 3))
                s_ = slice(b * 512, (b + 1) * 512)
                u = av(QT[:, s_], bank(bk), ACT.Copy, m)
                w = ts(dve, CQT[:, s_], QT[:, s_], -1.0, 1.0, ALU.mult, ALU.add, u)
                ring.release(k, u)
                qt.append([u, w])
            ring = Ring([2, 3, 4, 5])
            nr = Ring(NUM)
            aod = []
            for t in range(NT):
                s_ = slice(t * 128, (t + 1) * 128)
                toks = []
                for br, src in enumerate((QT, CQT)):
                    k, bk, free = ring.take()
                    m = mm(bank(bk, 288), src[:, s_], R[:, 2 * br:2 * br + 2, :], True, True, rd, qt[t // 4], free, sig=True)
                    toks.append((k, bk, m))
                kn, nb, nfree = nr.take()
                N = [nb[:, 0:144], nb[:, 144:288]]
                pieces = [ts(dve, N[i], PS[:, bk, 0:144], c("sin", t, t + 1), None, ALU.mult, None, m, nfree) for i, (k, bk, m) in enumerate(toks)]
                for i, (k, bk, m) in enumerate(toks):
                    pieces[i] = stt(N[i], PS[:, bk, 144:288], c("cos", t, t + 1), N[i], ALU.mult, ALU.add, pieces[i])
                    ring.release(k, pieces[i])
                n2 = nb.rearrange("p (b f) -> p b f", b=2)
                den = n2[:, :, 128:144]
                a = ts(dve, den, den, 1e-6, None, ALU.max, None, pieces)
                a = rcp(den, den, a)
                nv = n2[:, :, 0:128].rearrange("p b (h d) -> p b h d", d=8)
                pieces = tt(dve, nv, nv, den.unsqueeze(3).broadcast_to([P, 2, 16, 8]), ALU.mult, a)
                a = tt(dve, AO[:, t, :], nb[:, 0:128], nb[:, 144:272], ALU.add, pieces)
                nr.release(kn, a)
                aod.append(a)
            ring = Ring([0, 1])
            last_q = pe.last
            ev = []
            for b in range(NB):
                k, bk, free = ring.take()
                for j in range(4):
                    m = tr(PS[:, bk, j * 128:(j + 1) * 128], AO[:, 4 * b + j, :], aod[4 * b + j], qt, free, sig=(j == 3))
                u = av(AT[:, b * 512:(b + 1) * 512], bank(bk), ACT.Copy, m, last_q)
                ring.release(k, u)
                ev.append(u)
            ring = Ring([6, 7])
            res = []
            for b in range(NB):
                k, bk, free = ring.take()
                for j in range(4):
                    t = 4 * b + j
                    m = mm(PS[:, bk, j * 128:(j + 1) * 128], AT[:, t * 128:(t + 1) * 128], wo, True, True, ev[b], rd, free, sig=(j == 3))
                t0, u = ln_block(b, PS[:, bk, :].rearrange("p (t f) -> p t f", t=4), m, b % 2, c("bo0"))
                ring.release(k, t0)
                res.append(u)
            state["x"] = res[-1]

        def l0_ffn():
            G = wk(0, 128).rearrange("p (t e) -> p t e", t=NT)
            GT = wk(128, 2048)
            ACC = wk(2176, 2048).rearrange("p (t f) -> p t f", t=NT)
            H = [wk(4224 + i * 2048, 2048).rearrange("p (k n) -> p k n", k=4) for i in range(2)]
            S1 = [wk(8320 + i * 512, 512) for i in range(3)]
            L = wk(9856, 128).rearrange("p (t e) -> p t e", t=NT)
            M8 = wk(9984, 128).rearrange("p (t e) -> p t e", t=NT)
            IX = wk(10112, 128).rearrange("p (t e) -> p t e", t=NT)
            IF = wk(10240, 128).rearrange("p (t e) -> p t e", t=NT)
            GW = wk(10368, 64).rearrange("p (s t) -> p s t", s=4)
            O1 = wk(10432, 128).rearrange("p (t e) -> p t e", t=NT)
            router = W2[:, 512:520]
            xt = transpose_x([0, 1])
            for t in range(NT):
                m = mm(PS[:, 2, t * 8:t * 8 + 8], XT[:, t * 128:(t + 1) * 128], router, True, True, d_w2, xt[t // 4], sig=(t == NT - 1))
            a = tt(dve, L[:, :, :], PS[:, 2, 0:128].rearrange("p (t e) -> p t e", t=NT),
                   c("rb").unsqueeze(1).broadcast_to([P, NT, 8]), ALU.add, m)
            for t in range(NT):
                b = dve.do(lambda e, t=t: e.max(M8[:, t, :], L[:, t, :]), a)
            for t in range(NT):
                b2 = dve.do(lambda e, t=t: e.max_index(IX[:, t, :].bitcast(U32), M8[:, t, :], L[:, t, :]), b)
            a = cp(dve, IF[:, :, :], IX[:, :, :].bitcast(U32), b2)
            g = tt(dve, GW[:, 0, :], M8[:, :, 1], M8[:, :, 0], ALU.subtract, b)
            g = av(GW[:, 1, :], GW[:, 0, :], ACT.Exp, g)
            g = ts(dve, GW[:, 2, :], GW[:, 1, :], 1.0, None, ALU.add, None, g)
            g = rcp(GW[:, 2, :], GW[:, 2, :], g)
            g = tt(dve, GW[:, 3, :], GW[:, 1, :], GW[:, 2, :], ALU.mult, g)
            for t in range(NT):
                ts(dve, G[:, t, :], c("iota8"), IF[:, t, 0:1], GW[:, 2, t:t + 1], ALU.is_equal, ALU.mult, a, g)
                o1 = ts(dve, O1[:, t, :], c("iota8"), IF[:, t, 1:2], GW[:, 3, t:t + 1], ALU.is_equal, ALU.mult, a, g)
            g = tt(dve, G[:, :, :], G[:, :, :], O1[:, :, :], ALU.add, o1)
            ring = Ring([2, 3])
            gt = []
            for b_ in range(NB):
                k, bk, free = ring.take()
                for j in range(4):
                    m = tr(PS[0:8, bk, j * 128:(j + 1) * 128], G[:, 4 * b_ + j, :], g, a, free, sig=(j == 3))
                u = av(GT[0:8, b_ * 512:(b_ + 1) * 512], bank(bk, p1=8), ACT.Copy, m)
                ring.release(k, u)
                gt.append(u)
            accd = [None] * NT
            for b_ in range(NB):
                k, bk, free = ring.take()
                for j in range(4):
                    t = 4 * b_ + j
                    m = mm(PS[:, bk, j * 128:(j + 1) * 128], GT[0:8, t * 128:(t + 1) * 128], c("mb2", p1=8), True, True, gt[b_], free, sig=(j == 3))
                u = cp(dve, ACC[:, 4 * b_:4 * b_ + 4, :], PS[:, bk, :].rearrange("p (t f) -> p t f", t=4), m)
                ring.release(k, u)
                accd[b_] = u
            ring = Ring([0, 1, 2, 3, 4, 5])
            for i, u in enumerate((xt[2], xt[3], ring.free[2], ring.free[3])):
                ring.release(i, u)
            ring.free[2] = [accd[2]]
            ring.free[3] = [accd[3]]
            oring = Ring([6, 7])
            hr, s1r = Ring(H), Ring(S1)
            pend = []

            def second(e, b_, kh, hb, hd):
                k, bk, free = oring.take()
                w2e = W0[:, 8192 + e * 512:8192 + (e + 1) * 512].rearrange("p (k f) -> p k f", k=4)
                for j in range(4):
                    for kb in range(4):
                        m = mm(PS[:, bk, j * 128:(j + 1) * 128], hb[:, kb, j * 128:(j + 1) * 128], w2e[:, kb, :], kb == 0, kb == 3,
                               hd, d_moe[e], free, sig=(kb == 3 and j == 3))
                hr.release(kh, m)
                for j in range(4):
                    t = 4 * b_ + j
                    u = stt(ACC[:, t, :], PS[:, bk, j * 128:(j + 1) * 128], G[:, t, e:e + 1], ACC[:, t, :], ALU.mult, ALU.add, m, accd[b_])
                accd[b_] = u
                oring.release(k, u)

            for e in range(8):
                for b_ in range(NB):
                    kh, hb, hfree = hr.take()
                    hd = []
                    for kb in range(4):
                        k1, b1, f1 = ring.take()
                        m1 = mm(bank(b1), W0[:, e * 1024 + kb * 128:e * 1024 + (kb + 1) * 128], XT[:, b_ * 512:(b_ + 1) * 512], True, True,
                                d_moe[e], xt, f1, sig=True)
                        k2, b2, f2 = ring.take()
                        m2 = mm(bank(b2), W0[:, e * 1024 + 512 + kb * 128:e * 1024 + 512 + (kb + 1) * 128], XT[:, b_ * 512:(b_ + 1) * 512], True, True,
                                f2, sig=True)
                        ks, s1, sf = s1r.take()
                        a = av(s1, bank(b1), ACT.Silu, m1, sf, bias=c("mb1", e * 8 + kb, e * 8 + kb + 1))
                        ring.release(k1, a)
                        h = stt(hb[:, kb, :], bank(b2), c("mb1", e * 8 + 4 + kb, e * 8 + 5 + kb), s1, ALU.add, ALU.mult, m2, a, hfree)
                        ring.release(k2, h)
                        s1r.release(ks, h)
                        hd.append(h)
                        if kb == 1 and pend:
                            second(*pend.pop())
                    pend.append((e, b_, kh, hb, hd))
            second(*pend.pop())
            for b_ in range(NB):
                t0, u = ln_block(b_, ACC[:, 4 * b_:4 * b_ + 4, :], accd[b_], b_ % 2)
            state["x"] = u

        def l1_attn():
            w = W2[:, 520:1032]
            QT, KT = wk(0, 2048), wk(2048, 2048)
            K, V = wk(4096, 2048).rearrange("p (t f) -> p t f", t=NT), wk(6144, 2048).rearrange("p (t f) -> p t f", t=NT)
            DT, QD = wk(8192, 128), wk(8320, 2048)
            DROW, SC = wk(10368, 128), wk(10496, 16)
            M = wk(10512, 128)
            PT = [wk(10640 + i * 128, 128) for i in range(2)]
            OT = wk(10896, 2048)
            TM = [wk(12944 + i * 512, 512) for i in range(4)]
            xt = transpose_x([0, 1])
            p_ = c("decay")
            a = ts(dve, SC[:, 0:1], p_, -1.0, None, ALU.mult, None, d_cb)
            a = tt(dve, SC[:, 1:2], SC[:, 0:1], p_, ALU.min, a)
            a = av(SC[:, 2:3], SC[:, 1:2], ACT.Exp, a)
            a = ts(dve, SC[:, 2:3], SC[:, 2:3], 1.0, None, ALU.add, None, a)
            a = av(SC[:, 3:4], SC[:, 2:3], ACT.Ln, a)
            a = ts(dve, SC[:, 4:5], SC[:, 0:1], 0.0, SC[:, 3:4], ALU.max, ALU.add, a)
            a = ts(dve, SC[:, 5:6], SC[:, 4:5], -1.0, None, ALU.mult, None, a)
            la = SC[:, 5:6]
            d1 = av(DT, c("expn"), ACT.Exp, a, scale=la)
            d2 = av(DROW, c("trow"), ACT.Exp, a, scale=la)
            d3 = av(SC[:, 6:7], c("scol"), ACT.Exp, a, scale=la)
            d4 = av(SC[:, 8:9], c("trow", 0, 1), ACT.Exp, a, scale=la)
            d5 = ts(dve, SC[:, 9:10], la, 128.0, None, ALU.mult, None, a)
            d4 = av(SC[:, 7:8], SC[:, 9:10], ACT.Exp, d5)
            d1 = tt(dve, DT, DT, c("tri"), ALU.mult, d1)
            ring = Ring([2, 3, 4, 5])
            tr_ = Ring(TM)
            qd, kd, kvd = [], [], []
            for b in range(NB):
                s_ = slice(b * 512, (b + 1) * 512)
                k, bk, free = ring.take()
                m = mm(bank(bk), w[:, 0:128], XT[:, s_], True, True, d_w2, xt[b], free, sig=True)
                a = ts(dve, QT[:, s_], bank(bk), c("l1bq"), None, ALU.add, None, m)
                ring.release(k, a)
                a = tt(dve, QD[:, s_].rearrange("p (c n) -> p c n", n=128), QT[:, s_].rearrange("p (c n) -> p c n", n=128),
                       DROW.unsqueeze(1).broadcast_to([P, 4, 128]), ALU.mult, a, d2)
                qd.append(a)
                k, bk, free = ring.take()
                m = mm(bank(bk), w[:, 128:256], XT[:, s_], True, True, free, sig=True)
                kt, tb, tf = tr_.take()
                a = ts(dve, tb, bank(bk), c("l1bk"), 0.0, ALU.add, ALU.min, m, tf)
                a2 = ts(dve, KT[:, s_], bank(bk), c("l1bk"), 0.0, ALU.add, ALU.max, m)
                ring.release(k, a2)
                a = av(tb, tb, ACT.Exp, a)
                a = tt(dve, KT[:, s_], KT[:, s_], tb, ALU.add, a, a2)
                tr_.release(kt, a)
                kd.append(a)
            for t in range(NT):
                k, bk, free = ring.take()
                m = mm(bank(bk, 256), XT[:, t * 128:(t + 1) * 128], w[:, 128:384], True, True, free, sig=True)
                kt, tb, tf = tr_.take()
                a = tt(dve, tb[:, 0:128], PS[:, bk, 0:128], c("l1bkv", 0, 128), ALU.add, m, tf)
                v = tt(dve, V[:, t, :], PS[:, bk, 128:256], c("l1bkv", 128, 256), ALU.add, m)
                ring.release(k, v)
                x1 = ts(dve, tb[:, 128:256], tb[:, 0:128], 0.0, None, ALU.min, None, a)
                x1 = av(tb[:, 128:256], tb[:, 128:256], ACT.Exp, x1)
                x1 = stt(tb[:, 0:128], tb[:, 0:128], 0.0, tb[:, 128:256], ALU.max, ALU.add, x1)
                x1 = ts(dve, K[:, t, :], tb[:, 0:128], SC[:, 6:7], None, ALU.mult, None, x1, d3)
                tr_.release(kt, x1)
                kvd.append([x1, v])
            ring, ring2 = Ring([0, 1]), Ring([2, 3])
            ring3 = Ring([4, 5])
            ptr = Ring(PT)
            md = ms(dve, M, 0.0)
            od = []
            for t in range(NT):
                s_ = slice(t * 128, (t + 1) * 128)
                k, bk, free = ring.take()
                m = mm(bank(bk, 128), KT[:, s_], QT[:, s_], True, True, qd, kd, kvd, free, sig=True)
                kp, pb_, pf = ptr.take()
                a = tt(dve, pb_, bank(bk, 128), DT, ALU.mult, m, d1, pf)
                ring.release(k, a)
                k, bk, free = ring2.take()
                mm(bank(bk, 128), M, QD[:, s_], True, False, md, free)
                m = mm(bank(bk, 128), V[:, t, :], pb_, False, True, a, sig=True)
                ptr.release(kp, m)
                o_ = av(OT[:, s_], bank(bk, 128), ACT.Copy, m)
                ring2.release(k, o_)
                od.append(o_)
                k, bk, free = ring3.take()
                m2 = mm(bank(bk, 128), K[:, t, :], V[:, t, :], True, True, free, sig=True)
                md = stt(M, M, SC[:, 7:8], bank(bk, 128), ALU.mult, ALU.add, m2, m, d4, md)
                ring3.release(k, md)
            ring = Ring([6, 7])
            for b in range(NB):
                k, bk, free = ring.take()
                for j in range(4):
                    t = 4 * b + j
                    m = mm(PS[:, bk, j * 128:(j + 1) * 128], OT[:, t * 128:(t + 1) * 128], w[:, 384:512], True, True, od[t], free, sig=(j == 3))
                t0, u = ln_block(b, PS[:, bk, :].rearrange("p (t f) -> p t f", t=4), m, b % 2, c("l1bo"))
                ring.release(k, t0)
            state["x"] = u

        def tern(W, loaded, f):
            H1 = wk(0, 8192).rearrange("p (k n) -> p k n", k=4)
            H2 = wk(8192, 8192).rearrange("p (k n) -> p k n", k=4)
            S1 = [wk(16384 + i * 512, 512) for i in range(3)]
            w1, w2 = W[:, 0:512], W[:, 512:1024]
            h1 = W[:, 1024:3072].rearrange("p (k n) -> p k n", k=4)
            h2 = W[:, 3072:5120].rearrange("p (k n) -> p k n", k=4)
            w3 = W[:, 5120:5632].rearrange("p (k n) -> p k n", k=4)
            xt = transpose_x([0, 1])
            ring, s1r = Ring([2, 3, 4, 5, 6, 7]), Ring(S1)
            hd = [[] for _ in range(NB)]
            for b in range(NB):
                s_ = slice(b * 512, (b + 1) * 512)
                for ob in range(4):
                    o_ = slice(ob * 128, (ob + 1) * 128)
                    k1, b1, f1 = ring.take()
                    m1 = mm(bank(b1), w1[:, o_], XT[:, s_], True, True, loaded, xt[b], f1, sig=True)
                    k2, b2, f2 = ring.take()
                    m2 = mm(bank(b2), w2[:, o_], XT[:, s_], True, True, f2, sig=True)
                    ks, s1, sf = s1r.take()
                    a = av(s1, bank(b1), ACT.Silu, m1, sf, scale=c(f + "s1", ob, ob + 1))
                    ring.release(k1, a)
                    h = stt(H1[:, ob, s_], bank(b2), c(f + "s2", ob, ob + 1), s1, ALU.mult, ALU.mult, m2, a)
                    ring.release(k2, h)
                    s1r.release(ks, h)
                    hd[b].append(h)
            src, dst = H1, H2
            for wl, sc in ((h1, f + "h1"), (h2, f + "h2")):
                nd = [[] for _ in range(NB)]
                for b in range(NB):
                    s_ = slice(b * 512, (b + 1) * 512)
                    for ob in range(4):
                        k, bk, free = ring.take()
                        for kb in range(4):
                            m = mm(bank(bk), wl[:, kb, ob * 128:(ob + 1) * 128], src[:, kb, s_], kb == 0, kb == 3, hd[b], free, sig=(kb == 3))
                        a = av(dst[:, ob, s_], bank(bk), ACT.Gelu, m, hd[b], scale=c(sc, ob, ob + 1))
                        ring.release(k, a)
                        nd[b].append(a)
                hd = nd
                src, dst = dst, src
            for b in range(NB):
                k, bk, free = ring.take()
                for j in range(4):
                    t = 4 * b + j
                    for kb in range(4):
                        m = mm(PS[:, bk, j * 128:(j + 1) * 128], src[:, kb, t * 128:(t + 1) * 128], w3[:, kb, :], kb == 0, kb == 3, hd[b], free, sig=(kb == 3 and j == 3))
                p3 = PS[:, bk, :].rearrange("p (t f) -> p t f", t=4)
                a = tt(dve, XB[:, :, :], p3, c(f + "s3").unsqueeze(1).broadcast_to([P, 4, P]), ALU.mult, m, state.get("xb"))
                ring.release(k, a)
                t0, u = ln_block(b, XB[:, :, :], a, b % 2)
                state["xb"] = t0
            state["x"] = u

        def mamba():
            w_in, w_x, w_dt = W2[:, 1032:1288], W2[:, 1288:1384], W2[0:64, 1384:1512]
            PX, PZ = wk(0, 2051), wk(2051, 2051)
            o = 4102
            U, ZS = wk(o, 2048), wk(o + 2048, 2048)
            DE, DU = wk(0, 2048), wk(2048, 2048)
            LOW = wk(o + 4096, 2048)
            YA = LOW
            SPL = wk(o + 6144, 1024).bitcast(BF16)
            o += 7168
            RB = [wk(o + i * 2048, 2048) for i in range(4)]
            xt = transpose_x([0, 1])
            z = [ms(dve, PX[:, 0:1], 0.0), ms(dve, PX[:, 2049:2051], 0.0), ms(dve, PZ[:, 0:1], 0.0), ms(dve, PZ[:, 2049:2051], 0.0)]
            zs = ms(pool, SPL[96:128, :], 0.0)
            ring = Ring([2, 3, 4, 5])
            cd = []
            for h, dst in ((0, PX), (1, PZ)):
                for b in range(NB):
                    k, bk, free = ring.take()
                    m = mm(bank(bk), w_in[:, h * 128:(h + 1) * 128], XT[:, b * 512:(b + 1) * 512], True, True, d_w2, xt[b], free, sig=True)
                    a = av(dst[:, 1 + b * 512:1 + (b + 1) * 512], bank(bk), ACT.Copy, m)
                    ring.release(k, a)
                    cd.append(a)
            for src, wn, bn, dst, tmp in ((PX, "cxw", "cxb", U, RB[0]), (PZ, "czw", "czb", ZS, RB[1])):
                a = ts(dve, tmp, src[:, 0:T], c(wn, 0, 1), None, ALU.mult, None, cd, z)
                for j in range(1, 4):
                    a = stt(tmp, src[:, j:j + T], c(wn, j, j + 1), tmp, ALU.mult, ALU.add, a)
                if src is PX:
                    ud = av(dst, tmp, ACT.Silu, a, bias=c(bn))
                else:
                    zd = av(dst, tmp, ACT.Silu, a, bias=c(bn))
            conv_end = a
            BC = []
            ring = Ring([2, 3, 4, 5])
            for b in range(NB):
                s_ = slice(b * 512, (b + 1) * 512)
                k, bk, free = ring.take()
                m = mm(PS[0:64, bk, :], w_x[:, 0:64], U[:, s_], True, True, ud, zd, free, sig=True)
                l = av(LOW[0:64, s_], PS[0:64, bk, :], ACT.Copy, m)
                ring.release(k, l)
                k, bk, free = ring.take()
                m = mm(PS[0:32, bk, :], w_x[:, 64:96], U[:, s_], True, True, free, sig=True)
                p32 = RB[2][0:32, s_]
                a = cp(dve, SPL[0:32, s_], PS[0:32, bk, :], m)
                r = tt(dve, p32, PS[0:32, bk, :], SPL[0:32, s_], ALU.subtract, a)
                ring.release(k, r)
                a = cp(dve, SPL[32:64, s_], p32, r)
                pm = RB[3][0:32, s_]
                a = cp(dve, pm, SPL[32:64, s_], a)
                a = tt(dve, p32, p32, pm, ALU.subtract, a)
                a = cp(dve, SPL[64:96, s_], p32, a)
                BC.append([a, l])
            dd = []
            E1, E2 = RB[0], RB[1]
            inv2 = NR[:, 2, 100:101]
            iv = ts(dve, inv2, c("invdt"), 2.0, None, ALU.mult, None)
            for b in range(NB):
                s_ = slice(b * 512, (b + 1) * 512)
                k, bk, free = ring.take()
                m = mm(bank(bk), w_dt, LOW[0:64, s_], True, True, BC[b], free, sig=True)
                a = av(E1[:, s_], bank(bk), ACT.Abs, m, iv, bias=inv2)
                r = ts(dve, DE[:, s_], bank(bk), inv2, 0.0, ALU.add, ALU.max, a, conv_end)
                ring.release(k, a, r)
                dd.append([a, r])
            a = av(E1, E1, ACT.Exp, dd, scale=-1.0)
            a = ts(dve, E1, E1, 1.0, None, ALU.add, None, a)
            a = av(E2, E1, ACT.Ln, a)
            a = tt(dve, DE, DE, E2, ALU.add, a)
            dl = tt(dve, DU, DE, U, ALU.mult, a)
            ya = ts(pool, YA, U, c("Dp"), None, ALU.mult, None, BC, dd, ud, zs)
            ra, rh = Ring(RB[0:2]), Ring(RB[2:4])
            for r_ in (ra, rh):
                for i in range(len(r_.bufs)):
                    r_.release(i, dl)
            rB, rC = Ring([0, 1, 2, 3]), Ring([4, 5, 6, 7])
            for i in range(4):
                rB.release(i, dd)
                rC.release(i, dd)
            for n in range(16):
                ka, da, fa = ra.take()
                e_ = av(da, DE, ACT.Exp, dl, fa, scale=-float(n + 1))
                kh, hb, fh = rh.take()
                for b in range(NB):
                    s_ = slice(b * 512, (b + 1) * 512)
                    k, bk, free = rB.take()
                    m = mm(bank(bk), cb("selB", n * 128, (n + 1) * 128), SPL[:, s_], True, True, BC, zs, d_cbb, free, sig=True)
                    w_ = tt(dve, hb[:, s_], DU[:, s_], bank(bk), ALU.mult, m, fh)
                    rB.release(k, w_)
                s = dve.do(lambda e, hb=hb, da=da: e.tensor_tensor_scan(hb, da, hb, 0.0, ALU.mult, ALU.add), e_, w_)
                ra.release(ka, s)
                for b in range(NB):
                    s_ = slice(b * 512, (b + 1) * 512)
                    k, bk, free = rC.take()
                    m = mm(bank(bk), cb("selC", n * 128, (n + 1) * 128), SPL[:, s_], True, True, free, sig=True)
                    w_ = tt(dve, hb[:, s_], hb[:, s_], bank(bk), ALU.mult, m, s)
                    rC.release(k, w_)
                ya = tt(pool, YA, YA, hb, ALU.add, w_, ya)
                rh.release(kh, ya)
            ring = Ring([0, 1])
            wo = A_wout
            ring.release(0, rB.free[0])
            ring.release(1, rB.free[1])
            for b in range(NB):
                k, bk, free = ring.take()
                for j in range(4):
                    t = 4 * b + j
                    s_ = slice(t * 128, (t + 1) * 128)
                    mm(PS[:, bk, j * 128:(j + 1) * 128], YA[:, s_], wo[0], True, False, ya, d_wo2, free)
                    m = mm(PS[:, bk, j * 128:(j + 1) * 128], ZS[:, s_], wo[1], False, True, zd, sig=(j == 3))
                t0, u = ln_block(b, PS[:, bk, :].rearrange("p (t f) -> p t f", t=4), m, b % 2, c("bout"))
                ring.release(k, t0)
            state["x"] = u

        def local_layer(l):
            o0 = l * 3114
            wqkv = W0[:, o0:o0 + 1536]
            wo = W0[:, o0 + 1536:o0 + 2048].rearrange("p (k f) -> p k f", k=4)
            w1 = W0[:, o0 + 2048:o0 + 2730]
            w2 = W0[:, o0 + 2730:o0 + 3114].rearrange("p (k f) -> p k f", k=3)
            o = [0]

            def take(n):
                o[0] += n
                return wk(o[0] - n, n)
            CT = take(2048).rearrange("p (t s d) -> p t s d", t=NT, s=2)
            SN = take(2048).rearrange("p (t s d) -> p t s d", t=NT, s=2)
            QK = [take(1024) for _ in range(2)]
            RO = [take(1024) for _ in range(2)]
            PB = take(1024)
            VV = [take(520).rearrange("p (h d) -> p h d", h=8) for _ in range(5)]
            QT = [take(512).rearrange("p (h n) -> p h n", h=4) for _ in range(2)]
            KZ = [take(1024).rearrange("p (h n) -> p h n", h=8) for _ in range(2)]
            PX = take(1536).rearrange("p (h n) -> p h n", h=8)
            PT = [take(1536).rearrange("p (h n) -> p h n", h=8) for _ in range(2)]
            O, OTT = take(512), take(512)
            SS, RS_ = take(32), take(32)
            NM = [take(8) for _ in range(2)]
            DEN = take(8)
            tab = W1[:, 2560:5632].rearrange("p (s c t d) -> p s c t d", s=2, c=3, t=NT)
            td = None
            for s in range(2):
                for hf in range(2):
                    sc = c("qks", l * 128 + s * 64 + hf * 32, l * 128 + s * 64 + hf * 32 + 32).unsqueeze(1).broadcast_to([P, NT, 32])
                    td = tt(pool, CT[:, :, s, hf * 32:hf * 32 + 32], tab[:, s, 0, :, :], sc, ALU.mult, d_l3w, td)
                    oh = 1 - hf
                    td = tt(pool, SN[:, :, s, oh * 32:oh * 32 + 32], tab[:, s, 2 if oh == 0 else 1, :, :], sc, ALU.mult, td)
            zz = [ms(dve, k_[:, :, :], 0.0) for k_ in KZ] + [ms(dve, p_[0:64, :, 128:192], 0.0) for p_ in PT]
            zv = [ms(dve, v_[:, :, 64], 1.0) for v_ in VV]
            if l == 0:
                state["kept"] = load(x_keep, X[:, :, :].rearrange("p t f -> p (t f)"), state["x"])
            z0 = ms(dve, XT[64:128, 0:1], 0.0)
            xt = transpose_x([0, 1], shifted=True)
            ra = Ring([0, 2, 4, 6])
            ra.release(0, xt)
            ra.release(1, xt)
            qkr, ror, qtr, kzr, ptr, vr = Ring(QK), Ring(RO), Ring(QT), Ring(KZ), Ring(PT), Ring(VV)
            tl = [dict() for _ in range(NT)]
            hold = {"O": None, "OTT": None, "PB": None, "PX": None, "SS": None}

            def s0(t):
                d = tl[t]
                s_ = slice(t * 128, (t + 1) * 128)
                xd = [z0, xt[t // 4], xt[max(t * 128 - 1, 0) // 512]]
                k, bk, free = ra.take()
                mm(bank(bk), XT[:, s_], wqkv[:, 0:512], True, True, d_l2, xd, free)
                m = mm(bank(bk + 1), XT[:, s_], wqkv[:, 512:1024], True, True, sig=True)
                kq, qb_, qf = qkr.take()
                a = av(qb_.rearrange("p (b n) -> p b n", b=2), PS[:, bk:bk + 2, :], ACT.Copy, m, qf)
                ra.release(k, a)
                d["qk"] = (kq, qb_, a)

            def s0b(t):
                d = tl[t]
                kq, qb_, a = d["qk"]
                s_ = slice(t * 128, (t + 1) * 128)
                k, bk, free = ra.take()
                m = mm(bank(bk), XT[:, s_], wqkv[:, 1024:1536], True, True, free, sig=True)
                kv, vb, vf = vr.take()
                v = av(vb[:, :, 0:64], PS[:, bk, :].rearrange("p (h d) -> p h d", h=8), ACT.Copy, m, vf, zv)
                ra.release(k, v)
                d["v"] = (kv, vb, v)
                kr, rbuf, rf = ror.take()
                sq = av(rbuf, qb_, ACT.Square, a, rf)
                d["ro"] = (kr, rbuf, sq)

            def s0v(t):
                d = tl[t]
                kq, qb_, a = d["qk"]
                kr, rbuf, sq = d["ro"]
                ss, rs = SS[:, 0:16], RS_[:, 0:16]
                g = red(ss, rbuf.rearrange("p (h d) -> p h d", h=16), ALU.add, sq, hold["SS"])
                g = ts(dve, ss, ss, 1e-24, None, ALU.max, None, g)
                g = rsqrt(rs, ss, 16, 32, g)
                q4 = qb_.rearrange("p (h d) -> p h d", h=16)
                g = tt(dve, q4, q4, rs.unsqueeze(2).broadcast_to([P, 16, 64]), ALU.mult, g, a)
                hold["SS"] = g
                v = tt(dve, rbuf.rearrange("p (s h d) -> p s h d", s=2, h=8), qb_.rearrange("p (s h d) -> p s h d", s=2, h=8),
                       CT[:, t, :, :].unsqueeze(2).broadcast_to([P, 2, 8, 64]), ALU.mult, g, td)
                q5 = qb_.rearrange("p (s h f d) -> p s h f d", s=2, h=8, f=2)
                p5 = PB.rearrange("p (s h f d) -> p s h f d", s=2, h=8, f=2)
                for hf in range(2):
                    w_ = tt(pool, p5[:, :, :, hf, :], q5[:, :, :, 1 - hf, :],
                            SN[:, t, :, hf * 32:hf * 32 + 32].unsqueeze(2).broadcast_to([P, 2, 8, 32]), ALU.mult, g, td, hold["PB"])
                qkr.release(kq, w_, v)
                d["half"] = [w_, v]

            def s0w(t):
                d = tl[t]
                rbuf = d["ro"][1]
                r = tt(dve, rbuf, rbuf, PB, ALU.add, d["half"])
                hold["PB"] = r
                d["rot"] = r

            def s1(t):
                d = tl[t]
                kr, rbuf, _ = d["ro"]
                k, bk, free = ra.take()
                for j in range(8):
                    m = tr(PS[:, bk + j // 4, (j % 4) * 128:(j % 4 + 1) * 128], rbuf[:, j * 128:(j + 1) * 128], d["rot"], free, sig=(j == 7))
                ror.release(kr, m)
                kq, q_, qf = qtr.take()
                kz, z_, zf = kzr.take()
                a = av(q_, PS[:, bk, :].rearrange("p (h n) -> p h n", h=4), ACT.Copy, m, qf)
                pv = PS[:, bk + 1, :].rearrange("p (h n) -> p h n", h=4)
                z4 = z_.rearrange("p (h a) n -> p h a n", a=2)
                b1 = av(z4[0:64, :, 0, :], pv[0:64, :, :], ACT.Copy, m, zf, zz)
                b2 = av(z4[64:128, :, 1, :], pv[64:128, :, :], ACT.Copy, m, zf, zz)
                ra.release(k, a, b2)
                d["q"], d["k"] = (kq, q_, a), (kz, z_, b2)

            def s2(t, hg):
                d = tl[t]
                _, q_, qd = d["q"]
                _, z_, zd = d["k"]
                nm = NM[t % 2]
                lo = 0 if t else 64
                k, bk, free = ra.take()
                for i in range(4):
                    h = hg * 4 + i
                    b_, c0 = bk + i // 2, (i % 2) * 192
                    mm(PS[:, b_, c0 + lo:c0 + 192], cb("identb"), cb("maskS", lo, 192), True, False, d_cbb, free, qd, zd)
                    if t:
                        mm(PS[:, b_, c0:c0 + 64], q_[:, h // 2, :], tl[t - 1]["k"][1][:, h, 64:128], False, False)
                    m = mm(PS[:, b_, c0 + 64:c0 + 192], q_[:, h // 2, :], z_[:, h, :], False, True, sig=(i == 3))
                src = PS[:, bk:bk + 2, 0:384].rearrange("p b (h n) -> p b h n", h=2)[:, :, :, lo:192]
                r = red(nm[:, hg * 4:hg * 4 + 4], src, ALU.max, m, negate=True)
                for i in range(4):
                    h = hg * 4 + i
                    c0 = (i % 2) * 192
                    a = av(PX[:, h, lo:192], PS[:, bk + i // 2, c0 + lo:c0 + 192], ACT.Exp, r, hold["PX"], bias=nm[:, h:h + 1])
                ra.release(k, a)
                d[("p", hg)] = a
                if hg:
                    qtr.release(d["q"][0], m)
                    if t:
                        kzr.release(tl[t - 1]["k"][0], m)

            def s4(t):
                d = tl[t]
                kp, p_, pf = ptr.take()
                for hg in range(2):
                    k, bk, free = ra.take()
                    for i in range(4):
                        h = hg * 4 + i
                        m = tr(PS[:, bk, i * 128:(i + 1) * 128], PX[:, h, 64:192], d[("p", hg)], free, sig=(i == 3))
                    hs = slice(hg * 4, hg * 4 + 4)
                    d[("pt", hg)] = av(p_[:, hs, 0:128], bank(bk).rearrange("p (h n) -> p h n", h=4), ACT.Copy, m, pf)
                    if t:
                        for i in range(4):
                            h = hg * 4 + i
                            o_ = PS[64:128, bk + 1, i * 64:(i + 1) * 64]
                            m = mm(o_, PX[:, h, 0:64], eye[:, 0:64], True, True, sig=(i == 3))
                        d[("pt", hg)] = av(p_[64:128, hs, 128:192], PS[64:128, bk + 1, 0:256].rearrange("p (h n) -> p h n", h=4), ACT.Copy, m, pf, zz)
                    ra.release(k, d[("pt", hg)])
                hold["PX"] = m
                d["pT"] = (kp, p_)

            def s5(t):
                d = tl[t]
                kp, p_ = d["pT"]
                k, bk, free = ra.take()
                for h in range(8):
                    o_ = PS[:, bk + h // 4, (h % 4) * 65:(h % 4 + 1) * 65]
                    m = mm(o_, p_[:, h, 0:128], d["v"][1][:, h, :], True, True, d[("pt", h // 4)], d["v"][2], free, sig=(h == 7 and not t))
                    if t:
                        m = mm(o_[0:64, :], p_[:, h, 128:192], tl[t - 1]["v"][1][:, h, :], False, True, sig=(h == 7), skip=True)
                ptr.release(kp, m)
                if t:
                    vr.release(tl[t - 1]["v"][0], m)
                src = PS[:, bk:bk + 2, 0:260].rearrange("p b (h d) -> p b h d", h=4)
                a = rcp(DEN.rearrange("p (b h) -> p b h", b=2), src[:, :, :, 64], m, hold["O"])
                a = tt(dve, O.rearrange("p (b h d) -> p b h d", b=2, h=4), src[:, :, :, 0:64],
                       DEN.rearrange("p (b h) -> p b h", b=2).unsqueeze(3).broadcast_to([P, 2, 4, 64]), ALU.mult, a, hold["O"])
                ra.release(k, a)
                d["o"] = a

            def s6(t):
                d = tl[t]
                k, bk, free = ra.take()
                for j in range(4):
                    m = tr(PS[:, bk, j * 128:(j + 1) * 128], O[:, j * 128:(j + 1) * 128], d["o"], free, sig=(j == 3))
                hold["O"] = m
                d["ott"] = (k, bk, av(OTT, bank(bk), ACT.Copy, m, hold["OTT"]))

            def s7(t):
                k, bk, a = tl[t]["ott"]
                for j in range(4):
                    m = mm(bank(bk + 1, 128), OTT[:, j * 128:(j + 1) * 128], wo[:, j, :], j == 0, j == 3, a, sig=(j == 3))
                hold["OTT"] = m
                x = tt(dve, X[:, t, :], X[:, t, :], bank(bk + 1, 128), ALU.add, m, xt, state["kept"])
                ra.release(k, x)
                state["x"] = x

            for i in range(NT + 4):
                if 4 <= i:
                    s7(i - 4)
                if 1 <= i <= NT:
                    s0v(i - 1)
                if i < NT:
                    s0(i)
                if 3 <= i < NT + 3:
                    s4(i - 3)
                if i < NT:
                    s0b(i)
                if 3 <= i < NT + 3:
                    s5(i - 3)
                if 1 <= i <= NT:
                    s0w(i - 1)
                if 2 <= i < NT + 2:
                    s2(i - 2, 0)
                if 3 <= i < NT + 3:
                    s6(i - 3)
                if 2 <= i < NT + 2:
                    s2(i - 2, 1)
                if 1 <= i <= NT:
                    s1(i - 1)
            barrier()
            HN = wk(0, 2048)
            FH = [wk(2048 + i * 1536, 1536).rearrange("p (k n) -> p k n", k=3) for i in range(2)]
            GE = [wk(5120 + i * 512, 512) for i in range(3)]
            xt = transpose_x([0, 1], shifted=True)
            r2, r3 = Ring([2, 3, 4, 5]), Ring([6, 7])
            hnd = []
            for b0 in (0, 2):
                held = []
                for sl in range(2):
                    b = b0 + sl
                    k, bk, free = r2.take()
                    for j in range(4):
                        t = 4 * b + j
                        m = tr(PS[:, bk, j * 128:(j + 1) * 128], XT[:, t * 128:(t + 1) * 128], xt[b], xt[max(b - 1, 0)], free, sig=(j == 3))
                    s = ln_stats(sl, PS[:, bk, :].rearrange("p (j f) -> p j f", j=4), m)
                    held.append((k, bk))
                rs, s = ln_scale(0, 2, s)
                for sl in range(2):
                    k, bk = held[sl]
                    for j in range(4):
                        u = ts(dve, Y[:, sl, j, :], PS[:, bk, j * 128:(j + 1) * 128], MV[:, sl, j, 0:1], rs[:, 4 * sl + j:4 * sl + j + 1], ALU.subtract, ALU.mult, s, state.get(("y", sl)))
                    r2.release(k, u)
                    state[("y", sl)] = u
                for sl in range(2):
                    b = b0 + sl
                    k, bk, free = r3.take()
                    for j in range(4):
                        m = tr(PS[:, bk, j * 128:(j + 1) * 128], Y[:, sl, j, :], state[("y", sl)], free, sig=(j == 3))
                    state[("y", sl)] = m
                    a = av(HN[:, b * 512:(b + 1) * 512], bank(bk), ACT.Identity, m, scale=c("lg", l, l + 1), bias=c("lb", l, l + 1))
                    r3.release(k, a)
                    hnd.append(a)
            if l == 1:
                X5 = wk(8192, 2048)
                d_ = load(X5, x_keep, state["kept"], pe.last, act.last, dve.last, pool.last)
                state["x"] = tt(pool, X[:, :, :], X[:, :, :], X5.rearrange("p (t f) -> p t f", t=NT), ALU.add, d_, xt)
            ring, ger, fhr, oring = Ring([4, 5, 2, 3]), Ring(GE), Ring(FH), Ring([0, 1])
            for i in range(4):
                ring.release(i, r2.free[(i + 2) % 4])
            oring.release(0, xt)
            oring.release(1, xt)
            for b in range(NB):
                s_ = slice(b * 512, (b + 1) * 512)
                kf, fb, ff = fhr.take()
                hd = []
                for kb, (off, w_) in enumerate(BLK3):
                    k1, b1, f1 = ring.take()
                    m1 = mm(bank(b1, p1=w_), w1[:, HID2 + off:HID2 + off + w_], HN[:, s_], True, True, hnd[b], f1, sig=True)
                    k2, b2, f2 = ring.take()
                    m2 = mm(bank(b2, p1=w_), w1[:, off:off + w_], HN[:, s_], True, True, f2, sig=True)
                    kg, ge, gf = ger.take()
                    a = av(ge[0:w_, :], bank(b1, p1=w_), ACT.Gelu, m1, gf, bias=c("fb1", l * 6 + 3 + kb, l * 6 + 4 + kb, p1=w_))
                    ring.release(k1, a)
                    h = stt(fb[0:w_, kb, :], bank(b2, p1=w_), c("fb1", l * 6 + kb, l * 6 + kb + 1, p1=w_), ge[0:w_, :], ALU.add, ALU.mult, m2, a, ff)
                    ring.release(k2, h)
                    ger.release(kg, h)
                    hd.append(h)
                k, bk, free = oring.take()
                for j in range(4):
                    for kb, (off, w_) in enumerate(BLK3):
                        m = mm(PS[:, bk, j * 128:(j + 1) * 128], fb[0:w_, kb, j * 128:(j + 1) * 128], w2[0:w_, kb, :], kb == 0, kb == 2, hd, free, sig=(j == 3 and kb == 2))
                fhr.release(kf, m)
                pv = PS[:, bk, :].rearrange("p (t f) -> p t f", t=4)
                if l == 0:
                    xs = X[:, 4 * b:4 * b + 4, :]
                    u = tt(dve, xs, pv, xs, ALU.add, m, state["x"])
                    oring.release(k, u)
                    u = tt(dve, xs, xs, c("fb2", 0, 128).unsqueeze(1).broadcast_to([P, 4, P]), ALU.add, u)
                else:
                    t0, u = ln_block(b, pv, m, b % 2, c("fb2", 128, 256))
                    oring.release(k, t0)
            state["x"] = u

        def l3_attn():
            wq, wkv, ow = W1[:, 0:1024], W1[:, 1024:1536], W1[:, 1536:2560].rearrange("p (k f) -> p k f", k=8)
            K1 = wk(0, 4096).bitcast(F16).rearrange("p (g n) -> p g n", g=4)
            K2 = wk(4096, 4096).bitcast(F16).rearrange("p (g n) -> p g n", g=4)
            OT = wk(8192, 4096).rearrange("p (h n) -> p h n", h=8)
            PTB = [wk(12288 + i * 512, 512) for i in range(6)]
            OU = wk(19456, 512)
            QF = [wk(15360 + i * 512, 512) for i in range(2)]
            RC = XB[:, :, :].rearrange("p t f -> p (t f)")
            V = W0[:, 0:4096].rearrange("p (t g d) -> p t g d", t=NT, g=4)
            AC = [W0[:, 4096 + i * 512:4608 + i * 512] for i in range(4)]
            Q1 = [wk(16384 + i * 256, 256).bitcast(F16) for i in range(6)]
            Q2 = [wk(17920 + i * 256, 256).bitcast(F16) for i in range(6)]
            SC, QBS = NR[:, 0, 64:80], NR[:, 0, 80:96]
            PM = [NR[:, 1, 64 + i * 16:80 + i * 16].rearrange("p (t h s) -> p t h s", t=4, h=2) for i in range(2)]
            NM = [NR[:, 1, 128 + i * 4:132 + i * 4].bitcast(BF16).rearrange("p (t h) -> p t h", h=2) for i in range(2)]
            PICK = NR[64:66, 0, 96:98]
            xt = transpose_x([0, 1])
            a = ts(dve, SC[:, 0:1], c("scal"), -1.0, None, ALU.mult, None)
            a = tt(dve, SC[:, 1:2], SC[:, 0:1], c("scal"), ALU.min, a)
            a = av(SC[:, 2:3], SC[:, 1:2], ACT.Exp, a)
            a = ts(dve, SC[:, 2:3], SC[:, 2:3], 1.0, None, ALU.add, None, a)
            a = av(SC[:, 3:4], SC[:, 2:3], ACT.Ln, a)
            a = ts(dve, SC[:, 4:5], c("scal"), 0.0, SC[:, 3:4], ALU.max, ALU.add, a)
            scd = ts(dve, SC[:, 5:6], SC[:, 4:5], 8.0 * 1.442695041, None, ALU.mult, None, a)
            scale = SC[:, 5:6]
            qbd = ts(dve, QBS, c("qb"), scale, None, ALU.mult, None, scd)
            zq = [ms(dve, q_[64:128, :], 0.0) for q_ in Q2]
            pick = ts(dve, PICK, eye[64:66, 64:66], 1.0 / 64, None, ALU.mult, None)
            WQ2, WK2 = W1[:, 2560:4608], W1[:, 4608:5120]
            wd = [cp(dve, WK2.rearrange("p (h a d) -> p h a d", a=2, d=64), wkv[:, 0:256].rearrange("p (h d) -> p h d", d=64).unsqueeze(2).broadcast_to([P, 4, 2, 64]), d_l3w),
                  cp(pool, WQ2.rearrange("p (h a d) -> p h a d", a=2, d=64), wq.rearrange("p (h d) -> p h d", d=64).unsqueeze(2).broadcast_to([P, 16, 2, 64]), d_l3w)]
            ring = Ring([2, 3, 4, 5])
            khr = Ring([PTB[0].bitcast(F16)[:, 0:512], PTB[1].bitcast(F16)[:, 0:512]])
            k2z = ms(pool, K2[64:128, :, :], 0.0, pool.last)
            k2z = ms(pool, K2[64:66, :, :], 64.0, k2z)
            kd = [[k2z] for _ in range(4)]
            for g in range(4):
                wk2 = WK2[:, g * 128:(g + 1) * 128]
                for b in range(NB):
                    s_ = slice(b * 512, (b + 1) * 512)
                    k, bk, free = ring.take()
                    m = mm(bank(bk), wk2, XT[:, s_], True, True, wd, xt[b], free, sig=True)
                    kh, hb, hf = khr.take()
                    a = av(K2[0:64, g, s_], bank(bk, p1=64), ACT.Identity, m, bias=c("kb", g, g + 1, p1=64))
                    a1 = av(hb[64:128, :], bank(bk, p0=64), ACT.Identity, hf, bias=c("kb", g, g + 1, p0=64))
                    a2 = stt(K1[64:128, g, s_], bank(bk, p0=64), c("kb", g, g + 1, p0=64), hb[64:128, :], ALU.add, ALU.subtract, a1)
                    ring.release(k, a2)
                    khr.release(kh, a2)
                    kd[g] += [a2, cp(dve, K1[0:64, g, s_], K2[0:64, g, s_], a)]
            vd = []
            for t in range(NT):
                k, bk, free = ring.take()
                m = mm(bank(bk, 256), XT[:, t * 128:(t + 1) * 128], wkv[:, 256:512], True, True, free, sig=True)
                a = tt(dve, V[:, t, :, :], PS[:, bk, 0:256].rearrange("p (g d) -> p g d", g=4), c("vb").rearrange("p (g d) -> p g d", g=4), ALU.add, m)
                ring.release(k, a)
                vd.append(a)
            setup = [e.last for e in (act, dve, pool)]
            mr, sr, orr, misc = Ring([0, 2]), Ring([4, 5]), Ring([6]), Ring([7])
            nmr = [None, None]
            qr = [Ring([0, 1, 2]), Ring([3, 4, 5])]
            ptr, acr = Ring(PTB), Ring(AC)
            rcf = {"rc": None, "ot": None}
            jobs = [(b, pr) for b in range(NB) for pr in range(8)]
            info = {}
            qff = [None, None]

            def prefetch(job):
                b, pr = job
                g = pr // 2
                slot = pr % 2
                d = {"q": [None, None]}
                info[job] = d

                def qproj(i):
                    h = 2 * pr + i
                    k, bk, free = misc.take()
                    w_ = WQ2[:, h * 128:(h + 1) * 128]
                    m = mm(bank(bk), w_, XT[:, b * 512:(b + 1) * 512], True, True, xt, free, setup, sig=True)
                    kq, qi, qf = qr[i].take()
                    a = av(Q1[qi], bank(bk), ACT.Identity, m, qf, qbd, scd, scale=scale, bias=QBS[:, h:h + 1])
                    a1 = av(QF[i][0:64, :], bank(bk, p1=64), ACT.Identity, qff[i], scale=scale[0:64, :], bias=QBS[0:64, h:h + 1])
                    misc.release(k, a1)
                    a2 = tt(dve, Q2[qi][0:64, :], QF[i][0:64, :], Q1[qi][0:64, :], ALU.subtract, a1, zq[-1], qf)
                    qff[i] = a2
                    d["q"][i] = (kq, qi, a, a2)

                def maxes(i, t, hf):
                    _, qi, a, _ = d["q"][i]
                    k, bk, free = mr.take()
                    for n in range(2):
                        o_ = hf * 1024 + n * 512
                        m = mm(bank(bk + n), Q1[qi][:, t * 128:(t + 1) * 128], K1[:, g, o_:o_ + 512], True, True, a, kd[g], free, setup, sig=(n == 1))
                    r = red(PM[slot][:, t, i, hf:hf + 1], PS[:, bk:bk + 2, :].rearrange("p b n -> p (b n)"), ALU.max, m)
                    mr.release(k, r)
                    d[("m", i)] = r

                def rowmax():
                    d["nm"] = red(NM[slot], PM[slot], ALU.max, d[("m", 0)], d[("m", 1)], nmr[slot], negate=True)

                def row():
                    r = d["nm"]
                    k, bk, free = misc.take()
                    for t in range(4):
                        m = mm(PS[64:66, bk, t * 128:(t + 1) * 128], NM[slot][:, t, :], cb("identb"), True, True, r, free, sig=(t == 3))
                    nmr[slot] = m
                    for i in range(2):
                        kq, qi, a, a2 = d["q"][i]
                        u = av(Q2[qi][64:66, :], PS[64:66, bk, :], ACT.Copy, m, zq, pick, scale=PICK[:, i:i + 1])
                        d[("r", i)] = [u, a, a2]
                    misc.release(k, u)

                steps = [lambda: qproj(0), lambda: qproj(1)]
                for t in range(4):
                    for hf in range(2):
                        for i in range(2):
                            steps.append(lambda i=i, t=t, hf=hf: maxes(i, t, hf))
                steps += [rowmax, row]
                return steps

            def finish(b):
                h = {}

                def product(j):
                    if not j:
                        h["bank"] = misc.take()
                    k, bk, free = h["bank"]
                    for pr in range(8):
                        m = mm(PS[:, bk, j * 128:(j + 1) * 128], OT[:, pr, j * 128:(j + 1) * 128], ow[:, pr, :], pr == 0, pr == 7, rcf["otd"], free, sig=(j == 3 and pr == 7))
                    rcf["ot"] = m

                def norm():
                    k, bk, _ = h["bank"]
                    t0, u = ln_block(b, PS[:, bk, :].rearrange("p (t f) -> p t f", t=4), rcf["ot"], b % 2, c("ob"), pair=False)
                    misc.release(k, t0)
                    state["x2"] = u
                return [lambda: product(0), lambda: product(1), lambda: product(2), lambda: product(3), norm]

            def divide(pr, ac, acd, ou):
                h = {}

                def den():
                    h["bank"] = misc.take()
                    k, bk, free = h["bank"]
                    for i in range(2):
                        h["m"] = mm(PS[64 * i:64 * i + 64, bk, :], c("ones", 0, 64), ac[i][1], True, True, acd[i], free, sig=True)
                        acr.release(ac[i][0], h["m"])

                def part(j):
                    k, bk, _ = h["bank"]
                    s_ = slice(j * 128, (j + 1) * 128)
                    r = rcp(RC[:, s_], PS[:, bk, s_], h["m"])
                    if j == 3:
                        misc.release(k, r)
                    r = tt(dve, OT[:, pr, s_], OU[:, s_], RC[:, s_], ALU.mult, r, ou, rcf["ot"])
                    rcf["rc"] = rcf["otd"] = r
                return [den, lambda: part(0), lambda: part(1), lambda: part(2), lambda: part(3)]

            prep = [prefetch(j) for j in jobs] + [[], []]
            for s in prep[0] + prep[1][:10]:
                s()
            del prep[1][:10]
            PREP = {6: (0,), 7: (0, 1), 8: (0, 1), 9: (1,), 10: (0, 1), 11: (1,0), 12: (1, 1), 13: (1,), 14: (1,), 15: (1,)}
            TAIL = (1, 2, 3, 4, 5, 11, 12, 13, 14, 15)
            tail = []
            for ji, job in enumerate(jobs):
                b, pr = job
                g = pr // 2
                d = info[job]
                ko, ob, of = orr.take()
                ac = [acr.take() for _ in range(2)]
                acd = [None, None]
                pend = None

                def pv(kt, pts):
                    for i, (kp, p_, a) in enumerate(pts):
                        m = mm(PS[64 * i:64 * i + 64, ob, :], V[:, kt, g, :], p_, kt == 0, kt == 15, a, vd[kt], of, sig=True)
                        eng = pool if i else dve
                        if kt == 0:
                            u = cp(eng, ac[i][1], p_, a, ac[i][2], pool.last)
                        else:
                            u = tt(eng, ac[i][1], ac[i][1], p_, ALU.add, a, acd[i])
                        acd[i] = u
                        ptr.release(kp, m, u)
                    return m
                for kt in range(NT):
                    pts = []
                    for i in range(2):
                        kq, qi, a, _ = d["q"][i]
                        k, bk, free = sr.take()
                        s_ = slice(kt * 128, (kt + 1) * 128)
                        mm(bank(bk), K1[:, g, s_], Q1[qi], True, False, d[("r", i)], kd[g], free)
                        m = mm(bank(bk), K2[:, g, s_], Q2[qi], False, True, sig=True)
                        if kt == NT - 1:
                            qr[i].release(kq, m)
                        kp, p_, pf = ptr.take()
                        a = av(p_, bank(bk), ACT.Exp, m, pf, scale=1.0 / 64)
                        sr.release(k, a)
                        pts.append((kp, p_, a))
                    if pend:
                        pv(*pend)
                    pend = (kt, pts)
                    n1, n2 = prep[ji + 1], prep[ji + 2]
                    for todo in PREP.get(kt, (0,)):
                        todo = (n1, n2)[todo]
                        if todo:
                            todo.pop(0)()
                    if kt in TAIL and tail:
                        tail.pop(0)()
                m = pv(*pend)
                ou = av(OU, bank(ob), ACT.Copy, m, rcf["rc"])
                orr.release(ko, ou)
                assert not tail and not n1
                tail = divide(pr, ac, acd, ou)
                if pr == 7:
                    tail += finish(b)
            for s in tail:
                s()
            state["x"] = state["x2"]

        A_wout = [WO2[:, 0:128], WO2[:, 128:256]]

        phases = [l0_attn, l0_ffn, l1_attn, lambda: tern(W1[:, :], d_f1, "f1"), mamba,
                  lambda: (local_layer(0), barrier(), local_layer(1)), l3_attn, lambda: tern(W0[:, 6228:11860], d_f3, "f3")]
        pe.wait(d_cb)
        act.wait(d_cb)
        dve.wait(d_cb)
        pool.wait(d_cb)
        for i_, ph in enumerate(phases[:upto]):
            ph()
            ends = barrier()
            if i_ == 0:
                for e in (pe, act, dve, pool):
                    e.wait(d_cb2)
            if i_ == 1:
                d_l2 = load(W0[:, 0:6228], A["l2w"], ends)
                d_f3 = load(W0[:, 6228:11860], A["f3w"])
            if i_ == 3:
                d_l3w = load(W1[:, :], A["l3w"], ends)

        s_out = sem("s_out")
        sp.run(lambda e: e.dma_start(out.rearrange("(t p) f -> p t f", p=P), X[:, :, :]).then_inc(s_out, 16), state["x"])
        sp.wait((s_out, 16))

        block = ctx.enter_context(nc.Block())

        @block.sync
        def _(eng):
            for op in sp.ops:
                op(eng)

        @block.tensor
        def _(eng):
            for op in pe.ops:
                op(eng)

        @block.scalar
        def _(eng):
            for op in act.ops:
                op(eng)

        @block.vector
        def _(eng):
            for op in dve.ops:
                op(eng)

        @block.gpsimd
        def _(eng):
            for op in pool.ops:
                op(eng)


def cols(v):
    return np.ascontiguousarray(v.reshape(-1, P).T)


def rows(v):
    return np.broadcast_to(v.reshape(1, -1), (P, v.size))


def tall(a):
    k = a.shape[0] // P
    return np.ascontiguousarray(a.reshape(k, P, -1).transpose(1, 0, 2).reshape(P, -1))


def pad_rows(a, n=P):
    o = np.zeros((n,) + a.shape[1:], a.dtype)
    o[:a.shape[0]] = a
    return o


def twice(a):
    return np.concatenate([a, a], 0)


def lay_out(i):
    f = np.float32
    t = np.arange(T)
    s = {}
    ar = np.arange(P)
    s["ident"] = np.eye(P, dtype=f)
    s["bmask"] = (ar[:, None] // 8 == ar[None] // 8).astype(f)
    s["hmask"] = (ar[:, None] // 8 == np.arange(16)[None]).astype(f)
    idx = (f(np.pi / 2) * np.arange(1, T + 1, dtype=f) / f(T)).astype(f)
    s["sin"], s["cos"] = cols(np.sin(idx).astype(f)), cols(np.cos(idx).astype(f))
    s["ones"] = np.ones((P, P), f)
    s["b0"] = rows(np.concatenate([i["L0_attn_bq"], i["L0_attn_bk"], i["L0_attn_bv"]]))
    s["bo0"] = rows(i["L0_attn_bo"])
    s["rb"] = rows(i["L0_ffn_router_b"])
    s["iota8"] = rows(np.arange(8, dtype=f))
    s["mb1"] = cols(i["L0_ffn_b1"].reshape(-1))
    s["mb2"] = pad_rows(i["L0_ffn_b2"])
    s["l1bq"], s["l1bk"] = cols(i["L1_attn_bq"]), cols(i["L1_attn_bk"])
    s["l1bkv"] = rows(np.concatenate([i["L1_attn_bk"], i["L1_attn_bv"]]))
    s["l1bo"] = rows(i["L1_attn_bo"])
    s["decay"] = np.broadcast_to(np.asarray(i["L1_attn_decay_param"]).reshape(1, 1), (P, 1))
    n = ar[None, :] - 1 - ar[:, None]
    s["expn"] = np.maximum(n, 0).astype(f)
    s["tri"] = (n >= 0).astype(f)
    s["trow"] = rows(ar.astype(f))
    s["scol"] = (127 - ar).astype(f).reshape(P, 1)
    for k, m in (("f1", "L1_ffn_"), ("f3", "L3_ffn_")):
        s[k + "s1"], s[k + "s2"] = cols(i[m + "w1_s"]), cols(i[m + "w2_s"])
        s[k + "h1"], s[k + "h2"] = cols(i[m + "h1_s"]), cols(i[m + "h2_s"])
        s[k + "s3"] = rows(i[m + "w3_s"])
    s["cxw"] = i["L2_attn_conv_x_w"].reshape(4, P).T
    s["czw"] = i["L2_attn_conv_z_w"].reshape(4, P).T
    s["cxb"], s["czb"] = cols(i["L2_attn_conv_x_b"]), cols(i["L2_attn_conv_z_b"])
    s["invdt"], s["Dp"] = cols(i["L2_attn_inv_dt"]), cols(i["L2_attn_D"])
    s["bout"] = rows(i["L2_attn_b_out"])
    s["acol"] = np.zeros((P, 16), f)
    s["qks"] = rows(np.concatenate([i["L2_ffn_q_scale"], i["L2_ffn_k_scale"]], 1).reshape(-1))
    s["lg"], s["lb"] = i["L2_ffn_ln_g"].T, i["L2_ffn_ln_b"].T
    fb = np.zeros((2, 2, 3, P), f)
    for b, (o, w) in enumerate(BLK3):
        fb[:, :, b, :w] = i["L2_ffn_b1"].reshape(2, 2, HID2)[:, :, o:o + w]
    s["fb1"] = fb.reshape(12, P).T
    s["fb2"] = rows(i["L2_ffn_b2"].reshape(-1))
    s["scal"] = twice(i["L3_attn_scaling"].reshape(64, 1))
    qb = i["L3_attn_qkv_b"]
    s["qb"] = twice(qb[:1024].reshape(16, 64).T)
    s["kb"] = twice(qb[1024:1280].reshape(4, 64).T)
    s["vb"] = rows(qb[1280:])
    s["ob"] = rows(i["L3_attn_o_b"])
    a = {}
    a["cb"] = np.concatenate([np.asarray(s[k], f).reshape(P, w) for k, w in SPEC], 1)

    z = {}
    neg = -1e30
    q_, k_ = ar[:, None], np.arange(192)[None] - 64
    z["identb"] = np.eye(P)
    z["maskS"] = np.where((k_ <= q_) & (k_ >= q_ - 64), 0, neg)
    for nm, o in (("selB", 0), ("selC", 16)):
        m = np.zeros((P, 16, P))
        for st in range(16):
            for part in range(3):
                m[32 * part + o + st, st, :] = 1
        z[nm] = m.reshape(P, -1)
    a["cbb"] = (np.concatenate([z[k] for k, w in BSPEC], 1).astype(f).view(np.uint32) >> 16).astype(np.uint16)

    a["x"] = i["L0_attn_query"].reshape(T, P)
    w_x = i["L2_attn_W_xdbl"]
    a["w2"] = np.concatenate([
        i["L0_attn_Wq"], i["L0_attn_Wk"], i["L0_attn_Wv"], i["L0_attn_Wo"], i["L0_ffn_router_w"].T,
        i["L1_attn_Wq"], i["L1_attn_Wk"], i["L1_attn_Wv"], i["L1_attn_Wo"],
        i["L2_attn_W_in"], w_x, pad_rows(i["L2_attn_W_dt"])], 1)
    a["wout"] = tall(i["L2_attn_W_out"])
    a["mw1"] = np.ascontiguousarray(i["L0_ffn_w1"].reshape(8 * 1024, P).T)
    a["mw2"] = np.concatenate([tall(np.ascontiguousarray(w.T)) for w in i["L0_ffn_w2"]], 1)
    for k, m in (("f1w", "L1_ffn_"), ("f3w", "L3_ffn_")):
        a[k] = np.concatenate([i[m + "w1_w"].T, i[m + "w2_w"].T] + [tall(np.ascontiguousarray(i[m + n].T)) for n in ("h1_w", "h2_w", "w3_w")], 1)
    lw = []
    for l in range(2):
        lw += [i["L2_ffn_wqkv"][l], tall(i["L2_ffn_wo"][l]), i["L2_ffn_w1"][l], tall(pad_rows(i["L2_ffn_w2"][l], 384))]
    a["l2w"] = np.concatenate(lw, 1)
    half = np.arange(0, 64, 2, dtype=f)
    inv = (f(1.0) / f(10000.0) ** (half / f(64))).astype(f)
    fr = t.astype(f)[:, None] * inv[None]
    base = (half + f(0.4 * 64)) / f(1.4 * 64)
    pw = (t - T // 2).astype(f) / f(32)
    sc = base[None] ** pw[:, None]
    co, si = np.cos(fr), np.sin(fr)
    tb = np.stack([8 * co * sc, 8 * si * sc, -8 * si * sc, co / sc, si / sc, -si / sc]).astype(f)
    tb = tb.reshape(6, NT, P, 32).transpose(2, 0, 1, 3).reshape(P, 3072)
    a["l3w"] = np.concatenate([i["L3_attn_qkv_w"].T, tall(np.ascontiguousarray(i["L3_attn_o_w"].T)), tb], 1)
    return {k: np.ascontiguousarray(v) for k, v in a.items()}


def kernel(**inputs):
    import concourse.bacc as _bacc
    from concourse.bass_utils import run_bass_kernel_spmd as _run

    arrays = lay_out({k: np.asarray(v) for k, v in inputs.items()})
    nc = _bacc.Bacc("TRN2", target_bir_lowering=False, num_devices=1)
    aps = {k: nc.dram_tensor(f"in_{k}", v.shape, mybir.dt.from_np(v.dtype), kind="ExternalInput").ap() for k, v in arrays.items()}
    out = nc.dram_tensor("out_0", (T, P), F32, kind="ExternalOutput").ap()
    program(nc, aps, out)
    r = _run(nc, [{f"in_{k}": v for k, v in arrays.items()}], core_ids=[0])
    return r.results[0]["out_0"].reshape(1, T, P)
```

```python
from contextlib import ExitStack

import numpy as np

import concourse.bass as bass
from concourse import mybir

F32 = mybir.dt.float32
BF16 = mybir.dt.bfloat16
F16 = mybir.dt.float16
I32 = mybir.dt.int32
U32 = mybir.dt.uint32
ALU = mybir.AluOpType
ACT = mybir.ActivationFunctionType
AX = mybir.AxisListType

T, P, NT, NB = 2048, 128, 16, 4
HID2 = 341
BLK3 = [(0, 128), (128, 128), (256, 85)]

SPEC = [
    ("ident", 128), ("bmask", 128), ("hmask", 16), ("sin", 16), ("cos", 16), ("ones", 128),
    ("b0", 384), ("bo0", 128), ("rb", 8), ("iota8", 8), ("mb1", 64), ("mb2", 128),
    ("l1bq", 1), ("l1bk", 1), ("l1bkv", 256), ("l1bo", 128), ("decay", 1), ("expn", 128), ("tri", 128),
    ("trow", 128), ("scol", 1),
    ("f1s1", 4), ("f1s2", 4), ("f1h1", 4), ("f1h2", 4), ("f1s3", 128),
    ("cxw", 4), ("czw", 4), ("cxb", 1), ("czb", 1), ("invdt", 1), ("Dp", 1), ("bout", 128), ("acol", 16),
    ("qks", 256), ("lg", 2), ("lb", 2), ("fb1", 12), ("fb2", 256),
    ("scal", 1), ("qb", 16), ("kb", 4), ("vb", 256), ("ob", 128),
    ("f3s1", 4), ("f3s2", 4), ("f3h1", 4), ("f3h2", 4), ("f3s3", 128),
]
OFF, NC = {}, 0
for _n, _w in SPEC:
    OFF[_n] = (NC, _w)
    NC += _w
BSPEC = [("identb", 128), ("maskS", 192), ("selB", 2048), ("selC", 2048), ("selm", 1024)]
BOFF, NBC = {}, 0
for _n, _w in BSPEC:
    BOFF[_n] = (NBC, _w)
    NBC += _w


class Eng:

    def __init__(self, sem):
        self.sem, self.n, self.ops, self.seen = sem, 0, [], {}

    def wait(self, *after):
        for t in after:
            if t is None:
                continue
            if isinstance(t, list):
                self.wait(*t)
                continue
            sem, v = t
            if self.seen.get(id(sem), 0) < v:
                self.seen[id(sem)] = v
                self.ops.append(lambda e, s=sem, n=v: e.wait_ge(s, n))

    def run(self, fn, *after):
        self.wait(*after)
        self.ops.append(fn)

    def do(self, fn, *after):
        self.wait(*after)
        self.n += 1
        self.ops.append(lambda e: fn(e).then_inc(self.sem, 1))
        return (self.sem, self.n)

    @property
    def last(self):
        return (self.sem, self.n)


class Ring:

    def __init__(self, bufs):
        self.bufs, self.free, self.i = bufs, [[] for _ in bufs], 0

    def take(self):
        k = self.i % len(self.bufs)
        self.i += 1
        return k, self.bufs[k], self.free[k]

    def release(self, k, *tokens):
        self.free[k] = list(tokens)


def program(nc, A, out, upto=8):
    ctx = ExitStack()
    with ctx:
        def sb(name, shape, dt=F32):
            return ctx.enter_context(nc.sbuf_tensor(name, shape, dt))

        X = sb("X", [P, NT, P])
        XT = sb("XT", [P, T + 1])
        CB = sb("CB", [P, NC])
        CBB = sb("CBB", [P, NBC], BF16)
        W0 = sb("W0", [P, 12288])
        W1 = sb("W1", [P, 5632])
        W2 = sb("W2", [P, 1512])
        NWK = 21700
        WK = sb("WK", [P, NWK])
        WO2 = sb("WO2", [P, 256])
        XB = sb("XB", [P, 4, P])
        ST = sb("ST", [P, 4, 4, 6])
        MV = sb("MV", [P, 4, 4, 2])
        NR = sb("NR", [P, 3, 256])
        SX = sb("SX", [P, 32])
        PS = ctx.enter_context(nc.psum_tensor("PS", [P, 8, 512], F32))
        eye = CB[:, OFF["ident"][0]:OFF["ident"][0] + 128]

        def c(name, a=0, b=None, p0=0, p1=P):
            o, w = OFF[name]
            return CB[p0:p1, o + a:o + (w if b is None else b)]

        def cb(name, a=0, b=None, p0=0, p1=P):
            o, w = BOFF[name]
            return CBB[p0:p1, o + a:o + (w if b is None else b)]

        def wk(off, n):
            assert off + n <= NWK, (off, n)
            return WK[:, off:off + n]

        def sem(name):
            return ctx.enter_context(nc.semaphore(name))

        pe, act, dve, pool, sp = (Eng(sem(f"s_{n}")) for n in ("pe", "act", "dve", "pool", "sp"))
        engines = [pe, act, dve, pool, sp]

        def mm(o, l, r, start, stop, *after, sig=False, skip=False):
            f = lambda e: e.matmul(o, l, r, start=start, stop=stop, skip_group_check=skip)
            return pe.do(f, *after) if sig else pe.run(f, *after)

        def tr(o, i, *after, sig=False):
            f = lambda e: e.transpose(o, i, eye)
            return pe.do(f, *after) if sig else pe.run(f, *after)

        def av(o, i, func, *after, bias=0.0, scale=1.0):
            return act.do(lambda e: e.activation(o, i, func, bias=bias, scale=scale), *after)

        def tt(eng, o, a, b, op, *after):
            return eng.do(lambda e: e.tensor_tensor(o, a, b, op), *after)

        def ts(eng, o, a, s1, s2, op0, op1, *after):
            if op1 is None:
                return eng.do(lambda e: e.tensor_scalar(o, a, s1, None, op0), *after)
            return eng.do(lambda e: e.tensor_scalar(o, a, s1, s2, op0, op1), *after)

        def stt(o, a, s, b, op0, op1, *after):
            return dve.do(lambda e: e.scalar_tensor_tensor(out=o, in0=a, scalar=s, in1=b, op0=op0, op1=op1), *after)

        def cp(eng, o, i, *after):
            return eng.do(lambda e: e.tensor_copy(o, i), *after)

        def red(o, i, op, *after, negate=None):
            return dve.do(lambda e: e.tensor_reduce(o, i, AX.X, op, negate=negate), *after)

        def ms(eng, o, v, *after):
            return eng.do(lambda e: e.memset(o, v), *after)

        def rcp(o, i, *after):
            return dve.do(lambda e: e.reciprocal(o, i), *after)

        def load(dst, src, *after):
            s = sem(f"s_ld{load.n}")
            load.n += 1
            sp.run(lambda e: e.dma_start(dst, src).then_inc(s, 16), *after)
            return (s, 16)
        load.n = 0

        def barrier():
            ends = [e.last for e in (pe, act, dve, pool) if e.n]
            for e in (pe, act, dve, pool):
                e.wait(ends)
            return ends

        def rsqrt(o, v, n, slot, *after):
            a, b = NR[:, 0, slot:slot + n], NR[:, 1, slot:slot + n]
            t = dve.do(lambda e: e.tensor_single_scalar(a.bitcast(I32), v.bitcast(I32), 1, ALU.logical_shift_right), *after)
            t = ts(dve, o.bitcast(I32), a.bitcast(I32), -1.0, 1597463007.0, ALU.mult, ALU.add, t)
            for _ in range(3):
                t = tt(dve, a, o, o, ALU.mult, t)
                t = stt(b, a, -0.5, v, ALU.mult, ALU.mult, t)
                t = stt(o, b, 1.5, o, ALU.add, ALU.mult, t)
            return t

        def bank(b, n=512, p0=0, p1=P):
            return PS[p0:p1, b, 0:n]

        x_keep = nc.dram_tensor("x_keep", (P, T), F32, kind="Internal").ap()

        c1 = OFF["rb"][0]
        d_cb = load(CB[:, 0:c1], A["cb"][:, 0:c1])
        d_x = load(X[:, :, :], A["x"].rearrange("(t p) f -> p t f", p=P))
        d_w2 = load(W2[:, :], A["w2"])
        sp.wait(d_cb, d_x, d_w2)
        d_cb2 = load(CB[:, c1:], A["cb"][:, c1:])
        d_cbb = load(CBB[:, :].bitcast(mybir.dt.uint16), A["cbb"])
        d_moe = []
        for e_ in range(8):
            a_ = load(W0[:, e_ * 1024:(e_ + 1) * 1024], A["mw1"][:, e_ * 1024:(e_ + 1) * 1024])
            b_ = load(W0[:, 8192 + e_ * 512:8192 + (e_ + 1) * 512], A["mw2"][:, e_ * 512:(e_ + 1) * 512])
            d_moe.append([a_, b_])
        d_wo2 = load(WO2[:, :], A["wout"])
        d_f1 = load(W1[:, :], A["f1w"])

        state = {"x": d_x, "free": []}

        def transpose_x(banks, shifted=False):
            if not shifted and "xt" in state:
                return state.pop("xt")
            rows = state.pop("rows", None)
            ring = Ring(banks)
            done = []
            for b in range(NB):
                k, bk, free = ring.take()
                for j in range(4):
                    t = tr(PS[:, bk, j * 128:(j + 1) * 128], X[:, 4 * b + j, :], d_cb, rows[b] if rows else state["x"], free, sig=(j == 3))
                if not shifted:
                    if b % 2:
                        u = av(XT[:, b * 512:(b + 1) * 512], bank(bk), ACT.Copy, t)
                    else:
                        u = cp(dve, XT[:, b * 512:(b + 1) * 512], bank(bk), t)
                    done.append(u)
                    ring.release(k, u)
                else:
                    u = cp(dve, XT[0:64, b * 512:(b + 1) * 512], bank(bk, p1=64), t)
                    v = av(XT[64:128, b * 512 + 1:(b + 1) * 512 + 1], bank(bk, p0=64), ACT.Copy, t)
                    done.append([u, v])
                    ring.release(k, u, v)
            return done

        def ln_stats(slot, y, tok):
            for j in range(4):
                s = dve.do(lambda e, j=j: e.bn_stats(ST[:, slot, j, :], y[:, j, :]), tok)
            for j in range(4):
                a = dve.do(lambda e, j=j: e.bn_aggr(MV[:, slot, j, :], ST[:, slot, j, :]), s)
            return a

        def ln_scale(slot, n, tok):
            var = NR[:, 2, slot * 4:slot * 4 + 4 * n]
            rs = NR[:, 2, 16 + slot * 4:16 + slot * 4 + 4 * n]
            s = ts(dve, var.rearrange("p (s j) -> p s j", j=4), MV[:, slot:slot + n, :, 1], 1e-5, None, ALU.add, None, tok)
            return rs, rsqrt(rs, var, 4 * n, slot * 4, s)

        def add_bias(row, *after):
            state["x"] = tt(pool, X[:, :, :], X[:, :, :], row.unsqueeze(1).broadcast_to([P, NT, P]), ALU.add, state["x"], pool.last, *after)

        def ln_block(b, src, src_tok, n):
            xs = X[:, 4 * b:4 * b + 4, :]
            t0 = tt(dve, xs, src, xs, ALU.add, src_tok, state["x"])
            a = ln_stats(b, xs, t0)
            if (b + 1) % n:
                return t0
            b0 = b + 1 - n
            rs, s = ln_scale(b0, n, a)
            off = NR[:, 2, 32 + 4 * b0:32 + 4 * b0 + 4 * n]
            o = stt(off.rearrange("p (s j) -> p s j", j=4), MV[:, b0:b0 + n, :, 0], -1.0, rs.rearrange("p (s j) -> p s j", j=4), ALU.mult, ALU.mult, s)
            rows = state.setdefault("rows", [None] * NB)
            for i in range(4 * n):
                t, r = 4 * b0 + i, rs[:, i:i + 1]
                if i % 2:
                    v = av(X[:, t, :], X[:, t, :], ACT.Identity, o, scale=r, bias=off[:, i:i + 1])
                else:
                    u = ts(dve, X[:, t, :], X[:, t, :], MV[:, t // 4, t % 4, 0:1], r, ALU.subtract, ALU.mult, s)
                if i % 4 == 3:
                    rows[t // 4] = [u, v]
            if b == NB - 1:
                state["x"] = [tok for r in rows for tok in r]
            return t0

        def l0_attn():
            wqkv, wo = W2[:, 0:384], W2[:, 384:512]
            Q, K, V = wk(0, 2048).rearrange("p (t f) -> p t f", t=NT), wk(2048, 2048).rearrange("p (t f) -> p t f", t=NT), wk(4096, NT * 129).rearrange("p (t f) -> p t f", t=NT)
            o = 4096 + NT * 129
            TMP = [wk(o + i * 512, 512) for i in range(2)]
            o += 1024
            K4 = [wk(o + i * 512, 512).rearrange("p (s f) -> p s f", s=4) for i in range(2)]
            o += 1024
            R = wk(o, 576).rearrange("p (s f) -> p s f", s=4)
            o += 576
            QT, CQT = wk(o, 2048), wk(o + 2048, 2048)
            o += 4096
            NUM = [wk(o + i * 288, 288) for i in range(3)]
            o += 864
            AO = wk(o, 2048).rearrange("p (t f) -> p t f", t=NT)
            o += 2048
            SM = [wk(o + i * 64, 64) for i in range(2)]
            o += 128
            AT = QT
            xt = transpose_x([0, 1])
            one = ms(pool, V[:, :, 128], 1.0)
            add_bias(c("bo0"), xt)
            ring = Ring([2, 3, 0, 1])
            ring.release(2, xt)
            ring.release(3, xt)
            tmp, k4r = Ring(TMP), Ring(K4)
            kvd = None
            qd = []
            mid = {}
            last_kv = []
            proj = {}

            def project(t):
                k, bk, free = ring.take()
                proj[t] = (k, bk, mm(bank(bk, 384), XT[:, t * 128:(t + 1) * 128], wqkv, True, True, d_w2, xt[t // 4], free, sig=True))

            def first(t):
                k, bk, m = proj.pop(t)
                kt, tb, tfree = tmp.take()
                qk = tb[:, 0:256]
                a = tt(dve, qk, PS[:, bk, 0:256], c("b0", 0, 256), ALU.add, m, tfree)
                yield
                g = qk.rearrange("p (g d) -> p g d", d=8)
                sm = SM[t % 2]
                a1 = red(sm[:, 0:32], g, ALU.max, a)
                yield
                a2 = tt(dve, g, g, sm[:, 0:32].unsqueeze(2).broadcast_to([P, 32, 8]), ALU.subtract, a1)
                e = av(qk, qk, ACT.Exp, a2)
                yield
                v = tt(dve, V[:, t, 0:128], PS[:, bk, 256:384], c("b0", 256, 384), ALU.add, m)
                ring.release(k, v, a)
                mid[t] = (kt, g, e, v)

            def second(t):
                kt, g, a, v = mid.pop(t)
                sm = SM[t % 2]
                a = red(sm[:, 32:64], g, ALU.add, a)
                yield
                a = rcp(sm[:, 32:64], sm[:, 32:64], a)
                yield
                r = sm[:, 32:64].unsqueeze(2).broadcast_to([P, 32, 8])
                k_ = tt(dve, K[:, t, :].rearrange("p (g d) -> p g d", d=8), g[:, 16:32, :], r[:, 16:32, :], ALU.mult, a)
                q_ = tt(dve, Q[:, t, :].rearrange("p (g d) -> p g d", d=8), g[:, 0:16, :], r[:, 0:16, :], ALU.mult, a)
                tmp.release(kt, q_)
                qd.append(q_)
                yield
                kk, kb, kfree = k4r.take()
                sn, cs = c("sin", t, t + 1), c("cos", t, t + 1)
                w = ts(pool, kb[:, 2, :], K[:, t, :], -1.0, 1.0, ALU.mult, ALU.add, k_, kfree, pool.last)
                av(kb[:, 0, :], K[:, t, :], ACT.Copy, k_, kfree, scale=sn)
                av(kb[:, 1, :], K[:, t, :], ACT.Copy, scale=cs)
                a = av(kb[:, 3, :], kb[:, 2, :], ACT.Copy, w, scale=cs)
                a = av(kb[:, 2, :], kb[:, 2, :], ACT.Copy, a, scale=sn)
                for s in range(4):
                    m = mm(bank(4 + s, 129), kb[:, s, :], V[:, t, 0:129], t == 0, t == NT - 1, a, v, one, sig=(s == 3))
                k4r.release(kk, m)
                last_kv.append(m)
            for t in range(3):
                project(t)
            for t in range(NT + 1):
                if t + 3 < NT:
                    project(t + 3)
                turns = ([second(t - 1)] if t else []) + ([first(t)] if t < NT else [])
                for _ in range(4):
                    for turn in turns[::-1]:
                        next(turn, None)
            kvd = last_kv[-1]
            rd = []
            for s in range(4):
                tt(dve, R[:, s, 0:128], PS[:, 4 + s, 0:128], c("bmask"), ALU.mult, kvd)
                rd.append(ts(dve, R[:, s, 128:144], c("hmask"), PS[:, 4 + s, 128:129], None, ALU.mult, None, kvd))
            ring = Ring([0, 1])
            last_v = dve.last
            qt = []
            for b in range(NB):
                k, bk, free = ring.take()
                for j in range(4):
                    m = tr(PS[:, bk, j * 128:(j + 1) * 128], Q[:, 4 * b + j, :], qd[4 * b + j], free, last_v, sig=(j == 3))
                s_ = slice(b * 512, (b + 1) * 512)
                u = av(QT[:, s_], bank(bk), ACT.Copy, m)
                w = ts(dve, CQT[:, s_], QT[:, s_], -1.0, 1.0, ALU.mult, ALU.add, u)
                ring.release(k, u)
                qt.append([u, w])
            ring = Ring([2, 3, 4, 5])
            nr = Ring(NUM)
            aod = []
            num = {}

            def numer(t):
                s_ = slice(t * 128, (t + 1) * 128)
                toks = []
                for br, src in enumerate((QT, CQT)):
                    k, bk, free = ring.take()
                    m = mm(bank(bk, 288), src[:, s_], R[:, 2 * br:2 * br + 2, :], True, True, rd, qt[t // 4], free, sig=True)
                    toks.append((k, bk, m))
                kn, nb, nfree = nr.take()
                N = [nb[:, 0:144], nb[:, 144:288]]
                pieces = [av(N[i], PS[:, bk, 0:144], ACT.Copy, m, nfree, scale=c("sin", t, t + 1)) for i, (k, bk, m) in enumerate(toks)]
                for i, (k, bk, m) in enumerate(toks):
                    pieces[i] = stt(N[i], PS[:, bk, 144:288], c("cos", t, t + 1), N[i], ALU.mult, ALU.add, pieces[i])
                    ring.release(k, pieces[i])
                num[t] = (kn, nb, pieces)

            def quotient(t):
                kn, nb, pieces = num.pop(t)
                n2 = nb.rearrange("p (b f) -> p b f", b=2)
                den = n2[:, :, 128:144]
                a = ts(dve, den, den, 1e-6, None, ALU.max, None, pieces)
                a = rcp(den, den, a)
                nv = n2[:, :, 0:128].rearrange("p b (h d) -> p b h d", d=8)
                a = tt(dve, nv, nv, den.unsqueeze(3).broadcast_to([P, 2, 16, 8]), ALU.mult, a)
                a = tt(pool, AO[:, t, :], nb[:, 0:128], nb[:, 144:272], ALU.add, a)
                nr.release(kn, a)
                aod.append(a)
            for t in range(NT + 1):
                if t < NT:
                    numer(t)
                if t:
                    quotient(t - 1)
            ring = Ring([0, 1])
            last_q = pe.last
            ev = []
            for b in range(NB):
                k, bk, free = ring.take()
                for j in range(4):
                    m = tr(PS[:, bk, j * 128:(j + 1) * 128], AO[:, 4 * b + j, :], aod[4 * b + j], qt, free, sig=(j == 3))
                u = av(AT[:, b * 512:(b + 1) * 512], bank(bk), ACT.Copy, m, last_q)
                ring.release(k, u)
                ev.append(u)
            ring = Ring([6, 7])
            for b in range(NB):
                k, bk, free = ring.take()
                for j in range(4):
                    t = 4 * b + j
                    m = mm(PS[:, bk, j * 128:(j + 1) * 128], AT[:, t * 128:(t + 1) * 128], wo, True, True, ev[b], rd, free, sig=(j == 3))
                ring.release(k, ln_block(b, PS[:, bk, :].rearrange("p (t f) -> p t f", t=4), m, 4))

        def l0_ffn():
            XH, XL = wk(0, 1024).bitcast(F16), wk(1024, 1024).bitcast(F16)
            WH = [wk(2048 + e * 1536, 768).bitcast(F16) for e in range(8)]
            WL = [wk(2816 + e * 1536, 768).bitcast(F16) for e in range(8)]
            G3 = wk(14336, 1024).bitcast(BF16)
            GS = [wk(15360 + i * 512, 512) for i in range(2)]
            S1 = [wk(16384 + i * 512, 512) for i in range(3)]
            HF = [wk(17920 + i * 512, 512) for i in range(3)]
            HP = [wk(19456 + i * 512, 512).bitcast(F16).rearrange("p (s n) -> p s n", s=2) for i in range(4)]
            o = [19456]

            def small(n, w=8):
                o[0] += n
                return wk(o[0] - n, n).rearrange("p (t e) -> p t e", e=w)
            G, L, M8, IX, IF, O1, RG = (small(128) for _ in range(7))
            GW = small(64, 16)
            GP = small(768, 48).bitcast(BF16)
            MB1, MB2 = wk(21504, 64), wk(21568, 128)
            GT = XT
            router = W2[:, 512:520]
            state.pop("rows", None)
            ring = Ring([0, 1])
            xt, xd = [], []
            for b in range(NB):
                s_ = slice(b * 512, (b + 1) * 512)
                k, bk, free = ring.take()
                for j in range(4):
                    t = tr(PS[:, bk, j * 128:(j + 1) * 128], X[:, 4 * b + j, :], state["x"], free, sig=(j == 3))
                u = av(XT[:, s_], bank(bk), ACT.Copy, t)
                v = av(XH[:, s_], bank(bk), ACT.Copy, t)
                w = tt(dve, XL[:, s_], bank(bk), XH[:, s_], ALU.subtract, v)
                ring.release(k, w)
                xt.append(u)
                xd.append(w)
            def split_parts(e, part):
                for src, o_, n in ((W0[:, e * 1024:(e + 1) * 1024], 0, 256), (W0[:, 8192 + e * 512:8192 + (e + 1) * 512], 1024, 128)):
                    yield src[:, part * n:(part + 1) * n], slice(o_ + part * n, o_ + (part + 1) * n)

            def split_high(e, part):
                for src, q_ in split_parts(e, part):
                    h = av(WH[e][:, q_], src, ACT.Copy, d_moe[e], scale=64.0)
                return h

            def split_low(e, part, h):
                for src, q_ in split_parts(e, part):
                    wd[e].append(stt(WL[e][:, q_], src, 64.0, WH[e][:, q_], ALU.mult, ALU.subtract, h))
            wd = [[] for _ in range(8)]
            for part in range(4):
                split_low(0, part, split_high(0, part))
            cut = None
            mb1 = ts(dve, MB1, c("mb1"), 64.0, None, ALU.mult, None)
            mb2 = ts(dve, MB2[0:8, :], c("mb2", p1=8), 512.0, None, ALU.mult, None)
            g3z = ms(pool, GP, 0.0)
            for t in range(NT):
                m = mm(PS[:, 7, t * 8:t * 8 + 8], XT[:, t * 128:(t + 1) * 128], router, True, True, d_w2, xt[t // 4], sig=(t == NT - 1))
            a = tt(dve, L, PS[:, 7, 0:128].rearrange("p (t e) -> p t e", t=NT),
                   c("rb").unsqueeze(1).broadcast_to([P, NT, 8]), ALU.add, m)
            for t in range(NT):
                b = dve.do(lambda e, t=t: e.max(M8[:, t, :], L[:, t, :]), a)
            for t in range(NT):
                b2 = dve.do(lambda e, t=t: e.max_index(IX[:, t, :].bitcast(U32), M8[:, t, :], L[:, t, :]), b)
            a = cp(dve, IF, IX.bitcast(U32), b2)
            g = tt(dve, GW[:, 0, :], M8[:, :, 1], M8[:, :, 0], ALU.subtract, b)
            g = av(GW[:, 1, :], GW[:, 0, :], ACT.Exp, g)
            g = ts(dve, GW[:, 2, :], GW[:, 1, :], 1.0, None, ALU.add, None, g)
            g = rcp(GW[:, 2, :], GW[:, 2, :], g)
            g = tt(dve, GW[:, 3, :], GW[:, 1, :], GW[:, 2, :], ALU.mult, g)
            iota = c("iota8").unsqueeze(1).broadcast_to([P, NT, 8])
            pick = [tt(dve, o_, iota, IF[:, :, i:i + 1].broadcast_to([P, NT, 8]), ALU.is_equal, a) for i, o_ in enumerate((G, O1))]
            pick = [tt(dve, o_, o_, GW[:, 2 + i, :].unsqueeze(2).broadcast_to([P, NT, 8]), ALU.mult, pick[i], g) for i, o_ in enumerate((G, O1))]
            g = tt(dve, G, G, O1, ALU.add, pick)
            a = cp(dve, GP[:, :, 0:8], G, g, g3z)
            a = tt(dve, RG, G, GP[:, :, 0:8], ALU.subtract, a)
            a = cp(dve, GP[:, :, 32:40], RG, a)
            a = tt(dve, RG, RG, GP[:, :, 32:40], ALU.subtract, a)
            gp = cp(dve, GP[:, :, 64:72], RG, a)

            r1, r2, gr, ar = Ring([0, 1]), Ring([2, 3, 4]), Ring([5]), Ring([6, 7])
            for i in range(2):
                r1.release(i, xd)
            gsr, s1r, hfr, hpr = Ring(GS), Ring(S1), Ring(HF), Ring(HP)

            def first(j):
                s_ = slice(j["b"] * 512, (j["b"] + 1) * 512)
                e, kb = j["e"], j["kb"]
                toks = []
                for r_, o_ in ((r1, kb * 128), (r2, 512 + kb * 128)):
                    k, bk, free = r_.take()
                    for i, (wt, x_) in enumerate(((WH, XH), (WL, XH), (WH, XL))):
                        m = mm(bank(bk), wt[e][:, o_:o_ + 128], x_[:, s_], i == 0, i == 2, wd[e], xd, free, sig=(i == 2))
                    toks.append((k, bk, m))
                j["gated"], j["up"] = toks

            def silu(j):
                e, kb = j["e"], j["kb"]
                k1, b1, m1 = j["gated"]
                ks, s1, sf = s1r.take()
                a = av(s1, bank(b1), ACT.Silu, m1, sf, bias=c("mb1", e * 8 + kb, e * 8 + kb + 1), scale=1.0 / 64)
                r1.release(k1, a)
                gs, gd = j["gate"]
                j["s1"] = (ks, s1, tt(pool, s1, s1, gs, ALU.mult, a, gd))

            def hidden(j):
                e, kb = j["e"], j["kb"]
                k2, b2, m2 = j["up"]
                ks, s1, a = j["s1"]
                kh, hf, ff = hfr.take()
                h = stt(hf, bank(b2), MB1[:, e * 8 + 4 + kb:e * 8 + 5 + kb], s1, ALU.add, ALU.mult, m2, a, ff, mb1)
                r2.release(k2, h)
                s1r.release(ks, h)
                kp, hb, pf = hpr.take()
                j["h"] = (kh, hf, kp, hb, av(hb[:, 0, :], hf, ACT.Copy, h, pf))

            def low(j):
                kh, hf, kp, hb, hh = j["h"]
                j["hl"] = tt(dve, hb[:, 1, :], hf, hb[:, 0, :], ALU.subtract, hh)
                hfr.release(kh, j["hl"])

            def second(j):
                e, kb = j["e"], j["kb"]
                _, _, kp, hb, _ = j["h"]
                for i, (wt, hx) in enumerate(((WH, 0), (WL, 0), (WH, 1))):
                    m = mm(j["acc"][1], wt[e][:, 1024 + kb * 128:1024 + (kb + 1) * 128], hb[:, hx, :], False, e == 7 and kb == 3 and i == 2, j["hl"], sig=(i == 2))
                hpr.release(kp, m)
                return m

            jobs = [{"b": i // 32, "e": i // 4 % 8, "kb": i % 4} for i in range(128)]
            first(jobs[0])
            first(jobs[1])
            ring = Ring([6, 7])
            gt = []
            for b_ in range(NB):
                s_ = slice(b_ * 512, (b_ + 1) * 512)
                k, bk, free = ring.take()
                for j in range(4):
                    m = tr(PS[0:8, bk, j * 128:(j + 1) * 128], G[:, 4 * b_ + j, :], g, free, sig=(j == 3))
                u = av(GT[0:8, s_], bank(bk, p1=8), ACT.Copy, m)
                ring.release(k, u)
                k, bk, free = ring.take()
                for j in range(4):
                    m = mm(PS[0:96, bk, j * 128:(j + 1) * 128], GP[:, 4 * b_ + j, :], cb("identb"), True, True, gp, d_cbb, free, sig=(j == 3))
                v = av(G3[0:96, s_], bank(bk, p1=96), ACT.Copy, m)
                ring.release(k, v)
                gt.append([u, v])
            for i in range(2):
                ar.release(i, gt)
            for i in range(128 + 3):
                if i < 128:
                    j = jobs[i]
                    b_, e, kb = j["b"], j["e"], j["kb"]
                    s_ = slice(b_ * 512, (b_ + 1) * 512)
                    if not kb:
                        if i:
                            gsr.release(kgs, pool.last)
                        kg, bg, fg = gr.take()
                        m = mm(bank(bg), cb("selm", e * 128, (e + 1) * 128, p1=96), G3[0:96, s_], True, True, gt, fg, sig=True)
                        kgs, gs, gf = gsr.take()
                        gd = av(gs, bank(bg), ACT.Copy, m, gf)
                        gr.release(kg, gd)
                    if not kb and not e:
                        ka, ba, fa = ar.take()
                        mm(bank(ba), MB2[0:8, :], GT[0:8, s_], True, False, mb2, fa)
                    j["gate"], j["acc"] = (gs, gd), (ka, bank(ba))
                    if i > 1:
                        first(j)
                    silu(j)
                if 2 <= i < 130:
                    low(jobs[i - 2])
                if 1 <= i < 129:
                    hidden(jobs[i - 1])
                if cut:
                    split_low(*cut)
                    cut = None
                if i < 28:
                    cut = (i // 4 + 1, i % 4, split_high(i // 4 + 1, i % 4))
                if i >= 3:
                    j = jobs[i - 3]
                    m = second(j)
                    if j["e"] == 7 and j["kb"] == 3:
                        ka_, acc = j["acc"]
                        a = av(XB[:, :, :].rearrange("p t f -> p (t f)"), acc, ACT.Copy, m, state.get("xb"), scale=1.0 / 512)
                        ar.release(ka_, a)
                        kx, bx, fx = gr.take()
                        for q in range(4):
                            m = tr(PS[:, bx, q * 128:(q + 1) * 128], XB[:, q, :], a, fx, sig=(q == 3))
                        state["xb"] = m
                        gr.release(kx, ln_block(j["b"], PS[:, bx, :].rearrange("p (t f) -> p t f", t=4), m, 4))

        def l1_attn():
            w = W2[:, 520:1032]
            QT, KT = wk(0, 2048), wk(2048, 2048)
            K, V = wk(4096, 2048).rearrange("p (t f) -> p t f", t=NT), wk(6144, 2048).rearrange("p (t f) -> p t f", t=NT)
            DT, QD = wk(8192, 128), wk(8320, 2048)
            DROW, SC = wk(10368, 128), wk(10496, 16)
            OT = wk(10896, 2048)
            TM = [wk(12944 + i * 512, 512) for i in range(4)]
            xt = transpose_x([0, 1])
            add_bias(c("l1bo"), xt)
            p_ = c("decay")
            a = ts(dve, SC[:, 0:1], p_, -1.0, None, ALU.mult, None, d_cb)
            a = tt(dve, SC[:, 1:2], SC[:, 0:1], p_, ALU.min, a)
            a = av(SC[:, 2:3], SC[:, 1:2], ACT.Exp, a)
            a = ts(dve, SC[:, 2:3], SC[:, 2:3], 1.0, None, ALU.add, None, a)
            a = av(SC[:, 3:4], SC[:, 2:3], ACT.Ln, a)
            a = ts(dve, SC[:, 4:5], SC[:, 0:1], 0.0, SC[:, 3:4], ALU.max, ALU.add, a)
            a = ts(dve, SC[:, 5:6], SC[:, 4:5], -1.0, None, ALU.mult, None, a)
            la = SC[:, 5:6]
            d1 = av(DT, c("expn"), ACT.Exp, a, scale=la)
            d2 = av(DROW, c("trow"), ACT.Exp, a, scale=la)
            d3 = av(SC[:, 6:7], c("scol"), ACT.Exp, a, scale=la)
            d4 = av(SC[:, 8:9], c("trow", 0, 1), ACT.Exp, a, scale=la)
            d5 = ts(dve, SC[:, 9:10], la, 128.0, None, ALU.mult, None, a)
            d4 = av(SC[:, 7:8], SC[:, 9:10], ACT.Exp, d5)
            d1 = tt(dve, DT, DT, c("tri"), ALU.mult, d1)
            ring = Ring([2, 3, 4, 5])
            tr_ = Ring(TM)
            qd, kd = [], []
            for b in range(NB):
                s_ = slice(b * 512, (b + 1) * 512)
                k, bk, free = ring.take()
                m = mm(bank(bk), w[:, 0:128], XT[:, s_], True, True, d_w2, xt[b], free, sig=True)
                a = ts(dve, QT[:, s_], bank(bk), c("l1bq"), None, ALU.add, None, m)
                ring.release(k, a)
                a = tt(dve, QD[:, s_].rearrange("p (c n) -> p c n", n=128), QT[:, s_].rearrange("p (c n) -> p c n", n=128),
                       DROW.unsqueeze(1).broadcast_to([P, 4, 128]), ALU.mult, a, d2)
                qd.append(a)
                k, bk, free = ring.take()
                m = mm(bank(bk), w[:, 128:256], XT[:, s_], True, True, free, sig=True)
                kt, tb, tf = tr_.take()
                a = ts(dve, tb, bank(bk), c("l1bk"), 0.0, ALU.add, ALU.min, m, tf)
                a2 = ts(dve, KT[:, s_], bank(bk), c("l1bk"), 0.0, ALU.add, ALU.max, m)
                ring.release(k, a2)
                a = av(tb, tb, ACT.Exp, a)
                a = tt(dve, KT[:, s_], KT[:, s_], tb, ALU.add, a, a2)
                tr_.release(kt, a)
                kd.append(a)
            MS = wk(14992, 2048).rearrange("p (t f) -> p t f", t=NT)
            PT = [wk(17040 + i * 512, 512) for i in range(2)]
            ring3 = Ring([0, 1])
            for i in range(2):
                ring3.release(i, xt)
            two = lambda ap: ap.rearrange("p (t f) -> p t f", t=2)
            bias = c("l1bkv").rearrange("p (s f) -> p s f", s=2)
            mid, kvd = {}, []

            def kv_project(p):
                k, bk, free = ring.take()
                for j in range(2):
                    t = 2 * p + j
                    m = mm(PS[:, bk, j * 256:(j + 1) * 256], XT[:, t * 128:(t + 1) * 128], w[:, 128:384], True, True, free, sig=(j == 1))
                kt, tb, tf = tr_.take()
                p4 = PS[:, bk, :].rearrange("p (t s f) -> p t s f", t=2, s=2)
                a = tt(dve, two(tb[:, 0:256]), p4[:, :, 0, :], bias[:, 0:1, :].broadcast_to([P, 2, 128]), ALU.add, m, tf)
                v = tt(dve, V[:, 2 * p:2 * p + 2, :], p4[:, :, 1, :], bias[:, 1:2, :].broadcast_to([P, 2, 128]), ALU.add, m)
                ring.release(k, v)
                x1 = ts(dve, tb[:, 256:512], tb[:, 0:256], 0.0, None, ALU.min, None, a)
                x1 = av(tb[:, 256:512], tb[:, 256:512], ACT.Exp, x1)
                mid[p] = (kt, tb, x1, v)

            def kv_product(p):
                kt, tb, x1, v = mid[p]
                x1 = stt(tb[:, 0:256], tb[:, 0:256], 0.0, tb[:, 256:512], ALU.max, ALU.add, x1)
                x1 = ts(dve, K[:, 2 * p:2 * p + 2, :], two(tb[:, 0:256]), SC[:, 6:7], None, ALU.mult, None, x1, d3)
                tr_.release(kt, x1)
                k, bk, free = ring3.take()
                for j in range(2):
                    t = 2 * p + j
                    m = mm(PS[:, bk, j * 128:(j + 1) * 128], K[:, t, :], V[:, t, :], True, True, x1, v, free, sig=(j == 1))
                mid[p] = (k, bk, m)
                kvd.append(v)

            def kv_state(p, md):
                k, bk, m = mid.pop(p)
                for j in range(2):
                    t = 2 * p + j
                    src = PS[:, bk, j * 128:(j + 1) * 128]
                    if t == 0:
                        md = cp(dve, MS[:, 1, :], src, m)
                    elif t < NT - 1:
                        md = stt(MS[:, t + 1, :], MS[:, t, :], SC[:, 7:8], src, ALU.mult, ALU.add, m, d4, md)
                ring3.release(k, md)
                return md
            md = None
            for p in range(10):
                if p < 8:
                    kv_project(p)
                if 1 <= p < 9:
                    kv_product(p - 1)
                if p >= 2:
                    md = kv_state(p - 2, md)
            rp, ptr = Ring([6, 7]), Ring(PT)
            pd, od = {}, []
            four = lambda ap: ap.rearrange("p (t f) -> p t f", t=4)

            def scores(b):
                k, bk, free = rp.take()
                for j in range(4):
                    s_ = slice((4 * b + j) * 128, (4 * b + j + 1) * 128)
                    m = mm(PS[:, bk, j * 128:(j + 1) * 128], KT[:, s_], QT[:, s_], True, True, qd, kd, free, sig=(j == 3))
                kp, pb_, pf = ptr.take()
                a = tt(dve, four(pb_), four(bank(bk)), DT.unsqueeze(1).broadcast_to([P, 4, 128]), ALU.mult, m, d1, pf)
                rp.release(k, a)
                pd[b] = (kp, pb_, a)

            def outputs(b):
                kp, pb_, a = pd.pop(b)
                k, bk, free = ring.take()
                for j in range(4):
                    t = 4 * b + j
                    o_ = PS[:, bk, j * 128:(j + 1) * 128]
                    if t:
                        mm(o_, MS[:, t, :], QD[:, t * 128:(t + 1) * 128], True, False, md, qd, free)
                    m = mm(o_, V[:, t, :], pb_[:, j * 128:(j + 1) * 128], t == 0, True, a, kvd, free, sig=(j == 3))
                ptr.release(kp, m)
                o_ = av(OT[:, b * 512:(b + 1) * 512], bank(bk), ACT.Copy, m)
                ring.release(k, o_)
                od.append(o_)
            for b in range(NB + 1):
                if b < NB:
                    scores(b)
                if b:
                    outputs(b - 1)
            for b in range(NB):
                k, bk, free = rp.take()
                for j in range(4):
                    t = 4 * b + j
                    m = mm(PS[:, bk, j * 128:(j + 1) * 128], OT[:, t * 128:(t + 1) * 128], w[:, 384:512], True, True, od[b], free, sig=(j == 3))
                rp.release(k, ln_block(b, PS[:, bk, :].rearrange("p (t f) -> p t f", t=4), m, 4))

        def tern(W, loaded, f):
            H1 = wk(0, 8192).rearrange("p (k n) -> p k n", k=4)
            H2 = wk(8192, 8192).rearrange("p (k n) -> p k n", k=4)
            S1 = [wk(16384 + i * 512, 512) for i in range(3)]
            h1 = W[:, 1024:3072].rearrange("p (k n) -> p k n", k=4)
            h2 = W[:, 3072:5120].rearrange("p (k n) -> p k n", k=4)
            w3 = W[:, 5120:5632].rearrange("p (k n) -> p k n", k=4)
            WP = [wk(17920 + i * 512, 512).bitcast(F16) for i in range(2)]
            XP = [wk(18944 + i * 1024, 1024).bitcast(F16) for i in range(2)]
            wd = []
            for i in range(4):
                q_ = slice(i * 256, (i + 1) * 256)
                a = av(WP[0][:, q_], W[:, q_], ACT.Copy, loaded)
                wd.append(tt(dve, WP[1][:, q_], W[:, q_], WP[0][:, q_], ALU.subtract, a))
            xt = transpose_x([0, 1])
            xd = []
            for b in range(NB):
                s_ = slice(b * 512, (b + 1) * 512)
                a = av(XP[0][:, s_], XT[:, s_], ACT.Copy, xt[b])
                xd.append(tt(dve, XP[1][:, s_], XT[:, s_], XP[0][:, s_], ALU.subtract, a))
            w1, w2 = [w_[:, 0:512] for w_ in WP], [w_[:, 512:1024] for w_ in WP]
            ring, s1r = Ring([2, 3, 4, 5, 6, 7]), Ring(S1)

            def exact(bk, w_, o_, s_, *after):
                for i, (p, q) in enumerate(((0, 0), (1, 0), (0, 1))):
                    m = mm(bank(bk), w_[p][:, o_], XP[q][:, s_], i == 0, i == 2, *after, sig=(i == 2))
                return m
            hd = [[] for _ in range(NB)]
            for b in range(NB):
                s_ = slice(b * 512, (b + 1) * 512)
                for ob in range(4):
                    o_ = slice(ob * 128, (ob + 1) * 128)
                    k1, b1, f1 = ring.take()
                    m1 = exact(b1, w1, o_, s_, wd, xd[b], f1)
                    k2, b2, f2 = ring.take()
                    m2 = exact(b2, w2, o_, s_, f2)
                    ks, s1, sf = s1r.take()
                    a = av(s1, bank(b1), ACT.Silu, m1, sf, scale=c(f + "s1", ob, ob + 1))
                    ring.release(k1, a)
                    h = stt(H1[:, ob, s_], bank(b2), c(f + "s2", ob, ob + 1), s1, ALU.mult, ALU.mult, m2, a)
                    ring.release(k2, h)
                    s1r.release(ks, h)
                    hd[b].append(h)
            src, dst = H1, H2
            for wl, sc in ((h1, f + "h1"), (h2, f + "h2")):
                nd = [[] for _ in range(NB)]
                for b in range(NB):
                    s_ = slice(b * 512, (b + 1) * 512)
                    for ob in range(4):
                        k, bk, free = ring.take()
                        for kb in range(4):
                            m = mm(bank(bk), wl[:, kb, ob * 128:(ob + 1) * 128], src[:, kb, s_], kb == 0, kb == 3, hd[b], free, sig=(kb == 3))
                        a = av(dst[:, ob, s_], bank(bk), ACT.Gelu, m, hd[b], scale=c(sc, ob, ob + 1))
                        ring.release(k, a)
                        nd[b].append(a)
                hd = nd
                src, dst = dst, src
            for b in range(NB):
                k, bk, free = ring.take()
                for j in range(4):
                    t = 4 * b + j
                    for kb in range(4):
                        m = mm(PS[:, bk, j * 128:(j + 1) * 128], src[:, kb, t * 128:(t + 1) * 128], w3[:, kb, :], kb == 0, kb == 3, hd[b], free, sig=(kb == 3 and j == 3))
                p3 = PS[:, bk, :].rearrange("p (t f) -> p t f", t=4)
                a = tt(dve, XB[:, :, :], p3, c(f + "s3").unsqueeze(1).broadcast_to([P, 4, P]), ALU.mult, m, state.get("xb"))
                ring.release(k, a)
                state["xb"] = ln_block(b, XB[:, :, :], a, 4)

        def mamba():
            w_in, w_x, w_dt = W2[:, 1032:1288], W2[:, 1288:1384], W2[0:64, 1384:1512]
            PX, PZ = wk(0, 2051), wk(2051, 2051)
            o = 4102
            U, ZS = wk(o, 2048), wk(o + 2048, 2048)
            DE, DU = wk(0, 2048), W0[:, 6228:8276]
            LOW = wk(o + 4096, 2048)
            SPL = wk(o + 6144, 1024).bitcast(BF16)
            o += 7168
            RB = [wk(o + i * 2048, 2048) for i in range(5)]
            YA = RB[0]
            CS = [LOW[:, i * 512:(i + 1) * 512] for i in range(4)]
            xt = transpose_x([0, 1])
            z = [ms(dve, PX[:, 0:1], 0.0), ms(dve, PX[:, 2049:2051], 0.0), ms(dve, PZ[:, 0:1], 0.0), ms(dve, PZ[:, 2049:2051], 0.0)]
            zs = ms(pool, SPL[96:128, :], 0.0)
            add_bias(c("bout"), xt, zs)
            ring = Ring([2, 3, 4, 5])
            cd = {}

            def project(h, b):
                dst = (PX, PZ)[h]
                k, bk, free = ring.take()
                m = mm(bank(bk), w_in[:, h * 128:(h + 1) * 128], XT[:, b * 512:(b + 1) * 512], True, True, d_w2, xt[b], free, sig=True)
                cd[h, b] = av(dst[:, 1 + b * 512:1 + (b + 1) * 512], bank(bk), ACT.Copy, m)
                ring.release(k, cd[h, b])

            def conv(src, wn, tmp, j, a, n, *after):
                if not j:
                    return ts(dve, tmp[:, a:a + n], src[:, a:a + n], c(wn, 0, 1), None, ALU.mult, None, *after)
                return stt(tmp[:, a:a + n], src[:, a + j:a + j + n], c(wn, j, j + 1), tmp[:, a:a + n], ALU.mult, ALU.add, *after)
            BC = [None] * NB
            ud = [None] * NB
            dd = [None] * NB
            E1, E2 = RB[0], RB[1]
            inv2 = NR[:, 2, 100:101]
            iv = ts(dve, inv2, c("invdt"), 2.0, None, ALU.mult, None)

            def hidden(b):
                s_ = slice(b * 512, (b + 1) * 512)
                a = [cd[0, b], cd[0, min(b + 1, 3)], cd[0, max(b - 1, 0)], z]
                for j in range(4):
                    a = conv(PX, "cxw", RB[4], j, b * 512, 512, a)
                ud[b] = [a, av(U[:, s_], RB[4][:, s_], ACT.Silu, a, bias=c("cxb"))]

            def parts(b):
                s_ = slice(b * 512, (b + 1) * 512)
                k, bk, free = ring.take()
                m = mm(PS[0:64, bk, :], w_x[:, 0:64], U[:, s_], True, True, ud[b], free, sig=True)
                l = av(LOW[0:64, s_], PS[0:64, bk, :], ACT.Copy, m)
                ring.release(k, l)
                k, bk, free = ring.take()
                m = mm(PS[0:32, bk, :], w_x[:, 64:96], U[:, s_], True, True, free, sig=True)
                p32, pm = RB[2][0:32, s_], RB[3][0:32, s_]
                a = av(SPL[0:32, s_], PS[0:32, bk, :], ACT.Copy, m)
                r = tt(dve, p32, PS[0:32, bk, :], SPL[0:32, s_], ALU.subtract, a)
                ring.release(k, r)
                a = av(SPL[32:64, s_], p32, ACT.Copy, r)
                low[b] = (l, av(pm, SPL[32:64, s_], ACT.Copy, a))

            def last_part(b):
                s_ = slice(b * 512, (b + 1) * 512)
                p32, pm = RB[2][0:32, s_], RB[3][0:32, s_]
                l, a = low[b]
                a = tt(dve, p32, p32, pm, ALU.subtract, a)
                BC[b] = [a, l, av(SPL[64:96, s_], p32, ACT.Copy, a)]

            def delta(b):
                s_ = slice(b * 512, (b + 1) * 512)
                k, bk, free = ring.take()
                m = mm(bank(bk), w_dt, LOW[0:64, s_], True, True, BC[b], free, sig=True)
                a = av(E1[:, s_], bank(bk), ACT.Abs, m, iv, bias=inv2)
                r = ts(dve, DE[:, s_], bank(bk), inv2, 0.0, ALU.add, ALU.max, a, [u[0] for u in ud])
                ring.release(k, a, r)
                dd[b] = [a, r]
            for b in range(NB):
                project(0, b)
            low = {}
            for b in range(NB + 2):
                if b < NB:
                    hidden(b)
                    project(1, b)
                if 1 <= b < NB + 1:
                    parts(b - 1)
                if b >= 2:
                    last_part(b - 2)
            for b in range(NB):
                delta(b)
            ex = av(E1, E1, ACT.Exp, dd, scale=-1.0)
            dl = []
            for b in range(NB):
                s_ = slice(b * 512, (b + 1) * 512)
                a = av(E2[:, s_], E1[:, s_], ACT.Ln, ex, bias=c("ones", 0, 1))
                a = tt(dve, DE[:, s_], DE[:, s_], E2[:, s_], ALU.add, a)
                dl.append(tt(dve, DU[:, s_], DE[:, s_], U[:, s_], ALU.mult, a))
            ra, rh = Ring(RB[0:2]), Ring(RB[2:5])
            for r_ in (ra, rh):
                for i in range(len(r_.bufs)):
                    r_.release(i, dl)
            rB, rC, csr = Ring([0, 1]), Ring([2, 3]), Ring(CS)
            for i in range(2):
                rB.release(i, dd)
                rC.release(i, dd)
            st = [dict() for _ in range(16)]

            def scale_in(n, b):
                d = st[n]
                if not b:
                    d["h"] = rh.take()
                    d["a"] = ra.take()
                    d["e"] = av(d["a"][1], DE, ACT.Exp, dl, d["a"][2], scale=-float(n + 1))
                s_ = slice(b * 512, (b + 1) * 512)
                k, bk, free = rB.take()
                m = mm(bank(bk), cb("selB", n * 128, (n + 1) * 128), SPL[:, s_], True, True, BC, zs, d_cbb, free, sig=True)
                d["w"] = tt(dve, d["h"][1][:, s_], DU[:, s_], bank(bk), ALU.mult, m, d["h"][2])
                rB.release(k, d["w"])

            def scan(n):
                d = st[n]
                hb, da = d["h"][1], d["a"][1]
                d["s"] = dve.do(lambda e: e.tensor_tensor_scan(hb, da, hb, 0.0, ALU.mult, ALU.add), d["e"], d["w"])
                ra.release(d["a"][0], d["s"])
                d["done"] = []

            def scale_out(n, b):
                d = st[n]
                s_ = slice(b * 512, (b + 1) * 512)
                k, bk, free = rC.take()
                m = mm(bank(bk), cb("selC", n * 128, (n + 1) * 128), SPL[:, s_], True, True, free, sig=True)
                kc, cs, cf = csr.take()
                u = av(cs, bank(bk), ACT.Copy, m, cf, dl)
                rC.release(k, u)
                hb = d["h"][1]
                w_ = tt(pool, hb[:, s_], hb[:, s_], cs, ALU.mult, u, d["s"])
                csr.release(kc, w_)
                d["done"].append(w_)

            def total(n, b):
                if n < 0:
                    return
                d = st[n]
                m = mm(bank(4 + b), eye, d["h"][1][:, b * 512:(b + 1) * 512], n == 0, n == 15, d["done"][b], dd, sig=True)
                if b == 3:
                    rh.release(d["h"][0], m)
                return m
            scale_in(0, 0)
            scale_in(0, 1)
            zt = None
            for n in range(16):
                scale_in(n, 2)
                scale_in(n, 3)
                scan(n)
                scale_out(n, 0)
                scale_out(n, 1)
                for b in range(2):
                    if n < 15:
                        scale_in(n + 1, b)
                total(n - 1, 0)
                total(n - 1, 1)
                scale_out(n, 2)
                scale_out(n, 3)
                total(n - 1, 2)
                total(n - 1, 3)
                if n % 4 == 1:
                    zt = conv(PZ, "czw", ZS, n // 4, 0, T, zt, [cd[1, b] for b in range(NB)], z)
            for b in range(NB):
                m = total(15, b)
            zd = av(ZS, ZS, ACT.Silu, zt, bias=c("czb"))
            ya = []
            for b in range(NB):
                s_ = slice(b * 512, (b + 1) * 512)
                ya.append(stt(YA[:, s_], U[:, s_], c("Dp"), bank(4 + b), ALU.mult, ALU.add, m, ra.free[0], zs))
            ring = Ring([0, 1])
            wo = A_wout
            ring.release(0, rB.free[0])
            ring.release(1, rB.free[1])
            for b in range(NB):
                k, bk, free = ring.take()
                for j in range(4):
                    t = 4 * b + j
                    s_ = slice(t * 128, (t + 1) * 128)
                    mm(PS[:, bk, j * 128:(j + 1) * 128], YA[:, s_], wo[0], True, False, ya[b], d_wo2, free)
                    m = mm(PS[:, bk, j * 128:(j + 1) * 128], ZS[:, s_], wo[1], False, True, zd, sig=(j == 3))
                ring.release(k, ln_block(b, PS[:, bk, :].rearrange("p (t f) -> p t f", t=4), m, 4))

        def l3_constants():
            wkv = W1[:, 1024:1536]
            SC, QBS, PICK = SX[:, 0:8], SX[:, 8:16], SX[64:66, 16:18]
            WK2 = W1[:, 4608:5120]
            wd = cp(pool, WK2.rearrange("p (h a d) -> p h a d", a=2, d=64), wkv[:, 0:256].rearrange("p (h d) -> p h d", d=64).unsqueeze(2).broadcast_to([P, 4, 2, 64]), d_l3w, pool.last)
            top = ts(dve, SC[:, 6:7], c("scal"), 0.0, None, ALU.max, None)
            a = ts(dve, SC[:, 0:1], c("scal"), -1.0, None, ALU.mult, None)
            a = tt(dve, SC[:, 1:2], SC[:, 0:1], c("scal"), ALU.min, a)
            a = av(SC[:, 2:3], SC[:, 1:2], ACT.Exp, a)
            a = ts(pool, SC[:, 2:3], SC[:, 2:3], 1.0, None, ALU.add, None, a, wd)
            a = av(SC[:, 3:4], SC[:, 2:3], ACT.Ln, a)
            a = tt(pool, SC[:, 4:5], SC[:, 6:7], SC[:, 3:4], ALU.add, top, a)
            scd = ts(pool, SC[:, 5:6], SC[:, 4:5], 8.0 * 1.442695041, None, ALU.mult, None, a)
            scale = SC[:, 5:6]
            qb = c("qb").rearrange("p (h i) -> p h i", i=2)
            qbd = [ts(pool, QBS[0:64, 0:8], qb[0:64, :, 0], scale[0:64, :], None, ALU.mult, None, scd),
                   ts(pool, QBS[64:128, 0:8], qb[64:128, :, 1], scale[64:128, :], None, ALU.mult, None, scd, pool.last)]
            pick = ts(pool, PICK, eye[64:66, 64:66], 1.0 / 64, None, ALU.mult, None, pool.last)
            state["l3"] = WK2, scale, QBS, PICK, scd, qbd, pick, wd

        def local_layer(l):
            o0 = l * 3114
            wqkv = W0[:, o0:o0 + 1536]
            wo = W0[:, o0 + 1536:o0 + 2048].rearrange("p (k f) -> p k f", k=4)
            w1 = W0[:, o0 + 2048:o0 + 2730]
            w2 = W0[:, o0 + 2730:o0 + 3114].rearrange("p (k f) -> p k f", k=3)
            o = [0]

            def take(n):
                o[0] += n
                return wk(o[0] - n, n)
            CT = take(2048).rearrange("p (t s d) -> p t s d", t=NT, s=2)
            SN = take(2048).rearrange("p (t s d) -> p t s d", t=NT, s=2)
            QK = [take(1024) for _ in range(2)]
            RO = [take(1024) for _ in range(2)]
            PB = take(1024)
            VV = [take(512).rearrange("p (h d) -> p h d", h=8) for _ in range(6)]
            QT = [take(512).rearrange("p (h n) -> p h n", h=4) for _ in range(2)]
            KZ = [take(1024).rearrange("p (h n) -> p h n", h=8) for _ in range(3)]
            PX = [take(1536).rearrange("p (h n) -> p h n", h=8) for _ in range(2)]
            PT = [take(1536).rearrange("p (h n) -> p h n", h=8)]
            OTT = take(512)
            SS, RS_ = take(32), take(32)
            NM = [take(8) for _ in range(2)]
            DEN = [take(16).rearrange("p (s h) -> p s h", s=2) for _ in range(2)]
            tab = W1[:, 2560:5632].rearrange("p (s c t d) -> p s c t d", s=2, c=3, t=NT)
            td = None
            for s in range(2):
                for hf in range(2):
                    sc = c("qks", l * 128 + s * 64 + hf * 32, l * 128 + s * 64 + hf * 32 + 32).unsqueeze(1).broadcast_to([P, NT, 32])
                    td = tt(pool, CT[:, :, s, hf * 32:hf * 32 + 32], tab[:, s, 0, :, :], sc, ALU.mult, d_l3w, td)
                    oh = 1 - hf
                    td = tt(pool, SN[:, :, s, oh * 32:oh * 32 + 32], tab[:, s, 2 if oh == 0 else 1, :, :], sc, ALU.mult, td)
            zz = [ms(dve, k_[:, :, :], 0.0) for k_ in KZ] + [ms(dve, p_[0:64, :, 128:192], 0.0) for p_ in PT]
            if l == 0:
                state["kept"] = load(x_keep, X[:, :, :].rearrange("p t f -> p (t f)"), state["x"])
            z0 = ms(dve, XT[64:128, 0:1], 0.0)
            xt = transpose_x([0, 1], shifted=True)
            ra, rb = Ring([0, 2, 4]), Ring([6, 7])
            ra.release(0, xt)
            qkr, ror, qtr, kzr, ptr, vr = Ring(QK), Ring(RO), Ring(QT), Ring(KZ), Ring(PT), Ring(VV)
            tl = [dict() for _ in range(NT)]
            hold = {"OTT": None, "PB": None, "PX": [None, None], "SS": None}

            def s0(t):
                d = tl[t]
                s_ = slice(t * 128, (t + 1) * 128)
                xd = [z0, xt[t // 4], xt[max(t * 128 - 1, 0) // 512]]
                k, bk, free = ra.take()
                mm(bank(bk), XT[:, s_], wqkv[:, 0:512], True, True, d_l2, xd, free)
                m = mm(bank(bk + 1), XT[:, s_], wqkv[:, 512:1024], True, True, sig=True)
                kq, qb_, qf = qkr.take()
                a = av(qb_.rearrange("p (b n) -> p b n", b=2), PS[:, bk:bk + 2, :], ACT.Copy, m, qf)
                ra.release(k, a)
                d["qk"] = (kq, qb_, a)

            def s0b(t):
                d = tl[t]
                kq, qb_, a = d["qk"]
                s_ = slice(t * 128, (t + 1) * 128)
                k, bk, free = rb.take()
                m = mm(bank(bk), XT[:, s_], wqkv[:, 1024:1536], True, True, free, sig=True)
                kv, vb, vf = vr.take()
                v = av(vb, PS[:, bk, :].rearrange("p (h d) -> p h d", h=8), ACT.Copy, m, vf)
                rb.release(k, v)
                d["v"] = (kv, vb, v)

            def s0c(t):
                d = tl[t]
                kq, qb_, a = d["qk"]
                kr, rbuf, rf = ror.take()
                sq = av(rbuf, qb_, ACT.Square, a, rf)
                d["ro"] = (kr, rbuf, sq)

            def s0v(t):
                d = tl[t]
                kq, qb_, a = d["qk"]
                kr, rbuf, sq = d["ro"]
                ss, rs = SS[:, 0:16], RS_[:, 0:16]
                g = red(ss, rbuf.rearrange("p (h d) -> p h d", h=16), ALU.add, sq, hold["SS"])
                g = ts(dve, ss, ss, 1e-24, None, ALU.max, None, g)
                g = rsqrt(rs, ss, 16, 32, g)
                q4 = qb_.rearrange("p (h d) -> p h d", h=16)
                g = tt(dve, q4, q4, rs.unsqueeze(2).broadcast_to([P, 16, 64]), ALU.mult, g, a)
                hold["SS"] = g
                v = tt(dve, rbuf.rearrange("p (s h d) -> p s h d", s=2, h=8), qb_.rearrange("p (s h d) -> p s h d", s=2, h=8),
                       CT[:, t, :, :].unsqueeze(2).broadcast_to([P, 2, 8, 64]), ALU.mult, g, td)
                q5 = qb_.rearrange("p (s h f d) -> p s h f d", s=2, h=8, f=2)
                p5 = PB.rearrange("p (s h f d) -> p s h f d", s=2, h=8, f=2)
                for hf in range(2):
                    w_ = tt(pool, p5[:, :, :, hf, :], q5[:, :, :, 1 - hf, :],
                            SN[:, t, :, hf * 32:hf * 32 + 32].unsqueeze(2).broadcast_to([P, 2, 8, 32]), ALU.mult, g, td, hold["PB"])
                qkr.release(kq, w_, v)
                d["half"] = [w_, v]

            def s0w(t):
                d = tl[t]
                rbuf = d["ro"][1]
                r = tt(dve, rbuf, rbuf, PB, ALU.add, d["half"])
                hold["PB"] = r
                d["rot"] = r

            def s1(t):
                d = tl[t]
                kr, rbuf, _ = d["ro"]
                k, bk, free = ra.take()
                for j in range(8):
                    m = tr(PS[:, bk + j // 4, (j % 4) * 128:(j % 4 + 1) * 128], rbuf[:, j * 128:(j + 1) * 128], d["rot"], free, sig=(j == 7))
                ror.release(kr, m)
                kq, q_, qf = qtr.take()
                kz, z_, zf = kzr.take()
                a = av(q_, PS[:, bk, :].rearrange("p (h n) -> p h n", h=4), ACT.Copy, m, qf)
                pv = PS[:, bk + 1, :].rearrange("p (h n) -> p h n", h=4)
                z4 = z_.rearrange("p (h a) n -> p h a n", a=2)
                b1 = av(z4[0:64, :, 0, :], pv[0:64, :, :], ACT.Copy, m, zf, zz)
                b2 = av(z4[64:128, :, 1, :], pv[64:128, :, :], ACT.Copy, m, zf, zz)
                ra.release(k, a, b2)
                d["q"], d["k"] = (kq, q_, a), (kz, z_, b2)

            def s2(t, hg):
                d = tl[t]
                _, q_, qd = d["q"]
                _, z_, zd = d["k"]
                nm, px, den = NM[t % 2], PX[t % 2], DEN[t % 2]
                lo = 0 if t else 64
                k, bk, free = ra.take()
                for i in range(4):
                    h = hg * 4 + i
                    b_, c0 = bk + i // 2, (i % 2) * 192
                    mm(PS[:, b_, c0 + lo:c0 + 192], cb("identb"), cb("maskS", lo, 192), True, False, d_cbb, free, qd, zd)
                    if t:
                        mm(PS[:, b_, c0:c0 + 64], q_[:, h // 2, :], tl[t - 1]["k"][1][:, h, 64:128], False, False)
                    m = mm(PS[:, b_, c0 + 64:c0 + 192], q_[:, h // 2, :], z_[:, h, :], False, True, sig=(i == 3))
                src = PS[:, bk:bk + 2, 0:384].rearrange("p b (h n) -> p b h n", h=2)[:, :, :, lo:192]
                r = red(nm[:, hg * 4:hg * 4 + 4], src, ALU.max, m, negate=True)
                for i in range(4):
                    h = hg * 4 + i
                    c0 = (i % 2) * 192
                    src = PS[:, bk + i // 2, c0 + lo:c0 + 192]
                    act.wait(r, hold["PX"][t % 2])
                    a = act.do(lambda e, h=h, src=src: e.activation(px[:, h, lo:192], src, ACT.Exp, bias=nm[:, h:h + 1], scale=1.0, accum_out=den[:, 0, h:h + 1]))
                ra.release(k, a)
                d["e"] = a
                if hg:
                    qtr.release(d["q"][0], m)
                    if t:
                        kzr.release(tl[t - 1]["k"][0], m)

            def s3(t):
                d = tl[t]
                px, den = PX[t % 2], DEN[t % 2]
                lo = 0 if t else 64
                a = rcp(den[:, 1, :], den[:, 0, :], d["e"])
                for hg in range(2):
                    hs = slice(hg * 4, hg * 4 + 4)
                    d[("p", hg)] = tt(pool, px[:, hs, lo:192], px[:, hs, lo:192], den[:, 1, hs].unsqueeze(2).broadcast_to([P, 4, 192 - lo]), ALU.mult, a)

            def s4(t, hg):
                d = tl[t]
                if not hg:
                    d["pT"] = ptr.take()
                kp, p_, pf = d["pT"]
                px = PX[t % 2]
                k, bk, free = ra.take()
                hs = slice(hg * 4, hg * 4 + 4)
                for i in range(4):
                    m = tr(PS[:, bk, i * 128:(i + 1) * 128], px[:, hg * 4 + i, 64:192], d[("p", hg)], free, sig=(i == 3))
                d[("pt", hg)] = av(p_[:, hs, 0:128], bank(bk).rearrange("p (h n) -> p h n", h=4), ACT.Copy, m, pf)
                if t:
                    for i in range(4):
                        o_ = PS[64:128, bk + 1, i * 64:(i + 1) * 64]
                        m = mm(o_, px[:, hg * 4 + i, 0:64], eye[:, 0:64], True, True, sig=(i == 3))
                    d[("pt", hg)] = av(p_[64:128, hs, 128:192], PS[64:128, bk + 1, 0:256].rearrange("p (h n) -> p h n", h=4), ACT.Copy, m, pf, zz)
                ra.release(k, d[("pt", hg)])
                hold["PX"][t % 2] = m

            def s5(t):
                d = tl[t]
                kp, p_, _ = d["pT"]
                k, bk, free = rb.take()
                for j in range(4):
                    for q in range(2):
                        h = 2 * j + q
                        o_ = PS[64 * q:64 * q + 64, bk, j * 128:(j + 1) * 128]
                        m = mm(o_, d["v"][1][:, h, :], p_[:, h, 0:128], True, True, d[("pt", h // 4)], d["v"][2], free, sig=(h == 7 and not t))
                    if t:
                        for q in range(2):
                            h = 2 * j + q
                            m = mm(PS[64 * q:64 * q + 64, bk, j * 128:j * 128 + 64], tl[t - 1]["v"][1][:, h, :], p_[:, h, 128:192], False, True, sig=(h == 7), skip=True)
                ptr.release(kp, m)
                if t:
                    vr.release(tl[t - 1]["v"][0], m)
                d["ott"] = av(OTT, bank(bk), ACT.Copy, m, hold["OTT"])
                rb.release(k, d["ott"])

            def s7(t):
                k, bk, free = rb.take()
                for j in range(4):
                    m = mm(bank(bk, 128), OTT[:, j * 128:(j + 1) * 128], wo[:, j, :], j == 0, j == 3, tl[t]["ott"], free, sig=(j == 3))
                hold["OTT"] = m
                x = tt(dve, X[:, t, :], X[:, t, :], bank(bk, 128), ALU.add, m, xt, state["kept"])
                rb.release(k, x)
                state["x"] = x

            for i in range(NT + 5):
                if 5 <= i:
                    s7(i - 5)
                if 1 <= i <= NT:
                    s0v(i - 1)
                if 3 <= i < NT + 3:
                    s3(i - 3)
                if i < NT:
                    s0(i)
                if 4 <= i < NT + 4:
                    s4(i - 4, 0)
                if i < NT:
                    s0b(i)
                if 4 <= i < NT + 4:
                    s4(i - 4, 1)
                if 2 <= i < NT + 2:
                    s2(i - 2, 0)
                if 4 <= i < NT + 4:
                    s5(i - 4)
                if i < NT:
                    s0c(i)
                if 1 <= i <= NT:
                    s0w(i - 1)
                if 2 <= i < NT + 2:
                    s2(i - 2, 1)
                if 1 <= i <= NT:
                    s1(i - 1)
            barrier()
            HN = wk(0, 2048)
            FH = [wk(2048 + i * 1536, 1536).rearrange("p (k n) -> p k n", k=3) for i in range(2)]
            GE = [wk(5120 + i * 512, 512) for i in range(3)]
            xt = transpose_x([0, 1], shifted=True)
            if l == 1:
                l3_constants()
                X5 = wk(8192, 2048)
                d_ = load(X5, x_keep, state["kept"], pe.last, act.last, dve.last, pool.last)
                state["x"] = tt(pool, X[:, :, :], X[:, :, :], X5.rearrange("p (t f) -> p t f", t=NT), ALU.add, d_, xt)
            add_bias(c("fb2", l * 128, (l + 1) * 128), xt)
            r2, r3 = Ring([2, 3, 4, 5]), Ring([6, 7])
            YF = wk(10240, 2048).rearrange("p (s j f) -> p s j f", s=4, j=4)
            hnd, held = [], []
            for b in range(NB):
                k, bk, free = r2.take()
                for j in range(4):
                    t = 4 * b + j
                    m = tr(PS[:, bk, j * 128:(j + 1) * 128], XT[:, t * 128:(t + 1) * 128], xt[b], xt[max(b - 1, 0)], free, sig=(j == 3))
                s = ln_stats(b, PS[:, bk, :].rearrange("p (j f) -> p j f", j=4), m)
                held.append((k, bk))
            rs, s = ln_scale(0, 4, s)
            off = NR[:, 2, 32:48]
            o_ = stt(off.rearrange("p (s j) -> p s j", j=4), MV[:, :, :, 0], -1.0, rs.rearrange("p (s j) -> p s j", j=4), ALU.mult, ALU.mult, s)
            for b in range(NB):
                k, bk = held[b]
                for j in range(4):
                    i = 4 * b + j
                    src = PS[:, bk, j * 128:(j + 1) * 128]
                    if b % 2:
                        u = av(YF[:, b, j, :], src, ACT.Identity, o_, scale=rs[:, i:i + 1], bias=off[:, i:i + 1])
                    else:
                        u = ts(dve, YF[:, b, j, :], src, MV[:, b, j, 0:1], rs[:, i:i + 1], ALU.subtract, ALU.mult, s)
                r2.release(k, u)
                held[b] = u
            for b in range(NB):
                k, bk, free = r3.take()
                for j in range(4):
                    m = tr(PS[:, bk, j * 128:(j + 1) * 128], YF[:, b, j, :], held[b], free, sig=(j == 3))
                hn = HN[:, b * 512:(b + 1) * 512]
                if b % 2:
                    a = ts(dve, hn, bank(bk), c("lg", l, l + 1), c("lb", l, l + 1), ALU.mult, ALU.add, m)
                else:
                    a = av(hn, bank(bk), ACT.Identity, m, scale=c("lg", l, l + 1), bias=c("lb", l, l + 1))
                r3.release(k, a)
                hnd.append(a)
            ring, ger, fhr, oring = Ring([4, 5, 2, 3]), Ring(GE), Ring(FH), Ring([0, 1])
            for i in range(4):
                ring.release(i, r2.free[(i + 2) % 4])
            oring.release(0, xt)
            oring.release(1, xt)
            for b in range(NB):
                s_ = slice(b * 512, (b + 1) * 512)
                kf, fb, ff = fhr.take()
                hd = []
                for kb, (off, w_) in enumerate(BLK3):
                    k1, b1, f1 = ring.take()
                    m1 = mm(bank(b1, p1=w_), w1[:, HID2 + off:HID2 + off + w_], HN[:, s_], True, True, hnd[b], f1, sig=True)
                    k2, b2, f2 = ring.take()
                    m2 = mm(bank(b2, p1=w_), w1[:, off:off + w_], HN[:, s_], True, True, f2, sig=True)
                    kg, ge, gf = ger.take()
                    a = av(ge[0:w_, :], bank(b1, p1=w_), ACT.Gelu, m1, gf, bias=c("fb1", l * 6 + 3 + kb, l * 6 + 4 + kb, p1=w_))
                    ring.release(k1, a)
                    h = stt(fb[0:w_, kb, :], bank(b2, p1=w_), c("fb1", l * 6 + kb, l * 6 + kb + 1, p1=w_), ge[0:w_, :], ALU.add, ALU.mult, m2, a, ff)
                    ring.release(k2, h)
                    ger.release(kg, h)
                    hd.append(h)
                k, bk, free = oring.take()
                for j in range(4):
                    for kb, (off, w_) in enumerate(BLK3):
                        m = mm(PS[:, bk, j * 128:(j + 1) * 128], fb[0:w_, kb, j * 128:(j + 1) * 128], w2[0:w_, kb, :], kb == 0, kb == 2, hd, free, sig=(j == 3 and kb == 2))
                fhr.release(kf, m)
                pv = PS[:, bk, :].rearrange("p (t f) -> p t f", t=4)
                if l == 0:
                    xs = X[:, 4 * b:4 * b + 4, :]
                    u = tt(dve, xs, pv, xs, ALU.add, m, state["x"])
                    oring.release(k, u)
                else:
                    oring.release(k, ln_block(b, pv, m, 4))
            if l == 0:
                state["x"] = u

        def l3_attn():
            wq, wkv, ow = W1[:, 0:1024], W1[:, 1024:1536], W1[:, 1536:2560].rearrange("p (k f) -> p k f", k=8)
            K1 = wk(0, 4096).bitcast(F16).rearrange("p (g n) -> p g n", g=4)
            K2 = wk(4096, 4096).bitcast(F16).rearrange("p (g n) -> p g n", g=4)
            OT = wk(8192, 4096).rearrange("p (h n) -> p h n", h=8)
            PTB = [wk(12288 + i * 512, 512) for i in range(6)]
            OU = wk(19456, 512)
            QF = [wk(15360 + i * 512, 512) for i in range(2)]
            RC = XB[:, :, :].rearrange("p t f -> p (t f)")
            V = W0[:, 0:4096].rearrange("p (t g d) -> p t g d", t=NT, g=4)
            AC = [W0[:, 4096 + i * 512:4608 + i * 512] for i in range(4)]
            Q1 = [wk(16384 + i * 256, 256).bitcast(F16) for i in range(6)]
            Q2 = [wk(17920 + i * 256, 256).bitcast(F16) for i in range(6)]
            PM = [NR[:, 1, 64 + i * 32:96 + i * 32].rearrange("p (t h s) -> p t h s", t=4, h=2) for i in range(2)]
            NM = [NR[:, 1, 128 + i * 4:132 + i * 4].bitcast(BF16).rearrange("p (t h) -> p t h", h=2) for i in range(2)]
            xt = transpose_x([0, 1])
            add_bias(c("ob"), xt)
            WK2, scale, QBS, PICK, scd, qbd, pick, wd = state["l3"]
            room = [wk(19968 + i * 256, 256) for i in range(6)] + [W2[:, i * 256:(i + 1) * 256] for i in range(2)] + [W1[:, 2560 + i * 256:2816 + i * 256] for i in range(8)]
            K3 = [[room[g * 4 + b].bitcast(F16) for b in range(NB)] for g in range(4)]
            ring = Ring([4, 5, 6])
            k2z = ms(pool, K2[64:128, :, :], 0.0, pool.last)
            k2z = ms(pool, K2[64:66, :, :], 64.0, k2z)
            kd = [[] for _ in range(4)]
            vd = []

            def kproj(g, b):
                s_ = slice(b * 512, (b + 1) * 512)
                k, bk, free = ring.take()
                m = mm(bank(bk), WK2[:, g * 128:(g + 1) * 128], XT[:, s_], True, True, wd, xt[b], free, sig=True)
                hb = K3[g][b]
                a = av(K2[0:64, g, s_], bank(bk, p1=64), ACT.Identity, m, bias=c("kb", g, g + 1, p1=64))
                a1 = av(hb[64:128, :], bank(bk, p0=64), ACT.Identity, wd, bias=c("kb", g, g + 1, p0=64))
                a2 = stt(K1[64:128, g, s_], bank(bk, p0=64), c("kb", g, g + 1, p0=64), hb[64:128, :], ALU.add, ALU.subtract, a1)
                a3 = av(K1[0:64, g, s_], bank(bk, p1=64), ACT.Identity, m, bias=c("kb", g, g + 1, p1=64))
                ring.release(k, a2, a3)
                kd[g] += [a2, a3]

            def vproj(t):
                k, bk, free = ring.take()
                m = mm(bank(bk, 256), XT[:, t * 128:(t + 1) * 128], wkv[:, 256:512], True, True, free, xt[t // 4], sig=True)
                a = tt(dve, V[:, t, :, :], PS[:, bk, 0:256].rearrange("p (g d) -> p g d", g=4), c("vb").rearrange("p (g d) -> p g d", g=4), ALU.add, m)
                ring.release(k, a)
                vd.append(a)
            mr, sr, orr, misc = Ring([0, 2]), Ring([4, 5]), Ring([6]), Ring([7])
            mr.release(0, xt)
            nmr = [None, None]
            qr = [Ring([0, 1, 2]), Ring([3, 4, 5])]
            ptr, acr = Ring(PTB), Ring(AC)
            rcf = {"rc": None, "ot": None}
            jobs = [(b, pr) for b in range(NB) for pr in range(8)]
            info = {}
            qff = [None, None]

            def prefetch(job):
                b, pr = job
                g = pr // 2
                slot = pr % 2
                d = {"q": [None, None]}
                info[job] = d

                def qproj():
                    k, bk, free = misc.take()
                    m = mm(bank(bk), wq[:, pr * 128:(pr + 1) * 128], XT[:, b * 512:(b + 1) * 512], True, True, xt, d_l3w, free, sig=True)
                    d["f"] = av(QF[slot], bank(bk), ACT.Identity, m, qff[slot], qbd, scd, scale=scale, bias=QBS[:, pr:pr + 1])
                    misc.release(k, d["f"])

                def split(i):
                    kq, qi, qf = qr[i].take()
                    f_ = QF[slot][64 * i:64 * i + 64, :]
                    own, other = slice(64 * i, 64 * i + 64), slice(64 - 64 * i, 128 - 64 * i)
                    a1 = av(Q1[qi][own, :], f_, ACT.Copy, d["f"], qf)
                    a = cp(dve, Q1[qi][other, :], f_, d["f"], qf)
                    a2 = tt(dve if i else pool, Q2[qi][0:64, :], f_, Q1[qi][own, :], ALU.subtract, a1, zq[-1], qf)
                    qff[slot] = [a, a2] if i == 0 else qff[slot] + [a, a2]
                    d["q"][i] = (kq, qi, [a, a1], a2)

                def maxes(t, n):
                    k, bk, free = mr.take()
                    ts_ = slice(t * 128, (t + 1) * 128)
                    (_, q0, a0, _), (_, q1, a1, _) = d["q"]
                    mm(bank(bk), Q1[q0][0:64, ts_], K2[0:64, g, n * 512:(n + 1) * 512], True, True, a0, a1, kd[g], free)
                    m = mm(bank(bk + 1), Q1[q1][64:128, ts_], K3[g][n][64:128, :], True, True, sig=True)
                    r = red(PM[slot][:, t, :, n], PS[:, bk:bk + 2, :], ALU.max, m)
                    mr.release(k, r)
                    d["m"] = r

                def rowmax():
                    d["nm"] = red(NM[slot], PM[slot], ALU.max, d["m"], nmr[slot], negate=True)

                def row():
                    r = d["nm"]
                    k, bk, free = misc.take()
                    for t in range(4):
                        m = mm(PS[64:66, bk, t * 128:(t + 1) * 128], NM[slot][:, t, :], cb("identb"), True, True, r, free, sig=(t == 3))
                    nmr[slot] = m
                    for i in range(2):
                        kq, qi, a, a2 = d["q"][i]
                        u = av(Q2[qi][64:66, :], PS[64:66, bk, :], ACT.Copy, m, zq, pick, scale=PICK[:, i:i + 1])
                        d[("r", i)] = [u, a, a2]
                    misc.release(k, u)

                steps = [qproj, lambda: (split(0), split(1))]
                for t in range(4):
                    for n in range(4):
                        steps.append(lambda t=t, n=n: maxes(t, n))
                steps += [rowmax, row]
                return steps

            def finish(b):
                h = {}

                def product(j):
                    if not j:
                        h["bank"] = misc.take()
                    k, bk, free = h["bank"]
                    for pr in range(8):
                        m = mm(PS[:, bk, j * 128:(j + 1) * 128], OT[:, pr, j * 128:(j + 1) * 128], ow[:, pr, :], pr == 0, pr == 7, rcf["otd"], free, sig=(j == 3 and pr == 7))
                    rcf["ot"] = m

                def norm():
                    k, bk, _ = h["bank"]
                    misc.release(k, ln_block(b, PS[:, bk, :].rearrange("p (t f) -> p t f", t=4), rcf["ot"], 1))
                return [lambda: product(0), lambda: product(1), lambda: product(2), lambda: product(3), norm]

            def finish_last(b):
                def part(pr):
                    for j in range(4):
                        js = slice(j * 128, (j + 1) * 128)
                        for p in pr:
                            m = mm(PS[:, 2 + j, 0:128], OT[:, p, js], ow[:, p, :], p == 0, p == 7, rcf["otd"], mr.free[1], sr.free, sig=(p == 7 and j == 3))
                    rcf["ot"] = m

                return [lambda: part(range(7)), lambda: part(range(7, 8)), lambda: ln_block(b, PS[:, 2:6, 0:128], rcf["ot"], 1)]

            def divide(pr, ac, acd, ou):
                h = {}

                def den():
                    h["bank"] = misc.take()
                    k, bk, free = h["bank"]
                    for i in range(2):
                        h["m"] = mm(PS[64 * i:64 * i + 64, bk, :], c("ones", 0, 64), ac[i][1], True, True, acd[i], free, sig=True)
                        acr.release(ac[i][0], h["m"])

                def part(j):
                    k, bk, _ = h["bank"]
                    s_ = slice(j * 128, (j + 1) * 128)
                    r = rcp(RC[:, s_], PS[:, bk, s_], h["m"])
                    if j == 3:
                        misc.release(k, r)
                    h["r"] = r
                    if j == 3:
                        r = tt(pool, OT[:, pr, :], OU, RC, ALU.mult, r, ou, rcf["ot"])
                        rcf["rc"] = rcf["otd"] = r
                return [den, lambda: part(0), lambda: part(1), lambda: part(2), lambda: part(3)]

            prep = [prefetch(j) for j in jobs] + [[], []]
            for b in range(NB):
                kproj(0, b)
            zq = [ms(dve, q_[64:128, :], 0.0) for q_ in Q2]
            steps = prep[0] + prep[1][:10]
            del prep[1][:10]
            load_kv = [lambda g=g, b=b: kproj(g, b) for g in range(1, 4) for b in range(NB)] + [lambda t=t: vproj(t) for t in range(NT)]
            while steps or load_kv:
                for todo in (steps, load_kv):
                    if todo:
                        todo.pop(0)()
            sr.release(0, ring.free[0])
            sr.release(1, ring.free[1])
            orr.release(0, ring.free[2])
            PREP = {6: (0,), 7: (0, 1), 8: (0, 1), 9: (1,), 10: (0, 1), 11: (1,0), 12: (1, 1), 13: (1,), 14: (1,), 15: (1,)}
            TAIL = (1, 2, 3, 4, 5, 11, 12, 13, 14, 15)
            tail = []
            for ji, job in enumerate(jobs):
                b, pr = job
                g = pr // 2
                d = info[job]
                ko, ob, of = orr.take()
                ac = [acr.take() for _ in range(2)]
                acd = [None, None]
                pend = None

                def pv(kt, pts):
                    for i, (kp, p_, a) in enumerate(pts):
                        m = mm(PS[64 * i:64 * i + 64, ob, :], V[:, kt, g, :], p_, kt == 0, kt == 15, a, vd[kt], of, sig=True)
                        eng = pool if i else dve
                        if kt == 0:
                            u = cp(eng, ac[i][1], p_, a, ac[i][2], pool.last)
                        else:
                            u = tt(eng, ac[i][1], ac[i][1], p_, ALU.add, a, acd[i])
                        acd[i] = u
                        ptr.release(kp, m, u)
                    return m
                for kt in range(NT):
                    pts = []
                    for i in range(2):
                        kq, qi, a, _ = d["q"][i]
                        k, bk, free = sr.take()
                        s_ = slice(kt * 128, (kt + 1) * 128)
                        mm(bank(bk), K1[:, g, s_], Q1[qi], True, False, d[("r", i)], kd[g], k2z, free)
                        m = mm(bank(bk), K2[:, g, s_], Q2[qi], False, True, sig=True)
                        if kt == NT - 1:
                            qr[i].release(kq, m)
                        kp, p_, pf = ptr.take()
                        a = av(p_, bank(bk), ACT.Exp, m, pf, scale=1.0 / 64)
                        sr.release(k, a)
                        pts.append((kp, p_, a))
                    if pend:
                        pv(*pend)
                    pend = (kt, pts)
                    n1, n2 = prep[ji + 1], prep[ji + 2]
                    for todo in PREP.get(kt, (0,)):
                        todo = (n1, n2)[todo]
                        if todo:
                            todo.pop(0)()
                    if kt in TAIL and tail:
                        tail.pop(0)()
                m = pv(*pend)
                ou = av(OU, bank(ob), ACT.Copy, m, rcf["rc"])
                orr.release(ko, ou)
                assert not tail and not n1
                tail = divide(pr, ac, acd, ou)
                if ji == len(jobs) - 1:
                    early, last, norm = finish_last(b)
                    tail = tail[:1] + [early] + tail[1:] + [last, norm]
                elif pr == 7:
                    tail += finish(b)
            for s in tail:
                s()
        A_wout = [WO2[:, 0:128], WO2[:, 128:256]]

        phases = [l0_attn, l0_ffn, l1_attn, lambda: tern(W1[:, :], d_f1, "f1"), mamba,
                  lambda: (local_layer(0), barrier(), local_layer(1)), l3_attn, lambda: tern(W0[:, 6228:11860], d_f3, "f3")]
        pe.wait(d_cb)
        act.wait(d_cb)
        dve.wait(d_cb)
        pool.wait(d_cb)
        for i_, ph in enumerate(phases[:upto]):
            ph()
            if i_ + 1 < len(phases) and i_ not in (0, 4):
                state["xt"] = transpose_x([0, 1])
            ends = barrier()
            if i_ == 0:
                for e in (pe, act, dve, pool):
                    e.wait(d_cb2)
            if i_ == 1:
                d_l2 = load(W0[:, 0:6228], A["l2w"], ends)
            if i_ == 3:
                d_l3w = load(W1[:, :], A["l3w"], ends)
            if i_ == 4:
                d_f3 = load(W0[:, 6228:11860], A["f3w"], ends)

        s_out = sem("s_out")
        sp.run(lambda e: e.dma_start(out.rearrange("(t p) f -> p t f", p=P), X[:, :, :]).then_inc(s_out, 16), state["x"])
        sp.wait((s_out, 16))

        block = ctx.enter_context(nc.Block())

        @block.sync
        def _(eng):
            for op in sp.ops:
                op(eng)

        @block.tensor
        def _(eng):
            for op in pe.ops:
                op(eng)

        @block.scalar
        def _(eng):
            for op in act.ops:
                op(eng)

        @block.vector
        def _(eng):
            for op in dve.ops:
                op(eng)

        @block.gpsimd
        def _(eng):
            for op in pool.ops:
                op(eng)


def cols(v):
    return np.ascontiguousarray(v.reshape(-1, P).T)


def rows(v):
    return np.broadcast_to(v.reshape(1, -1), (P, v.size))


def tall(a):
    k = a.shape[0] // P
    return np.ascontiguousarray(a.reshape(k, P, -1).transpose(1, 0, 2).reshape(P, -1))


def pad_rows(a, n=P):
    o = np.zeros((n,) + a.shape[1:], a.dtype)
    o[:a.shape[0]] = a
    return o


def twice(a):
    return np.concatenate([a, a], 0)


def lay_out(i):
    f = np.float32
    t = np.arange(T)
    s = {}
    ar = np.arange(P)
    s["ident"] = np.eye(P, dtype=f)
    s["bmask"] = (ar[:, None] // 8 == ar[None] // 8).astype(f)
    s["hmask"] = (ar[:, None] // 8 == np.arange(16)[None]).astype(f)
    idx = (f(np.pi / 2) * np.arange(1, T + 1, dtype=f) / f(T)).astype(f)
    s["sin"], s["cos"] = cols(np.sin(idx).astype(f)), cols(np.cos(idx).astype(f))
    s["ones"] = np.ones((P, P), f)
    s["b0"] = rows(np.concatenate([i["L0_attn_bq"], i["L0_attn_bk"], i["L0_attn_bv"]]))
    s["bo0"] = rows(i["L0_attn_bo"])
    s["rb"] = rows(i["L0_ffn_router_b"])
    s["iota8"] = rows(np.arange(8, dtype=f))
    s["mb1"] = cols(i["L0_ffn_b1"].reshape(-1))
    s["mb2"] = pad_rows(i["L0_ffn_b2"])
    s["l1bq"], s["l1bk"] = cols(i["L1_attn_bq"]), cols(i["L1_attn_bk"])
    s["l1bkv"] = rows(np.concatenate([i["L1_attn_bk"], i["L1_attn_bv"]]))
    s["l1bo"] = rows(i["L1_attn_bo"])
    s["decay"] = np.broadcast_to(np.asarray(i["L1_attn_decay_param"]).reshape(1, 1), (P, 1))
    n = ar[None, :] - 1 - ar[:, None]
    s["expn"] = np.maximum(n, 0).astype(f)
    s["tri"] = (n >= 0).astype(f)
    s["trow"] = rows(ar.astype(f))
    s["scol"] = (127 - ar).astype(f).reshape(P, 1)
    for k, m in (("f1", "L1_ffn_"), ("f3", "L3_ffn_")):
        s[k + "s1"], s[k + "s2"] = cols(i[m + "w1_s"]), cols(i[m + "w2_s"])
        s[k + "h1"], s[k + "h2"] = cols(i[m + "h1_s"]), cols(i[m + "h2_s"])
        s[k + "s3"] = rows(i[m + "w3_s"])
    s["cxw"] = i["L2_attn_conv_x_w"].reshape(4, P).T
    s["czw"] = i["L2_attn_conv_z_w"].reshape(4, P).T
    s["cxb"], s["czb"] = cols(i["L2_attn_conv_x_b"]), cols(i["L2_attn_conv_z_b"])
    s["invdt"], s["Dp"] = cols(i["L2_attn_inv_dt"]), cols(i["L2_attn_D"])
    s["bout"] = rows(i["L2_attn_b_out"])
    s["acol"] = np.zeros((P, 16), f)
    s["qks"] = rows(np.concatenate([i["L2_ffn_q_scale"], i["L2_ffn_k_scale"]], 1).reshape(-1))
    s["lg"], s["lb"] = i["L2_ffn_ln_g"].T, i["L2_ffn_ln_b"].T
    fb = np.zeros((2, 2, 3, P), f)
    for b, (o, w) in enumerate(BLK3):
        fb[:, :, b, :w] = i["L2_ffn_b1"].reshape(2, 2, HID2)[:, :, o:o + w]
    s["fb1"] = fb.reshape(12, P).T
    s["fb2"] = rows(i["L2_ffn_b2"].reshape(-1))
    s["scal"] = twice(i["L3_attn_scaling"].reshape(64, 1))
    qb = i["L3_attn_qkv_b"]
    s["qb"] = twice(qb[:1024].reshape(16, 64).T)
    s["kb"] = twice(qb[1024:1280].reshape(4, 64).T)
    s["vb"] = rows(qb[1280:])
    s["ob"] = rows(i["L3_attn_o_b"])
    a = {}
    a["cb"] = np.concatenate([np.asarray(s[k], f).reshape(P, w) for k, w in SPEC], 1)

    z = {}
    neg = -1e30
    q_, k_ = ar[:, None], np.arange(192)[None] - 64
    z["identb"] = np.eye(P)
    z["maskS"] = np.where((k_ <= q_) & (k_ >= q_ - 64), 0, neg)
    for nm, o in (("selB", 0), ("selC", 16)):
        m = np.zeros((P, 16, P))
        for st in range(16):
            for part in range(3):
                m[32 * part + o + st, st, :] = 1
        z[nm] = m.reshape(P, -1)
    m = np.zeros((P, 8, P))
    for h in range(8):
        for part in range(3):
            m[32 * part + h, h, :] = 0.125
    z["selm"] = m.reshape(P, -1)
    a["cbb"] = (np.concatenate([z[k] for k, w in BSPEC], 1).astype(f).view(np.uint32) >> 16).astype(np.uint16)

    a["x"] = i["L0_attn_query"].reshape(T, P)
    w_x = i["L2_attn_W_xdbl"]
    a["w2"] = np.concatenate([
        i["L0_attn_Wq"], i["L0_attn_Wk"], i["L0_attn_Wv"], i["L0_attn_Wo"], i["L0_ffn_router_w"].T,
        i["L1_attn_Wq"], i["L1_attn_Wk"], i["L1_attn_Wv"], i["L1_attn_Wo"],
        i["L2_attn_W_in"], w_x, pad_rows(i["L2_attn_W_dt"])], 1)
    a["wout"] = tall(i["L2_attn_W_out"])
    a["mw1"] = np.ascontiguousarray(i["L0_ffn_w1"].reshape(8 * 1024, P).T)
    a["mw2"] = np.concatenate([tall(np.ascontiguousarray(w.T)) for w in i["L0_ffn_w2"]], 1)
    for k, m in (("f1w", "L1_ffn_"), ("f3w", "L3_ffn_")):
        a[k] = np.concatenate([i[m + "w1_w"].T, i[m + "w2_w"].T] + [tall(np.ascontiguousarray(i[m + n].T)) for n in ("h1_w", "h2_w", "w3_w")], 1)
    lw = []
    for l in range(2):
        lw += [i["L2_ffn_wqkv"][l], tall(i["L2_ffn_wo"][l]), i["L2_ffn_w1"][l], tall(pad_rows(i["L2_ffn_w2"][l], 384))]
    a["l2w"] = np.concatenate(lw, 1)
    half = np.arange(0, 64, 2, dtype=f)
    inv = (f(1.0) / f(10000.0) ** (half / f(64))).astype(f)
    fr = t.astype(f)[:, None] * inv[None]
    base = (half + f(0.4 * 64)) / f(1.4 * 64)
    pw = (t - T // 2).astype(f) / f(32)
    sc = base[None] ** pw[:, None]
    co, si = np.cos(fr), np.sin(fr)
    tb = np.stack([8 * co * sc, 8 * si * sc, -8 * si * sc, co / sc, si / sc, -si / sc]).astype(f)
    tb = tb.reshape(6, NT, P, 32).transpose(2, 0, 1, 3).reshape(P, 3072)
    a["l3w"] = np.concatenate([i["L3_attn_qkv_w"].T, tall(np.ascontiguousarray(i["L3_attn_o_w"].T)), tb], 1)
    return {k: np.ascontiguousarray(v) for k, v in a.items()}


def kernel(**inputs):
    import concourse.bacc as _bacc
    from concourse.bass_utils import run_bass_kernel_spmd as _run

    arrays = lay_out({k: np.asarray(v) for k, v in inputs.items()})
    nc = _bacc.Bacc("TRN2", target_bir_lowering=False, num_devices=1)
    aps = {k: nc.dram_tensor(f"in_{k}", v.shape, mybir.dt.from_np(v.dtype), kind="ExternalInput").ap() for k, v in arrays.items()}
    out = nc.dram_tensor("out_0", (T, P), F32, kind="ExternalOutput").ap()
    program(nc, aps, out)
    r = _run(nc, [{f"in_{k}": v for k, v in arrays.items()}], core_ids=[0])
    return r.results[0]["out_0"].reshape(1, T, P)
```
